# Optimizing a Trainium2 kernel written in Bass

```python
import numpy as np
import jax
import jax.numpy as jnp

def _softmax(x, axis=-1):
    return jax.nn.softmax(x, axis=axis)

def _gelu(x):
    return jax.nn.gelu(x, approximate=True)

def _silu(x):
    return jax.nn.silu(x)

def _sigmoid(x):
    return jax.nn.sigmoid(x)

def _layernorm(x, axis=-1, eps=1e-05):
    m = jnp.mean(x, axis=axis, keepdims=True)
    v = jnp.var(x, axis=axis, keepdims=True)
    return (x - m) / jnp.sqrt(v + eps)

def _scatter_add(tgt, idx, src, axis=0):
    return tgt.at[idx].add(src)

def _segment_sum(src, seg, n):
    return jax.ops.segment_sum(src, seg, n)
kernel_name = 'mk_cond_seq_d4_seqx_r8_789198'

def setup_inputs(seed: int=0):
    np.random.seed(seed)
    _w = jnp.asarray

    def _rec_inputs():
        import jax
        import jax.numpy as jnp
        _rk = jax.random.key(seed)
        x = 1.648e-05 + 1 * jax.random.normal(jax.random.fold_in(_rk, 1), (16, 128, 144), jnp.float32)
        _lenS = 128 - jax.random.randint(jax.random.fold_in(_rk, 7), (16,), 0, max(1, 128 // 4) + 1, jnp.int32)
        _lenS2 = 128 - jax.random.randint(jax.random.fold_in(_rk, 8), (16,), 0, max(1, 128 // 4) + 1, jnp.int32)
        cond_1152 = 0.00914911 + 1.00357 * jax.random.normal(jax.random.fold_in(_rk, 11), (16, 144), jnp.float32)
        return (x, cond_1152)
    x, cond_1152 = _rec_inputs()

    def _L0_cond_setup():
        import jax, jax.numpy as jnp
        import numpy as np
        B, L, C = (8, 128, 144)
        H = 16
        D = C // H
        FF = int(C * 4.0)
        EPS = 1e-06

        def _layernorm(x):
            mu = jnp.mean(x, axis=-1, keepdims=True)
            var = jnp.mean(jnp.square(x - mu), axis=-1, keepdims=True)
            return (x - mu) * jax.lax.rsqrt(var + EPS)

        def _modulate(x, shift, scale):
            return x * (1.0 + scale) + shift

        def _attention(h, W_qkv, b_qkv, W_proj, b_proj):
            b, l, c = h.shape
            qkv = h @ W_qkv + b_qkv
            qkv = qkv.reshape(b, l, 3, H, D)
            q, k, v = (qkv[:, :, 0], qkv[:, :, 1], qkv[:, :, 2])
            scale = D ** (-0.5)
            scores = jnp.einsum('blhd,bmhd->bhlm', q * scale, k)
            attn = jax.nn.softmax(scores, axis=-1)
            o = jnp.einsum('bhlm,bmhd->blhd', attn, v).reshape(b, l, c)
            return o @ W_proj + b_proj
        key = jax.random.key(seed)
        ks = jax.random.split(key, 12)
        s = 0.02
        return {'x': jax.random.normal(ks[0], (B, L, C), jnp.float32), 'c': jax.random.normal(ks[1], (B, 1, C), jnp.float32), 'W_qkv': jax.random.normal(ks[2], (C, 3 * C), jnp.float32) * s, 'b_qkv': jnp.zeros((3 * C,), jnp.float32), 'W_proj': jax.random.normal(ks[3], (C, C), jnp.float32) * s, 'b_proj': jnp.zeros((C,), jnp.float32), 'W_fc1': jax.random.normal(ks[4], (C, FF), jnp.float32) * s, 'b_fc1': jnp.zeros((FF,), jnp.float32), 'W_fc2': jax.random.normal(ks[5], (FF, C), jnp.float32) * s, 'b_fc2': jnp.zeros((C,), jnp.float32), 'W_ada': jax.random.normal(ks[6], (C, 6 * C), jnp.float32) * s, 'b_ada': jnp.zeros((6 * C,), jnp.float32)}
    _L0_cond_all = _L0_cond_setup()
    _L0_cond_in = {k: v for k, v in _L0_cond_all.items() if k in ('W_qkv', 'b_qkv', 'W_proj', 'b_proj', 'W_fc1', 'b_fc1', 'W_fc2', 'b_fc2', 'W_ada', 'b_ada')}
    del _L0_cond_all

    def _L1_cond_setup():
        import jax, jax.numpy as jnp
        import numpy as np
        DIM = 144
        HEADS = 16
        HEAD_DIM = DIM // HEADS
        HIDDEN = int(DIM * 4.0)
        EPS = 1e-12

        def rmsnorm(x, g, d):
            n = jnp.linalg.norm(x, axis=-1, keepdims=True)
            return x / jnp.maximum(n, EPS) * d ** 0.5 * g

        def modulate(x, scale, shift):
            return x * (1.0 + scale[:, None, :]) + shift[:, None, :]
        key = jax.random.key(seed)
        ks = jax.random.split(key, 12)
        B, N = (8, 128)
        s = 0.02
        return {'x': jax.random.normal(ks[0], (B, N, DIM), jnp.float32), 'c': jax.random.normal(ks[1], (B, DIM), jnp.float32), 'g1': jnp.ones((1,), jnp.float32), 'g2': jnp.ones((1,), jnp.float32), 'qkv_w': jax.random.normal(ks[2], (3 * DIM, DIM), jnp.float32) * s, 'qkv_b': jnp.zeros((3 * DIM,), jnp.float32), 'qg': jnp.ones((1,), jnp.float32), 'kg': jnp.ones((1,), jnp.float32), 'proj_w': jax.random.normal(ks[3], (DIM, DIM), jnp.float32) * s, 'proj_b': jnp.zeros((DIM,), jnp.float32), 'fc1_w': jax.random.normal(ks[4], (HIDDEN, DIM), jnp.float32) * s, 'fc1_b': jnp.zeros((HIDDEN,), jnp.float32), 'fc2_w': jax.random.normal(ks[5], (DIM, HIDDEN), jnp.float32) * s, 'fc2_b': jnp.zeros((DIM,), jnp.float32), 'ada_w': jax.random.normal(ks[6], (6 * DIM, DIM), jnp.float32) * s, 'ada_b': jnp.zeros((6 * DIM,), jnp.float32)}
    _L1_cond_all = _L1_cond_setup()
    _L1_cond_in = {k: v for k, v in _L1_cond_all.items() if k in ('g1', 'g2', 'qkv_w', 'qkv_b', 'qg', 'kg', 'proj_w', 'proj_b', 'fc1_w', 'fc1_b', 'fc2_w', 'fc2_b', 'ada_w', 'ada_b')}
    del _L1_cond_all

    def _L2_cond_setup():
        import jax, jax.numpy as jnp
        import numpy as np
        B, S, D = (8, 128, 144)
        H = 16
        HD = D // H
        HID = int(D * 4.0)
        LN_EPS = 1e-05

        def layer_norm(x, w, b):
            m = jnp.mean(x, axis=-1, keepdims=True)
            v = jnp.mean(jnp.square(x - m), axis=-1, keepdims=True)
            return (x - m) * jax.lax.rsqrt(v + LN_EPS) * w + b

        def modulate(x, shift, scale):
            return x * (1.0 + scale[:, None, :]) + shift[:, None, :]

        def attention(x, wq, wk, wv, wo, wo_b):
            b, s, d = x.shape
            q = (x @ wq).reshape(b, s, H, HD).transpose(0, 2, 1, 3)
            k = (x @ wk).reshape(b, s, H, HD).transpose(0, 2, 1, 3)
            v = (x @ wv).reshape(b, s, H, HD).transpose(0, 2, 1, 3)
            scale = 1.0 / np.sqrt(HD).astype(np.float32)
            att = jnp.einsum('bhqd,bhkd->bhqk', q, k) * scale
            att = jax.nn.softmax(att, axis=-1)
            out = jnp.einsum('bhqk,bhkd->bhqd', att, v)
            out = out.transpose(0, 2, 1, 3).reshape(b, s, d)
            return out @ wo + wo_b
        key = jax.random.key(seed)
        ks = jax.random.split(key, 16)
        s = 0.02
        return {'x': jax.random.normal(ks[0], (B, S, D), jnp.float32), 'c': jax.random.normal(ks[1], (B, D), jnp.float32), 'ln1_w': jnp.ones((D,), jnp.float32), 'ln1_b': jnp.zeros((D,), jnp.float32), 'wq': jax.random.normal(ks[2], (D, D), jnp.float32) * s, 'wk': jax.random.normal(ks[3], (D, D), jnp.float32) * s, 'wv': jax.random.normal(ks[4], (D, D), jnp.float32) * s, 'wo': jax.random.normal(ks[5], (D, D), jnp.float32) * s, 'wo_b': jnp.zeros((D,), jnp.float32), 'ln2_w': jnp.ones((D,), jnp.float32), 'ln2_b': jnp.zeros((D,), jnp.float32), 'fc1_w': jax.random.normal(ks[6], (D, HID), jnp.float32) * s, 'fc1_b': jnp.zeros((HID,), jnp.float32), 'fc2_w': jax.random.normal(ks[7], (HID, D), jnp.float32) * s, 'fc2_b': jnp.zeros((D,), jnp.float32), 'ada_w': jax.random.normal(ks[8], (D, 6 * D), jnp.float32) * s, 'ada_b': jnp.zeros((6 * D,), jnp.float32)}
    _L2_cond_all = _L2_cond_setup()
    _L2_cond_in = {k: v for k, v in _L2_cond_all.items() if k in ('ln1_w', 'ln1_b', 'wq', 'wk', 'wv', 'wo', 'wo_b', 'ln2_w', 'ln2_b', 'fc1_w', 'fc1_b', 'fc2_w', 'fc2_b', 'ada_w', 'ada_b')}
    del _L2_cond_all

    def _L3_cond_setup():
        import jax, jax.numpy as jnp
        import numpy as np
        HID = 144
        HEADS = 16
        HD = HID // HEADS
        MLP = int(HID * 4.0)

        def _ln(x, eps, gamma=None, beta=None):
            mu = jnp.mean(x, axis=-1, keepdims=True)
            var = jnp.mean(jnp.square(x - mu), axis=-1, keepdims=True)
            y = (x - mu) / jnp.sqrt(var + eps)
            if gamma is not None:
                y = y * gamma + beta
            return y
        key = jax.random.key(seed)
        ks = jax.random.split(key, 12)
        B, N, C = (8, 128, HID)
        s = lambda k, *sh: jax.random.normal(k, sh, dtype=jnp.float32) * 0.02
        return {'x': jax.random.normal(ks[0], (B, N, C), dtype=jnp.float32), 'c': jax.random.normal(ks[1], (B, C), dtype=jnp.float32), 'w_qkv': s(ks[2], C, 3 * C), 'b_qkv': jnp.zeros((3 * C,), jnp.float32), 'w_proj': s(ks[3], C, C), 'b_proj': jnp.zeros((C,), jnp.float32), 'qn_g': jnp.ones((HD,), jnp.float32), 'qn_b': jnp.zeros((HD,), jnp.float32), 'kn_g': jnp.ones((HD,), jnp.float32), 'kn_b': jnp.zeros((HD,), jnp.float32), 'w1': s(ks[4], C, MLP), 'b1': jnp.zeros((MLP,), jnp.float32), 'w2': s(ks[5], MLP, C), 'b2': jnp.zeros((C,), jnp.float32), 'w_ada': s(ks[6], C, 6 * C), 'b_ada': jnp.zeros((6 * C,), jnp.float32)}
    _L3_cond_all = _L3_cond_setup()
    _L3_cond_in = {k: v for k, v in _L3_cond_all.items() if k in ('w_qkv', 'b_qkv', 'w_proj', 'b_proj', 'qn_g', 'qn_b', 'kn_g', 'kn_b', 'w1', 'b1', 'w2', 'b2', 'w_ada', 'b_ada')}
    del _L3_cond_all
    return {'x': x, 'cond_1152': cond_1152, 'L0_cond_W_qkv': _L0_cond_in['W_qkv'], 'L0_cond_b_qkv': _L0_cond_in['b_qkv'], 'L0_cond_W_proj': _L0_cond_in['W_proj'], 'L0_cond_b_proj': _L0_cond_in['b_proj'], 'L0_cond_W_fc1': _L0_cond_in['W_fc1'], 'L0_cond_b_fc1': _L0_cond_in['b_fc1'], 'L0_cond_W_fc2': _L0_cond_in['W_fc2'], 'L0_cond_b_fc2': _L0_cond_in['b_fc2'], 'L0_cond_W_ada': _L0_cond_in['W_ada'], 'L0_cond_b_ada': _L0_cond_in['b_ada'], 'L1_cond_g1': _L1_cond_in['g1'], 'L1_cond_g2': _L1_cond_in['g2'], 'L1_cond_qkv_w': _L1_cond_in['qkv_w'], 'L1_cond_qkv_b': _L1_cond_in['qkv_b'], 'L1_cond_qg': _L1_cond_in['qg'], 'L1_cond_kg': _L1_cond_in['kg'], 'L1_cond_proj_w': _L1_cond_in['proj_w'], 'L1_cond_proj_b': _L1_cond_in['proj_b'], 'L1_cond_fc1_w': _L1_cond_in['fc1_w'], 'L1_cond_fc1_b': _L1_cond_in['fc1_b'], 'L1_cond_fc2_w': _L1_cond_in['fc2_w'], 'L1_cond_fc2_b': _L1_cond_in['fc2_b'], 'L1_cond_ada_w': _L1_cond_in['ada_w'], 'L1_cond_ada_b': _L1_cond_in['ada_b'], 'L2_cond_ln1_w': _L2_cond_in['ln1_w'], 'L2_cond_ln1_b': _L2_cond_in['ln1_b'], 'L2_cond_wq': _L2_cond_in['wq'], 'L2_cond_wk': _L2_cond_in['wk'], 'L2_cond_wv': _L2_cond_in['wv'], 'L2_cond_wo': _L2_cond_in['wo'], 'L2_cond_wo_b': _L2_cond_in['wo_b'], 'L2_cond_ln2_w': _L2_cond_in['ln2_w'], 'L2_cond_ln2_b': _L2_cond_in['ln2_b'], 'L2_cond_fc1_w': _L2_cond_in['fc1_w'], 'L2_cond_fc1_b': _L2_cond_in['fc1_b'], 'L2_cond_fc2_w': _L2_cond_in['fc2_w'], 'L2_cond_fc2_b': _L2_cond_in['fc2_b'], 'L2_cond_ada_w': _L2_cond_in['ada_w'], 'L2_cond_ada_b': _L2_cond_in['ada_b'], 'L3_cond_w_qkv': _L3_cond_in['w_qkv'], 'L3_cond_b_qkv': _L3_cond_in['b_qkv'], 'L3_cond_w_proj': _L3_cond_in['w_proj'], 'L3_cond_b_proj': _L3_cond_in['b_proj'], 'L3_cond_qn_g': _L3_cond_in['qn_g'], 'L3_cond_qn_b': _L3_cond_in['qn_b'], 'L3_cond_kn_g': _L3_cond_in['kn_g'], 'L3_cond_kn_b': _L3_cond_in['kn_b'], 'L3_cond_w1': _L3_cond_in['w1'], 'L3_cond_b1': _L3_cond_in['b1'], 'L3_cond_w2': _L3_cond_in['w2'], 'L3_cond_b2': _L3_cond_in['b2'], 'L3_cond_w_ada': _L3_cond_in['w_ada'], 'L3_cond_b_ada': _L3_cond_in['b_ada']}

def reference(x, cond_1152, L0_cond_W_qkv, L0_cond_b_qkv, L0_cond_W_proj, L0_cond_b_proj, L0_cond_W_fc1, L0_cond_b_fc1, L0_cond_W_fc2, L0_cond_b_fc2, L0_cond_W_ada, L0_cond_b_ada, L1_cond_g1, L1_cond_g2, L1_cond_qkv_w, L1_cond_qkv_b, L1_cond_qg, L1_cond_kg, L1_cond_proj_w, L1_cond_proj_b, L1_cond_fc1_w, L1_cond_fc1_b, L1_cond_fc2_w, L1_cond_fc2_b, L1_cond_ada_w, L1_cond_ada_b, L2_cond_ln1_w, L2_cond_ln1_b, L2_cond_wq, L2_cond_wk, L2_cond_wv, L2_cond_wo, L2_cond_wo_b, L2_cond_ln2_w, L2_cond_ln2_b, L2_cond_fc1_w, L2_cond_fc1_b, L2_cond_fc2_w, L2_cond_fc2_b, L2_cond_ada_w, L2_cond_ada_b, L3_cond_w_qkv, L3_cond_b_qkv, L3_cond_w_proj, L3_cond_b_proj, L3_cond_qn_g, L3_cond_qn_b, L3_cond_kn_g, L3_cond_kn_b, L3_cond_w1, L3_cond_b1, L3_cond_w2, L3_cond_b2, L3_cond_w_ada, L3_cond_b_ada):
    import jax
    import jax.numpy as jnp

    def _L0_cond_ref(x, c, W_qkv, b_qkv, W_proj, b_proj, W_fc1, b_fc1, W_fc2, b_fc2, W_ada, b_ada):
        import jax, jax.numpy as jnp
        import numpy as np
        B, L, C = (8, 128, 144)
        H = 16
        D = C // H
        FF = int(C * 4.0)
        EPS = 1e-06

        def _layernorm(x):
            mu = jnp.mean(x, axis=-1, keepdims=True)
            var = jnp.mean(jnp.square(x - mu), axis=-1, keepdims=True)
            return (x - mu) * jax.lax.rsqrt(var + EPS)

        def _modulate(x, shift, scale):
            return x * (1.0 + scale) + shift

        def _attention(h, W_qkv, b_qkv, W_proj, b_proj):
            b, l, c = h.shape
            qkv = h @ W_qkv + b_qkv
            qkv = qkv.reshape(b, l, 3, H, D)
            q, k, v = (qkv[:, :, 0], qkv[:, :, 1], qkv[:, :, 2])
            scale = D ** (-0.5)
            scores = jnp.einsum('blhd,bmhd->bhlm', q * scale, k)
            attn = jax.nn.softmax(scores, axis=-1)
            o = jnp.einsum('bhlm,bmhd->blhd', attn, v).reshape(b, l, c)
            return o @ W_proj + b_proj
        ada = jax.nn.silu(c) @ W_ada + b_ada
        shift_msa, scale_msa, gate_msa, shift_mlp, scale_mlp, gate_mlp = jnp.split(ada, 6, axis=-1)
        h = _modulate(_layernorm(x), shift_msa, scale_msa)
        x = x + gate_msa * _attention(h, W_qkv, b_qkv, W_proj, b_proj)
        h = _modulate(_layernorm(x), shift_mlp, scale_mlp)
        mlp = jax.nn.gelu(h @ W_fc1 + b_fc1, approximate=True) @ W_fc2 + b_fc2
        x = x + gate_mlp * mlp
        return x

    def _L1_cond_ref(x, c, g1, g2, qkv_w, qkv_b, qg, kg, proj_w, proj_b, fc1_w, fc1_b, fc2_w, fc2_b, ada_w, ada_b):
        import jax, jax.numpy as jnp
        import numpy as np
        DIM = 144
        HEADS = 16
        HEAD_DIM = DIM // HEADS
        HIDDEN = int(DIM * 4.0)
        EPS = 1e-12

        def rmsnorm(x, g, d):
            n = jnp.linalg.norm(x, axis=-1, keepdims=True)
            return x / jnp.maximum(n, EPS) * d ** 0.5 * g

        def modulate(x, scale, shift):
            return x * (1.0 + scale[:, None, :]) + shift[:, None, :]
        B, N, D = x.shape
        mod = jax.nn.silu(c) @ ada_w.T + ada_b
        shift_msa, scale_msa, gate_msa, shift_mlp, scale_mlp, gate_mlp = jnp.split(mod, 6, axis=-1)
        gate_msa = jnp.tanh(gate_msa)
        gate_mlp = jnp.tanh(gate_mlp)
        h = modulate(rmsnorm(x, g1, D), scale_msa, shift_msa)
        qkv = h @ qkv_w.T + qkv_b
        qkv = qkv.reshape(B, N, 3, HEADS, HEAD_DIM).transpose(2, 0, 3, 1, 4)
        q, k, v = (qkv[0], qkv[1], qkv[2])
        q = rmsnorm(q, qg, HEAD_DIM)
        k = rmsnorm(k, kg, HEAD_DIM)
        q = q * HEAD_DIM ** (-0.5)
        attn = jax.nn.softmax(jnp.einsum('bhqd,bhkd->bhqk', q, k), axis=-1)
        o = jnp.einsum('bhqk,bhkd->bhqd', attn, v)
        o = o.transpose(0, 2, 1, 3).reshape(B, N, D)
        o = o @ proj_w.T + proj_b
        x = x + gate_msa[:, None, :] * o
        h2 = modulate(rmsnorm(x, g2, D), scale_mlp, shift_mlp)
        m = jax.nn.gelu(h2 @ fc1_w.T + fc1_b, approximate=True) @ fc2_w.T + fc2_b
        x = x + gate_mlp[:, None, :] * m
        return x

    def _L2_cond_ref(x, c, ln1_w, ln1_b, wq, wk, wv, wo, wo_b, ln2_w, ln2_b, fc1_w, fc1_b, fc2_w, fc2_b, ada_w, ada_b):
        import jax, jax.numpy as jnp
        import numpy as np
        B, S, D = (8, 128, 144)
        H = 16
        HD = D // H
        HID = int(D * 4.0)
        LN_EPS = 1e-05

        def layer_norm(x, w, b):
            m = jnp.mean(x, axis=-1, keepdims=True)
            v = jnp.mean(jnp.square(x - m), axis=-1, keepdims=True)
            return (x - m) * jax.lax.rsqrt(v + LN_EPS) * w + b

        def modulate(x, shift, scale):
            return x * (1.0 + scale[:, None, :]) + shift[:, None, :]

        def attention(x, wq, wk, wv, wo, wo_b):
            b, s, d = x.shape
            q = (x @ wq).reshape(b, s, H, HD).transpose(0, 2, 1, 3)
            k = (x @ wk).reshape(b, s, H, HD).transpose(0, 2, 1, 3)
            v = (x @ wv).reshape(b, s, H, HD).transpose(0, 2, 1, 3)
            scale = 1.0 / np.sqrt(HD).astype(np.float32)
            att = jnp.einsum('bhqd,bhkd->bhqk', q, k) * scale
            att = jax.nn.softmax(att, axis=-1)
            out = jnp.einsum('bhqk,bhkd->bhqd', att, v)
            out = out.transpose(0, 2, 1, 3).reshape(b, s, d)
            return out @ wo + wo_b
        mod = jax.nn.silu(c) @ ada_w + ada_b
        sh_msa, sc_msa, g_msa, sh_mlp, sc_mlp, g_mlp = jnp.split(mod, 6, axis=1)
        h = modulate(layer_norm(x, ln1_w, ln1_b), sh_msa, sc_msa)
        x = x + g_msa[:, None, :] * attention(h, wq, wk, wv, wo, wo_b)
        h = modulate(layer_norm(x, ln2_w, ln2_b), sh_mlp, sc_mlp)
        h = jax.nn.gelu(h @ fc1_w + fc1_b, approximate=False) @ fc2_w + fc2_b
        x = x + g_mlp[:, None, :] * h
        return x

    def _L3_cond_ref(x, c, w_qkv, b_qkv, w_proj, b_proj, qn_g, qn_b, kn_g, kn_b, w1, b1, w2, b2, w_ada, b_ada):
        import jax, jax.numpy as jnp
        import numpy as np
        HID = 144
        HEADS = 16
        HD = HID // HEADS
        MLP = int(HID * 4.0)

        def _ln(x, eps, gamma=None, beta=None):
            mu = jnp.mean(x, axis=-1, keepdims=True)
            var = jnp.mean(jnp.square(x - mu), axis=-1, keepdims=True)
            y = (x - mu) / jnp.sqrt(var + eps)
            if gamma is not None:
                y = y * gamma + beta
            return y
        B, N, C = x.shape
        H, hd = (HEADS, HD)
        scale = hd ** (-0.5)
        mod = jax.nn.silu(c) @ w_ada + b_ada
        sh_msa, sc_msa, g_msa, sh_mlp, sc_mlp, g_mlp = jnp.split(mod, 6, axis=1)
        xn = _ln(x, 1e-06)
        xn = xn * (1 + sc_msa[:, None, :]) + sh_msa[:, None, :]
        qkv = (xn @ w_qkv + b_qkv).reshape(B, N, 3, H, hd)
        q, k, v = (qkv[:, :, 0], qkv[:, :, 1], qkv[:, :, 2])
        q = _ln(q, 1e-05, qn_g, qn_b)
        k = _ln(k, 1e-05, kn_g, kn_b)
        attn = jnp.einsum('bqhd,bkhd->bhqk', q, k) * scale
        attn = jax.nn.softmax(attn, axis=-1)
        o = jnp.einsum('bhqk,bkhd->bqhd', attn, v).reshape(B, N, C)
        o = o @ w_proj + b_proj
        x = x + g_msa[:, None, :] * o
        xn2 = _ln(x, 1e-06)
        xn2 = xn2 * (1 + sc_mlp[:, None, :]) + sh_mlp[:, None, :]
        h = jax.nn.gelu(xn2 @ w1 + b1, approximate=False)
        m = h @ w2 + b2
        x = x + g_mlp[:, None, :] * m
        return x
    x = _L0_cond_ref(x, cond_1152[:, None, :], L0_cond_W_qkv, L0_cond_b_qkv, L0_cond_W_proj, L0_cond_b_proj, L0_cond_W_fc1, L0_cond_b_fc1, L0_cond_W_fc2, L0_cond_b_fc2, L0_cond_W_ada, L0_cond_b_ada)
    x = _L1_cond_ref(x, cond_1152, L1_cond_g1, L1_cond_g2, L1_cond_qkv_w, L1_cond_qkv_b, L1_cond_qg, L1_cond_kg, L1_cond_proj_w, L1_cond_proj_b, L1_cond_fc1_w, L1_cond_fc1_b, L1_cond_fc2_w, L1_cond_fc2_b, L1_cond_ada_w, L1_cond_ada_b)
    x = _L2_cond_ref(x, cond_1152, L2_cond_ln1_w, L2_cond_ln1_b, L2_cond_wq, L2_cond_wk, L2_cond_wv, L2_cond_wo, L2_cond_wo_b, L2_cond_ln2_w, L2_cond_ln2_b, L2_cond_fc1_w, L2_cond_fc1_b, L2_cond_fc2_w, L2_cond_fc2_b, L2_cond_ada_w, L2_cond_ada_b)
    x = _L3_cond_ref(x, cond_1152, L3_cond_w_qkv, L3_cond_b_qkv, L3_cond_w_proj, L3_cond_b_proj, L3_cond_qn_g, L3_cond_qn_b, L3_cond_kn_g, L3_cond_kn_b, L3_cond_w1, L3_cond_b1, L3_cond_w2, L3_cond_b2, L3_cond_w_ada, L3_cond_b_ada)
    return x

_drawn_inputs = setup_inputs


def setup_inputs(seed=0):
    import zlib

    import numpy as np

    out = dict(_drawn_inputs(seed))
    spreads = {'L0_cond_b_qkv': (0.0, 0.8),
     'L0_cond_b_proj': (0.0, 0.483),
     'L0_cond_b_fc1': (0.0, 0.8),
     'L0_cond_b_fc2': (0.0, 0.48),
     'L0_cond_b_ada': (0.0, 0.501),
     'L1_cond_qkv_b': (0.0, 0.8),
     'L1_cond_proj_b': (0.0, 0.49),
     'L1_cond_fc1_b': (0.0, 0.8),
     'L1_cond_fc2_b': (0.0, 0.478),
     'L1_cond_ada_b': (0.0, 0.601),
     'L2_cond_ln1_w': (1.0, 0.6),
     'L2_cond_ln1_b': (0.0, 0.8),
     'L2_cond_wo_b': (0.0, 0.413),
     'L2_cond_ln2_w': (1.0, 0.6),
     'L2_cond_ln2_b': (0.0, 0.8),
     'L2_cond_fc1_b': (0.0, 0.8),
     'L2_cond_fc2_b': (0.0, 0.519),
     'L2_cond_ada_b': (0.0, 0.513),
     'L3_cond_b_qkv': (0.0, 0.8),
     'L3_cond_b_proj': (0.0, 0.448),
     'L3_cond_qn_g': (1.0, 0.6),
     'L3_cond_qn_b': (0.0, 2.0),
     'L3_cond_kn_g': (1.0, 0.6),
     'L3_cond_kn_b': (0.0, 2.0),
     'L3_cond_b1': (0.0, 0.8),
     'L3_cond_b2': (0.0, 0.429),
     'L3_cond_b_ada': (0.0, 0.478)}
    factors = {'L0_cond_W_qkv': 8.0,
     'L0_cond_W_proj': 8.0,
     'L0_cond_W_fc1': 5.387,
     'L0_cond_W_fc2': 5.017,
     'L1_cond_qkv_w': 8.0,
     'L1_cond_proj_w': 8.0,
     'L1_cond_fc1_w': 5.406,
     'L1_cond_fc2_w': 5.046,
     'L1_cond_ada_w': 2.741,
     'L2_cond_wq': 8.0,
     'L2_cond_wk': 8.0,
     'L2_cond_wv': 8.0,
     'L2_cond_wo': 8.0,
     'L2_cond_fc1_w': 5.082,
     'L2_cond_fc2_w': 4.58,
     'L3_cond_w_qkv': 8.0,
     'L3_cond_w_proj': 8.0,
     'L3_cond_w1': 5.441,
     'L3_cond_w2': 4.906}
    for name, (base, spread) in spreads.items():
        noise = np.random.default_rng([zlib.crc32(name.encode()), seed]).standard_normal(out[name].shape)
        drawn = base * np.exp(spread * noise) if base else spread * noise
        out[name] = jnp.asarray(drawn.astype(out[name].dtype))
    for name, factor in factors.items():
        out[name] = (out[name] * factor).astype(out[name].dtype)
    return out
```

```python
from contextlib import ExitStack

import concourse.bass as bass
from concourse import mybir

F32 = mybir.dt.float32
BF16 = mybir.dt.bfloat16
I32 = mybir.dt.int32
ALU = mybir.AluOpType
ACT = mybir.ActivationFunctionType
AX_X = mybir.AxisListType.X

L = 4
B, T, C = 16, 128, 144
H = 16
D = C // H
P = 128
CR = C - P
KB = CR + 1
FF = 4 * C
FC = (FF + P - 1) // P
FL = FF - (FC - 1) * P
PAIRS = B // 2
QKV, PROJ, FC1, ADA = 0, 3 * C, 4 * C, 4 * C + FF
WCOLS = ADA
ACOLS = 6 * C
SHIFT, SCALE, GATE = 0, C, 2 * C
SW = D + 1
NSLOT = 6
MROW = NSLOT * SW
HW = 64
GRP = 4
NG = H // GRP
VW = 32
HEAD_ORDER = [8 * (g // 2) + 2 * a + g % 2 for g in range(NG) for a in range(GRP)]
LN_EPS = (1e-6, None, 1e-5, 1e-6)
QK_EPS = 1e-5
TINY = 1e-24
MAGIC = float(0x5F3759DF)
NORMED = (False, True, False, True)
Q_STEPS = {1: 14, 3: 16}


def build(nc, x_in, cT, wcat, w2cat, aff, qkaff, ident, out):
    scratch = nc.dram_tensor("mod_scratch", (B, L, ACOLS), F32, kind="Internal").ap()
    ctx = ExitStack()
    with ctx:
        def sb(name, shape, dt=F32):
            return ctx.enter_context(nc.sbuf_tensor(name, shape, dt))

        def sem(name):
            return ctx.enter_context(nc.semaphore(name))

        x = sb("x", [P, B, C])
        xn = sb("xn", [P, B, C])
        mod1 = sb("mod1", [P, B, 3 * C])
        mod2 = sb("mod2", [P, B, 3 * C])
        wa = sb("wa", [P, 2, WCOLS])
        wb = sb("wb", [KB, 2, WCOLS])
        w2 = sb("w2", [P, 2, FC, C])
        idf = sb("idf", [P, P])
        idb = sb("idb", [P, P], BF16)
        half_neg = sb("half_neg", [P, 2])
        qk_g = sb("qk_g", [P, 2, 2 * C])
        qk_b = sb("qk_b", [P, 2 * C])
        hs = sb("hs", [P, 2, C + 1])
        hs2 = sb("hs2", [P, 2, 2, C + 1])
        hA = sb("hA", [P, P])
        hB = sb("hB", [KB, P])
        stack = sb("stack", [P, 2, 2 * H, HW], BF16)
        rem = sb("rem", [P, 2, 2 * C])
        qT = sb("qT", [P, 2, H // 2, T], BF16)
        kT = sb("kT", [P, 2, H // 2, T], BF16)
        mx = sb("mx", [P, 2, H])
        mrem = sb("mrem", [P, 2, H])
        zeros = sb("zeros", [P, H])
        m3 = sb("m3", [P, 2, P], BF16)
        mT = sb("mT", [48, 2, T], BF16)
        e = sb("e", [P, H, T])
        v = sb("v", [P, 2, H, VW])
        oT = sb("oT", [P, NG, T])
        rsum = sb("rsum", [P, H])
        o = sb("o", [P, C + 1])
        otA = sb("otA", [P, P])
        otB = sb("otB", [KB, P])
        gated = sb("gated", [P, C])
        qkv = sb("qkv", [P, 2, 3 * C])
        qsq = sb("qsq", [P, 2 * C])
        qss = sb("qss", [P, 2 * H])
        qrs = sb("qrs", [P, 2 * H])
        qt1 = sb("qt1", [P, 2 * H])
        qt2 = sb("qt2", [P, 2 * H])
        qy = sb("qy", [P, 2, 2 * C])
        st6 = sb("st6", [P, 2, 2, 6])
        mv = sb("mv", [P, 2, 2, 2])
        var = sb("var", [P, 2, 2])
        rstd = sb("rstd", [P, 2, 2])
        h2A = sb("h2A", [P, 2, 2 * T])
        h2B = sb("h2B", [KB, 2, 2 * T])
        gT = sb("gT", [P, 2, FC, 2 * T])
        gated2 = sb("gated2", [P, 2, C])
        ada_a = sb("ada_a", [P, ACOLS])
        ada_b = sb("ada_b", [KB, ACOLS])
        c_a = sb("c_a", [P, B])
        c_b = sb("c_b", [CR, B])
        s_a = sb("s_a", [P, B])
        s_b = sb("s_b", [KB, B])
        aff_sb = sb("aff_sb", [B, L, 2, 2, C])
        m_sb = sb("m_sb", [B, L, ACOLS])
        sc1 = sb("sc1", [B, 2, C])
        shb = sb("shb", [B, 2, C])

        bank = [ctx.enter_context(nc.psum_tensor(f"bank{i}", [P, 512], F32)) for i in range(8)]

        ld_const, ld_x, ld_ada, ld_mod1, ld_mod2, ld_aff = (
            sem(n) for n in ("ld_const", "ld_x", "ld_ada", "ld_mod1", "ld_mod2", "ld_aff"))
        ld_w = [sem(f"ld_w{i}") for i in range(2)]
        set_ones, set_idb, silu_done, ada_mm, ada_sc, ada_b1, ada_mod, ada_gate, mod_out, set_qk = (
            sem(n) for n in ("set_ones", "set_idb", "silu_done", "ada_mm", "ada_sc", "ada_b1", "ada_mod",
                             "ada_gate", "mod_out", "set_qk"))
        hT_pe, qkv_pe, tk_pe, tq_pe, s_pe, mT_pe, st_pe, av_pe, ob_pe, oT_pe, proj_pe = (
            sem(n) for n in ("hT_pe", "qkv_pe", "tk_pe", "tq_pe", "s_pe", "mT_pe", "st_pe", "av_pe",
                             "ob_pe", "oT_pe", "proj_pe"))
        hs_mul, hs_rdy, hT_sb, x1_rdy, x2_rdy, rem_rdy, x3_rdy, slots_rdy, v_sb, kT_sb, qT_sb = (
            sem(n) for n in ("hs_mul", "hs_rdy", "hT_sb", "x1_rdy", "x2_rdy", "rem_rdy", "x3_rdy",
                             "slots_rdy", "v_sb", "kT_sb", "qT_sb"))
        mx_rdy, m_step, m_rdy, mT_sb, m_rows, e_rdy, ot_sb, rsum_rdy, o_rdy, oT_sb, gate_rdy, x_att = (
            sem(n) for n in ("mx_rdy", "m_step", "m_rdy", "mT_sb", "m_rows", "e_rdy", "ot_sb", "rsum_rdy",
                             "o_rdy", "oT_sb", "gate_rdy", "x_att"))
        qkv_sb, q_mid, q_gain, q_rdy = (sem(n) for n in ("qkv_sb", "q_mid", "q_gain", "q_rdy"))
        q_step = {l: sem(f"q_step{l}") for l in range(L) if NORMED[l]}
        h2T_pe, fc1_pe, fc2_pe, h2T_sb, gelu_rdy, gate2_rdy, x_mlp, hs2_mul, hs2_rdy = (
            sem(n) for n in ("h2T_pe", "fc1_pe", "fc2_pe", "h2T_sb", "gelu_rdy", "gate2_rdy", "x_mlp",
                             "hs2_mul", "hs2_rdy"))
        ln_mv, ln_sq, ln_sum = ([sem(f"{n}{k + 1}") for k in range(2)]
                                       for n in ("ln_mv", "ln_sq", "ln_sum"))
        ln1_var, ln1_rstd, xn1_rdy, ln2_var, ln2_rstd, xn2_rdy, out_done = (
            sem(n) for n in ("ln1_var", "ln1_rstd", "xn1_rdy", "ln2_var", "ln2_rstd", "xn2_rdy", "out_done"))

        def ge(eng, s, value):
            if isinstance(value, int) and value <= 0:
                return
            assert isinstance(value, int) or value.min_val > 0
            eng.wait_ge(s, value)

        def upto(l, b, per=1):
            return (b + (16 * l + 1)) * per

        def upto_p(l, j, per=1):
            return (j + (PAIRS * l + 1)) * per

        def upto_n(l, b, per=1):
            return (b + (16 * (l // 2) + 1)) * per

        def lags(l, behind=0):
            d = int(NORMED[l])
            return dict(ahead=0, qkv=behind, split=d + behind, score=1 + d + behind, prob=2 + d + behind,
                        out=3 + d + behind)

        def attention(eng, l, slot, behind=0):
            lag = lags(l, behind)
            first = lag["out"] + 1 + (lag["out"] + 1) % 2
            if l == 0:
                first += 2

            def plain(s):
                slot(l, s, lambda k: s - lag[k] if 0 <= s - lag[k] < B else None)
            for s in range(first):
                plain(s)
            with eng.Fori(first // 2, B // 2) as i:
                for u in range(2):
                    slot(l, first + u, lambda k, u=u: 2 * i + (u - lag[k]))
            for s in range(B, B + lag["out"]):
                plain(s)

        def mlp(eng, l, slot):
            def plain(j):
                slot(l, j, lambda k: j - k if 0 <= j - k < PAIRS else None)
            for j in (-1, 0, 1):
                plain(j)
            with eng.Fori(1, PAIRS // 2 - 1) as i:
                for u in range(2):
                    slot(l, 2 + u, lambda k, u=u: 2 * i + (u - k))
            for j in (PAIRS - 2, PAIRS - 1, PAIRS):
                plain(j)

        def head(g, a):
            return HEAD_ORDER[GRP * g + a]

        def last(l, s, lag):
            return 0 <= s - 1 - lag < B

        def load_mod(eng, l, half):
            eng.dma_start((mod1, mod2)[half][:],
                          scratch[:, l, half * 3 * C:(half + 1) * 3 * C].partition_broadcast(P)
                          ).then_inc((ld_mod1, ld_mod2)[half], 16)

        def load_w(eng, l):
            eng.dma_start(wa[:, l % 2, :], wcat[l, 0:P, 0:WCOLS]).then_inc(ld_w[l % 2], 16)
            eng.dma_start(wb[:, l % 2, :], wcat[l, P:P + KB, 0:WCOLS]).then_inc(ld_w[l % 2], 16)
            eng.dma_start(w2[:, l % 2], w2cat[l]).then_inc(ld_w[l % 2], 16)

        block = ctx.enter_context(nc.Block())

        @block.sync
        def _(sp):
            sp.dma_start(c_a[:], cT[0:P, :]).then_inc(ld_const, 16)
            sp.dma_start(c_b[:], cT[P:C, :]).then_inc(ld_const, 16)
            sp.dma_start(idf[:], ident).then_inc(ld_const, 16)
            sp.dma_start(aff_sb[:], aff.partition_broadcast(B)).then_inc(ld_aff, 16)
            for l in range(L):
                if l:
                    sp.wait_ge(ada_mm, l)
                sp.dma_start(ada_a[:], wcat[l, 0:P, ADA:]).then_inc(ld_ada, 16)
                sp.dma_start(ada_b[:], wcat[l, P:P + KB, ADA:]).then_inc(ld_ada, 16)
                if l == 0:
                    for q in range(4):
                        sp.dma_start(x[:, 4 * q:4 * q + 4, :],
                                     x_in[4 * q:4 * q + 4].rearrange("b t c -> t b c")).then_inc(ld_x, 16)
                    sp.dma_start(qk_g[:], qkaff[:, 0, :].partition_broadcast(P)).then_inc(ld_aff, 16)
                    sp.dma_start(qk_b[:], qkaff[1, 1, :].partition_broadcast(P)).then_inc(ld_aff, 16)
            sp.wait_ge(ada_mod, 2 * L)
            sp.wait_ge(ada_gate, L)
            sp.dma_start(scratch, m_sb[:]).then_inc(mod_out, 16)
            sp.wait_ge(mod_out, 16)

            load_mod(sp, 0, 0)
            load_w(sp, 0)
            load_mod(sp, 0, 1)
            load_w(sp, 1)

            def slot(l, s, at):
                n = at("prob")
                if n is None:
                    return
                par = (s - lags(l)["prob"]) % 2
                sp.wait_ge(mT_sb, upto(l, n))
                for half in range(2):
                    sp.dma_start(qT[HW * half + MROW:HW * half + MROW + 3, par],
                                 mT[24 * half:24 * half + 24, par, :]).then_inc(m_rows, 16)

            for l in range(L):
                attention(sp, l, slot)
            for q in range(PAIRS):
                sp.wait_ge(x_mlp, upto_p(L - 1, q))
                sp.dma_start(out[2 * q:2 * q + 2].rearrange("b t c -> t b c"), x[:, 2 * q:2 * q + 2, :]
                             ).then_inc(out_done, 16)
            sp.wait_ge(out_done, 16 * PAIRS)

        @block.tensor
        def _(pe):
            pe.wait_ge(silu_done, 2)
            for l in range(L):
                pe.wait_ge(ld_ada, 32 * (l + 1))
                if l:
                    pe.wait_ge(ada_mod, 2 * l)
                    pe.wait_ge(ada_gate, l)
                for half in range(2):
                    cols = slice(half * 3 * C, (half + 1) * 3 * C)
                    pe.matmul(bank[half][0:B, 0:3 * C], s_a[:], ada_a[:, cols], start=True, stop=False)
                    mm = pe.matmul(bank[half][0:B, 0:3 * C], s_b[:], ada_b[:, cols], start=False, stop=True)
                mm.then_inc(ada_mm, 1)
            pe.wait_ge(ada_mod, 2 * L)
            pe.wait_ge(ada_gate, L)
            pe.wait_ge(set_idb, 1)

            bank2b = bank[2][:].bitcast(BF16)
            bank3b = bank[3][:].bitcast(BF16)
            bank0b = bank[0][:].bitcast(BF16)

            def slot(l, s, at):
                lag = lags(l)
                w = l % 2
                n = at("qkv")
                if n is not None:
                    pe.wait_ge(hs_rdy, upto(l, n))
                    if last(l, s, lag["out"]):
                        pe.wait_ge(oT_sb, upto(l, at("out") - 1))
                    elif last(l, s, lag["prob"]):
                        pe.wait_ge(mT_sb, upto(l, at("prob") - 1))
                    elif last(l, s, 0):
                        pe.wait_ge(hT_sb, upto(l, n - 1))
                    par = s % 2
                    pe.transpose(bank[0][:, 0:P], hs[:, par, 0:P], idf[:])
                    pe.transpose(bank[0][0:KB, P:2 * P], hs[:, par, P:C + 1], idf[:]).then_inc(hT_pe, 1)
                n = at("out")
                if n is not None:
                    pe.wait_ge(ot_sb, upto(l, n))
                    if last(l, s, lag["out"]):
                        pe.wait_ge(gate_rdy, upto(l, n - 1))
                    elif last(l, s, lag["score"]):
                        pe.wait_ge(qT_sb, upto(l, at("score") - 1))
                    for g in range(NG):
                        tr = pe.transpose(bank[2][:, g * P:(g + 1) * P], oT[:, g, :], idf[:])
                    tr.then_inc(ob_pe, 1)
                n = at("score")
                if n is not None:
                    par = (s - lag["score"]) % 2
                    pe.wait_ge(slots_rdy, upto(l, n, 4))
                    pe.wait_ge(x3_rdy, upto(l, n, 2))
                    if last(l, s, lag["prob"]):
                        pe.wait_ge(ot_sb, upto(l, at("prob") - 1))
                    elif last(l, s, lag["score"]):
                        pe.wait_ge(kT_sb, upto(l, n - 1))
                    for i in range(H // 2):
                        tr = pe.transpose(bank3b[:, i * P:(i + 1) * P],
                                          stack[:, par, H + 2 * i:H + 2 * i + 2, :], idb[:])
                    tr.then_inc(tk_pe, 1)
                n = at("prob")
                if n is not None:
                    par = (s - lag["prob"]) % 2
                    pe.wait_ge(m_rdy, upto(l, n))
                    if at("qkv") is not None:
                        pe.wait_ge(hT_sb, upto(l, at("qkv")))
                    else:
                        pe.wait_ge(oT_sb, upto(l, at("out") - 1))
                    pe.transpose(bank0b[:, 0:P], m3[:, par, :], idb[:]).then_inc(mT_pe, 1)
                n = at("qkv")
                if n is not None:
                    if s == 0:
                        pe.wait_ge(ld_w[w], 48 * (l // 2 + 1))
                        if l:
                            pe.wait_ge(gate2_rdy, upto_p(l - 1, PAIRS - 1))
                    pe.wait_ge(hT_sb, upto(l, n))
                    if last(l, s, 0):
                        if NORMED[l]:
                            pe.wait_ge(qkv_sb, upto_n(l, n - 1))
                        else:
                            pe.wait_ge(v_sb, upto(l, n - 1))
                            pe.wait_ge(rem_rdy, upto(l, n - 1))
                    pe.matmul(bank[1][:, 0:3 * C], hA[:], wa[:, w, QKV:QKV + 3 * C], start=True, stop=False)
                    pe.matmul(bank[1][:, 0:3 * C], hB[:], wb[:, w, QKV:QKV + 3 * C], start=False, stop=True
                              ).then_inc(qkv_pe, 1)
                n = at("score")
                if n is not None:
                    par = (s - lag["score"]) % 2
                    if at("out") is not None:
                        pe.wait_ge(o_rdy, upto(l, at("out")))
                    elif last(l, s, lag["score"]):
                        pe.wait_ge(qT_sb, upto(l, n - 1))
                    for i in range(H // 2):
                        tr = pe.transpose(bank2b[:, i * P:(i + 1) * P],
                                          stack[:, par, 2 * i:2 * i + 2, :], idb[:])
                    tr.then_inc(tq_pe, 1)
                n = at("out")
                if n is not None:
                    pe.wait_ge(o_rdy, upto(l, n))
                    if at("prob") is not None:
                        pe.wait_ge(mT_sb, upto(l, at("prob")))
                    else:
                        pe.wait_ge(oT_sb, upto(l, n - 1))
                    pe.transpose(bank[0][:, 0:P], o[:, 0:P], idf[:])
                    pe.transpose(bank[0][0:KB, P:2 * P], o[:, P:C + 1], idf[:]).then_inc(oT_pe, 1)

                def key_scores(n, par, half):
                    if half == 0:
                        pe.wait_ge(m_rows, upto(l, n, 32))
                    ge(pe, e_rdy, upto(l, n, 4) - 4 + 2 * half)
                    for a in range(GRP):
                        for odd in range(2):
                            r = slice(HW * odd, HW * odd + MROW + 3)
                            mm = pe.matmul(bank[6 + odd][:, a * T:(a + 1) * T], kT[r, par, GRP * half + a, :],
                                           qT[r, par, GRP * half + a, :], start=True, stop=True)
                            if a == GRP - 1:
                                mm.then_inc(st_pe, 1)

                def query_scores(n, par, half):
                    if half == 0:
                        pe.wait_ge(kT_sb, upto(l, n))
                        pe.wait_ge(qT_sb, upto(l, n))
                    ge(pe, mx_rdy, upto(l, n, 4) - 4 + 2 * half)
                    for a in range(GRP):
                        for odd in range(2):
                            r = slice(HW * odd, HW * odd + MROW)
                            mm = pe.matmul(bank[4 + odd][:, a * T:(a + 1) * T], qT[r, par, GRP * half + a, :],
                                           kT[r, par, GRP * half + a, :], start=True, stop=True)
                            if a == GRP - 1:
                                mm.then_inc(s_pe, 1)

                def values(n, par, g):
                    pe.wait_ge(e_rdy, upto(l, n, 4) - 3 + g)
                    if g == 0:
                        pe.wait_ge(v_sb, upto(l, n))
                        if at("score") is not None:
                            pe.wait_ge(kT_sb, upto(l, at("score")))
                        else:
                            pe.wait_ge(ot_sb, upto(l, n - 1))
                    for a in range(GRP):
                        h = head(g, a)
                        mm = pe.matmul(bank[3][VW * a:VW * (a + 1), g * T:(g + 1) * T], v[:, par, h, :],
                                       e[:, g * GRP + a, :], start=True, stop=True, tile_position=(0, VW * a))
                    mm.then_inc(av_pe, 1)

                ns, ps = at("score"), (s - lag["score"]) % 2
                np_, pp = at("prob"), (s - lag["prob"]) % 2
                if np_ is not None:
                    key_scores(np_, pp, 0)
                if ns is not None:
                    query_scores(ns, ps, 0)
                n = at("out")
                if n is not None:
                    pe.wait_ge(oT_sb, upto(l, n))
                    if at("score") is not None:
                        pe.wait_ge(qT_sb, upto(l, at("score")))
                    pe.matmul(bank[2][:, 0:C], otA[:], wa[:, w, PROJ:PROJ + C], start=True, stop=False)
                    pe.matmul(bank[2][:, 0:C], otB[:], wb[:, w, PROJ:PROJ + C], start=False, stop=True
                              ).then_inc(proj_pe, 1)
                for g in (0, 1):
                    if np_ is not None:
                        values(np_, pp, g)
                if np_ is not None:
                    key_scores(np_, pp, 1)
                if ns is not None:
                    query_scores(ns, ps, 1)
                for g in (2, 3):
                    if np_ is not None:
                        values(np_, pp, g)

            def mlp_slot(l, j, at):
                w = l % 2
                n = at(0)
                if n is not None:
                    par = j % 2
                    pe.wait_ge(hs2_rdy, upto_p(l, n))
                    if j == 0:
                        pe.wait_ge(oT_sb, upto(l, B - 1))
                    else:
                        pe.wait_ge(h2T_sb, upto_p(l, n - 1, 2))
                    for u in range(2):
                        pe.transpose(bank[0][:, u * P:(u + 1) * P], hs2[:, par, u, 0:P], idf[:])
                    for u in range(2):
                        tr = pe.transpose(bank[0][0:KB, (2 + u) * P:(3 + u) * P], hs2[:, par, u, P:C + 1],
                                          idf[:])
                    tr.then_inc(h2T_pe, 1)
                n = at(1)
                if n is not None:
                    par = (j - 1) % 2
                    pe.wait_ge(gelu_rdy, upto_p(l, n, 3))
                    if j > 1:
                        pe.wait_ge(gate2_rdy, upto_p(l, n - 1))
                    elif NORMED[l]:
                        pe.wait_ge(qkv_sb, upto_n(l, B - 1))
                    else:
                        pe.wait_ge(v_sb, upto(l, B - 1))
                        pe.wait_ge(rem_rdy, upto(l, B - 1))
                    for u in range(2):
                        for c in range(FC):
                            k = P if c < FC - 1 else FL + 1
                            mm = pe.matmul(bank[1][:, u * C:(u + 1) * C], gT[0:k, par, c, u * T:(u + 1) * T],
                                           w2[0:k, w, c, :], start=(c == 0), stop=(c == FC - 1))
                    mm.then_inc(fc2_pe, 1)
                n = at(0)
                if n is not None:
                    par = j % 2
                    pe.wait_ge(h2T_sb, upto_p(l, n, 2))
                    if j == 0:
                        pe.wait_ge(gate_rdy, upto(l, B - 1))
                        pe.wait_ge(mx_rdy, upto(l, B - 1, 4))
                    for c in range(FC):
                        m = P if c < FC - 1 else FL
                        dst = bank[2 + 3 * par + c // 2][0:m, (c % 2) * 2 * T:(c % 2 + 1) * 2 * T]
                        cols = slice(FC1 + c * P, FC1 + c * P + m)
                        pe.matmul(dst, wa[:, w, cols], h2A[:, par, :], start=True, stop=False)
                        mm = pe.matmul(dst, wb[:, w, cols], h2B[:, par, :], start=False, stop=True)
                        if c % 2 or c == FC - 1:
                            mm.then_inc(fc1_pe, 1)

            for l in range(L):
                attention(pe, l, slot)
                mlp(pe, l, mlp_slot)

        @block.scalar
        def _(act):
            act.wait_ge(ld_const, 48)
            act.wait_ge(set_ones, 1)
            act.activation(s_a[:], c_a[:], ACT.Silu).then_inc(silu_done, 1)
            act.activation(s_b[0:CR, :], c_b[:], ACT.Silu).then_inc(silu_done, 1)
            gates = m_sb[:].rearrange("b l (h k c) -> b l h k c", h=2, k=3)
            for l in range(L):
                act.wait_ge(ada_mm, l + 1)
                for half in range(2):
                    i = act.activation(gates[:, l, half, 2, :], bank[half][0:B, GATE:GATE + C],
                                       ACT.Tanh if l == 1 else ACT.Copy)
                i.then_inc(ada_gate, 1)

            def slot(l, s, at):
                lag = lags(l)
                n = at("qkv")
                if n is not None:
                    act.wait_ge(hT_pe, upto(l, n))
                    ge(act, qkv_pe, upto(l, n - 1))
                    act.copy(hA[:], bank[0][:, 0:P])
                    act.copy(hB[:], bank[0][0:KB, P:2 * P]).then_inc(hT_sb, 1)
                n = at("score")
                if n is not None:
                    par = (s - lag["score"]) % 2
                    act.wait_ge(tk_pe, upto(l, n))
                    ge(act, st_pe, upto(l, n - 2, 4))
                    act.copy(kT[:, par], bank[3][:].bitcast(BF16)).then_inc(kT_sb, 1)
                n = at("prob")
                if n is not None:
                    par = (s - lag["prob"]) % 2
                    act.wait_ge(mT_pe, upto(l, n))
                    ge(act, m_rows, upto(l, n - 2, 32))
                    act.copy(mT[:, par, :], bank[0][0:48, 0:P // 2].bitcast(BF16)).then_inc(mT_sb, 1)

                def first_part():
                    n = at("split")
                    if n is None:
                        return
                    par = (s - lag["split"]) % 2
                    if NORMED[l]:
                        act.wait_ge(q_rdy, upto_n(l, n))
                        src = qy[:, par, :]
                    else:
                        act.wait_ge(qkv_pe, upto(l, n))
                        src = bank[1][:, 0:2 * C]
                    ge(act, tq_pe, upto(l, n - 2))
                    ge(act, tk_pe, upto(l, n - 2))
                    act.copy(stack[:, par, :, 0:D], src.rearrange("p (h d) -> p h d", d=D)).then_inc(x1_rdy, 1)

                first_part()
                if NORMED[l]:
                    n = at("qkv")
                    if n is not None:
                        act.wait_ge(qkv_pe, upto(l, n))
                        if s >= 2:
                            act.wait_ge(v_sb, upto(l, n - 2))
                            act.wait_ge(q_mid, upto_n(l, n - 2))
                        act.copy(qkv[:, s % 2, :], bank[1][:, 0:3 * C]).then_inc(qkv_sb, 1)

                def exps(groups):
                    n = at("prob")
                    if n is None:
                        return
                    for g in groups:
                        act.wait_ge(st_pe, upto(l, n, 4) - 3 + g)
                        ge(act, av_pe, upto(l, n - 1, 4) - 3 + g)
                        act.activation(e[:, g * GRP:(g + 1) * GRP, :], bank[6 + g % 2][:], ACT.Exp,
                                       scale=float(D) ** -0.5).then_inc(e_rdy, 1)

                exps((0, 1))
                n = at("split")
                if n is not None:
                    par = (s - lag["split"]) % 2
                    act.wait_ge(rem_rdy, upto(l, n))
                    act.copy(stack[:, par, :, 3 * SW:3 * SW + D],
                             rem[:, par, :].rearrange("p (h d) -> p h d", d=D)).then_inc(x2_rdy, 1)
                n = at("out")
                if n is not None:
                    act.wait_ge(oT_pe, upto(l, n))
                    ge(act, proj_pe, upto(l, n - 1))
                    act.copy(otA[:], bank[0][:, 0:P])
                    act.copy(otB[:], bank[0][0:KB, P:2 * P]).then_inc(oT_sb, 1)
                exps((2, 3))
                n = at("prob")
                if n is not None:
                    act.wait_ge(av_pe, upto(l, n, 4))
                    ge(act, ob_pe, upto(l, n - 1))
                    act.copy(oT[:], bank[3][:]).then_inc(ot_sb, 1)
                n = at("split")
                if n is not None:
                    par = (s - lag["split"]) % 2
                    ge(act, av_pe, upto(l, n - 2, 4))
                    if NORMED[l]:
                        act.wait_ge(qkv_sb, upto_n(l, n))
                        src = qkv[:, par, 2 * C:3 * C]
                    else:
                        src = bank[1][:, 2 * C:3 * C]
                    act.copy(v[:, par, :, 0:D], src.rearrange("p (h d) -> p h d", d=D)).then_inc(v_sb, 1)

            def mlp_slot(l, j, at):
                n = at(0)
                if n is None:
                    return
                par = j % 2
                act.wait_ge(h2T_pe, upto_p(l, n))
                ge(act, fc1_pe, upto_p(l, n - 2, 3))
                act.copy(h2A[:, par, :], bank[0][:, 0:2 * P]).then_inc(h2T_sb, 1)
                act.copy(h2B[:, par, :], bank[0][0:KB, 2 * P:4 * P]).then_inc(h2T_sb, 1)
                ge(act, fc2_pe, upto_p(l, n - 2))
                for k in range(3):
                    act.wait_ge(fc1_pe, upto_p(l, n, 3) - 2 + k)
                    m = P if k < 2 else FL
                    cs = slice(2 * k, min(2 * k + 2, FC))
                    width = 4 * T if k < 2 else 2 * T
                    act.activation(gT[0:m, par, cs, :], bank[2 + 3 * par + k][0:m, 0:width],
                                   ACT.Gelu_apprx_tanh if l < 2 else ACT.Gelu).then_inc(gelu_rdy, 1)

            for l in range(L):
                attention(act, l, slot)
                if l + 1 < L:
                    act.wait_ge(gate_rdy, upto(l, B - 1))
                    load_mod(act, l + 1, 0)
                mlp(act, l, mlp_slot)
                if l + 1 < L:
                    act.wait_ge(gate2_rdy, upto_p(l, PAIRS - 1))
                    load_mod(act, l + 1, 1)
                    if l + 2 < L:
                        load_w(act, l + 2)

        @block.vector
        def _(dve):
            dve.memset(s_b[:], 1.0).then_inc(set_ones, 1)
            dve.memset(zeros[:], 0.0)
            dve.memset(m3[:], 0.0)
            dve.memset(half_neg[:], -0.5).then_inc(set_ones, 1)
            dve.memset(stack[:], 0.0).then_inc(set_ones, 1)
            dve.memset(v[:], 0.0).then_inc(set_ones, 1)
            dve.memset(hs[:, :, C:C + 1], 1.0)
            dve.memset(hs2[:, :, :, C:C + 1], 1.0)
            dve.memset(o[:, C:C + 1], 1.0)
            dve.memset(gT[FL:FL + 1, :, FC - 1, :], 1.0).then_inc(set_ones, 1)
            dve.wait_ge(set_ones, 4)
            dve.memset(stack[:, :, H:2 * H, MROW:MROW + 3], -1.0)
            dve.memset(v[:, :, :, D:D + 1], 1.0).then_inc(set_ones, 1)
            dve.wait_ge(ld_const, 48)
            dve.tensor_copy(idb[:], idf[:]).then_inc(set_idb, 1)
            dve.wait_ge(ld_aff, 48)
            dve.tensor_scalar(qk_g[:, 0, :], qk_g[:, 0, :], float(D) ** 0.5, None, ALU.mult).then_inc(set_qk, 1)
            dve.tensor_scalar(aff_sb[:, 1, :, 0, :], aff_sb[:, 1, :, 0, :], float(C) ** 0.5, None,
                              ALU.mult).then_inc(set_qk, 1)
            dve.wait_ge(set_qk, 2)
            halves = m_sb[:].rearrange("b l (h k c) -> b l h k c", h=2, k=3)
            for l in range(L):
                dve.wait_ge(ada_gate, l + 1)
                if l:
                    dve.wait_ge(ada_mod, 2 * l)
                for half in range(2):
                    i = dve.tensor_scalar(sc1[:, half, :], bank[half][0:B, SCALE:SCALE + C], 1.0, None, ALU.add)
                i.then_inc(ada_sc, 1)
                dve.wait_ge(ada_sc, l + 1)
                dve.tensor_tensor(halves[:, l, :, 1, :], sc1[:], aff_sb[:, l, :, 0, :], ALU.mult).then_inc(ada_mod, 1)
                dve.tensor_tensor(shb[:], sc1[:], aff_sb[:, l, :, 1, :], ALU.mult).then_inc(ada_b1, 1)
                dve.wait_ge(ada_b1, l + 1)
                for half in range(2):
                    i = dve.tensor_tensor(halves[:, l, half, 0, :], bank[half][0:B, SHIFT:SHIFT + C],
                                          shb[:, half, :], ALU.add)
                i.then_inc(ada_mod, 1)

            def statistics(l, j, k):
                var_s = (ln1_var, ln2_var)[k]
                for u in range(2):
                    i = dve.bn_stats(st6[:, k, u, :], x[:, bass.ds(2 * j + u, 1), :])
                dve.drain()
                for u in range(2):
                    i = dve.bn_aggr(mv[:, k, u, :], st6[:, k, u, :])
                i.then_inc(ln_mv[k], 1)
                dve.wait_ge(ln_mv[k], upto_p(l, j))
                if LN_EPS[l] is None:
                    dve.tensor_tensor(var[:, k, :], mv[:, k, :, 0], mv[:, k, :, 0], ALU.mult
                                      ).then_inc(ln_sq[k], 1)
                    dve.wait_ge(ln_sq[k], j + 1)
                    dve.tensor_tensor(var[:, k, :], var[:, k, :], mv[:, k, :, 1], ALU.add
                                      ).then_inc(ln_sum[k], 1)
                    dve.wait_ge(ln_sum[k], j + 1)
                    dve.tensor_scalar(var[:, k, :], var[:, k, :], float(C), TINY, ALU.mult, ALU.max
                                      ).then_inc(var_s, 1)
                else:
                    dve.tensor_scalar(var[:, k, :], mv[:, k, :, 1], LN_EPS[l], None, ALU.add).then_inc(var_s, 1)

            def normalise(l, j, k):
                rstd_s, done = ((ln1_rstd, xn1_rdy), (ln2_rstd, xn2_rdy))[k]
                dve.wait_ge(rstd_s, upto_p(l, j))
                for u in range(2):
                    dst, src = xn[:, bass.ds(2 * j + u, 1), :], x[:, bass.ds(2 * j + u, 1), :]
                    if LN_EPS[l] is None:
                        i = dve.tensor_scalar(dst, src, rstd[:, k, u:u + 1], None, ALU.mult)
                    else:
                        i = dve.tensor_scalar(dst, src, mv[:, k, u, 0:1], rstd[:, k, u:u + 1],
                                              ALU.subtract, ALU.mult)
                i.then_inc(done, 1)

            dve.wait_ge(ld_x, 64)
            for j in range(2):
                statistics(0, j, 0)
                normalise(0, j, 0)
            with dve.Fori(2, PAIRS) as j:
                statistics(0, j, 0)
                normalise(0, j, 0)

            def rsqrt_heads(link):
                link(dve.tensor_scalar(qt1[:].bitcast(I32), qss[:].bitcast(I32), 1, None,
                                       ALU.arith_shift_right))
                link(dve.tensor_scalar(qrs[:].bitcast(I32), qt1[:].bitcast(I32), -1.0, MAGIC,
                                       ALU.mult, ALU.add))
                for _ in range(3):
                    link(dve.scalar_tensor_tensor(out=qt1[:], in0=qrs[:], scalar=-0.5, in1=qss[:],
                                                  op0=ALU.mult, op1=ALU.mult))
                    link(dve.tensor_tensor(qt2[:], qt1[:], qrs[:], ALU.mult))
                    link(dve.scalar_tensor_tensor(out=qrs[:], in0=qt2[:], scalar=1.5, in1=qrs[:],
                                                  op0=ALU.add, op1=ALU.mult))

            def heads(ap):
                return ap.rearrange("p (h d) -> p h d", d=D)

            def each_head(ap):
                return ap.unsqueeze(2).to_broadcast([P, 2 * H, D])

            def slot(l, s, at):
                lag = lags(l)
                n = at("out")
                if n is not None:
                    acc = bank[2][:].rearrange("p (h w) -> p h w", w=VW)
                    dve.wait_ge(ob_pe, upto(l, n))
                    ge(dve, oT_pe, upto(l, n - 1))
                    dve.reciprocal(rsum[:], acc[:, :, D]).then_inc(rsum_rdy, 1)
                    dve.wait_ge(rsum_rdy, upto(l, n))
                    dve.tensor_tensor(o[:, 0:C].rearrange("p (h d) -> p h d", d=D), acc[:, :, 0:D],
                                      rsum[:].unsqueeze(2).to_broadcast([P, H, D]), ALU.mult).then_inc(o_rdy, 1)

                def query_stack():
                    n = at("score")
                    if n is None:
                        return
                    par = (s - lag["score"]) % 2
                    dve.wait_ge(tq_pe, upto(l, n))
                    ge(dve, st_pe, upto(l, n - 2, 4))
                    dve.tensor_copy(qT[:, par], bank[2][:].bitcast(BF16)).then_inc(qT_sb, 1)

                def remainder():
                    n = at("split")
                    if n is None:
                        return
                    par = (s - lag["split"]) % 2
                    src = qy[:, par, :] if NORMED[l] else bank[1][:, 0:2 * C]
                    dve.wait_ge(x1_rdy, upto(l, n))
                    ge(dve, x3_rdy, upto(l, n - 2, 2))
                    dve.tensor_tensor(heads(rem[:, par, :]), heads(src), stack[:, par, :, 0:D], ALU.subtract
                                      ).then_inc(rem_rdy, 1)

                query_stack()
                remainder()

                def maxima(groups):
                    n = at("score")
                    if n is None:
                        return
                    par = (s - lag["score"]) % 2
                    for g in groups:
                        dve.wait_ge(s_pe, upto(l, n, 4) - 3 + g)
                        if g == 0:
                            ge(dve, m_rdy, upto(l, n - 2))
                        dve.tensor_reduce(mx[:, par, g * GRP:(g + 1) * GRP],
                                          bank[4 + g % 2][:].rearrange("p (h k) -> p h k", k=T), AX_X, ALU.max
                                          ).then_inc(mx_rdy, 1)

                maxima((0, 1))
                n = at("split")
                if n is not None:
                    par = (s - lag["split"]) % 2
                    slots = stack[:, par, :, 0:MROW].rearrange("p h (k d) -> p h k d", d=SW)
                    dve.wait_ge(x2_rdy, upto(l, n))
                    dve.tensor_copy(slots[:, 0:H, 1:5:3, :],
                                    slots[:, 0:H, 0:1, :].to_broadcast([P, H, 2, SW])).then_inc(slots_rdy, 1)
                    dve.tensor_copy(slots[:, 0:H, 2, :], slots[:, 0:H, 3, :]).then_inc(slots_rdy, 1)
                    dve.tensor_copy(slots[:, H:2 * H, 2:6:3, :],
                                    slots[:, H:2 * H, 0:1, :].to_broadcast([P, H, 2, SW])).then_inc(slots_rdy, 1)
                    dve.tensor_copy(slots[:, H:2 * H, 1, :], slots[:, H:2 * H, 3, :]).then_inc(slots_rdy, 1)
                n = at("out")
                if n is not None:
                    dve.wait_ge(proj_pe, upto(l, n))
                    ge(dve, x_att, upto(l, n - 1))
                    dve.tensor_tensor(gated[:], bank[2][:, 0:C],
                                      mod1[:, bass.ds(n, 1), GATE:GATE + C], ALU.mult).then_inc(gate_rdy, 1)
                maxima((2, 3))
                n = at("qkv")
                if NORMED[l] and n is not None:
                    qk = qkv[:, s % 2, 0:2 * C]
                    y = qy[:, s % 2, :]
                    dve.wait_ge(qkv_sb, upto_n(l, n))
                    ge(dve, x1_rdy, upto(l, n - 2))
                    ge(dve, rem_rdy, upto(l, n - 2))
                    steps = Q_STEPS[l]
                    done = [0]

                    def link(i):
                        done[0] += 1
                        i.then_inc(q_step[l], 1)
                        dve.wait_ge(q_step[l], steps * n + done[0])

                    if l == 3:
                        link(dve.tensor_reduce(qss[:], heads(qk), AX_X, ALU.add))
                        link(dve.scalar_tensor_tensor(out=heads(qk), in0=each_head(qss[:]), scalar=-1.0 / D,
                                                      in1=heads(qk), op0=ALU.mult, op1=ALU.add))
                    link(dve.tensor_tensor(qsq[:], qk, qk, ALU.mult))
                    link(dve.tensor_reduce(qss[:], heads(qsq[:]), AX_X, ALU.add))
                    if l == 3:
                        link(dve.tensor_scalar(qss[:], qss[:], 1.0 / D, QK_EPS, ALU.mult, ALU.add))
                    else:
                        link(dve.tensor_scalar(qss[:], qss[:], TINY, None, ALU.max))
                    rsqrt_heads(link)
                    assert done[0] == steps
                    dve.tensor_tensor(heads(y), heads(qk), each_head(qrs[:]), ALU.mult).then_inc(q_mid, 1)
                    dve.wait_ge(q_mid, upto_n(l, n))

            def mlp_slot(l, j, at):
                n2 = at(-1)
                if n2 is not None:
                    dve.wait_ge(ld_x, 64)
                    dve.wait_ge(x_att, upto(l, 2 * n2 + 1))
                    statistics(l, n2, 1)
                n = at(1)
                if n is not None:
                    if j == 1:
                        dve.wait_ge(ld_mod2, 16 * (l + 1))
                    dve.wait_ge(fc2_pe, upto_p(l, n))
                    ge(dve, x_mlp, upto_p(l, n - 1))
                    dve.tensor_tensor(gated2[:], bank[1][:, 0:2 * C].rearrange("p (u c) -> p u c", u=2),
                                      mod2[:, bass.ds(2 * n, 2), GATE:GATE + C], ALU.mult).then_inc(gate2_rdy, 1)
                    dve.wait_ge(gate2_rdy, upto_p(l, n))
                    xx = x[:, bass.ds(2 * n, 2), :]
                    dve.tensor_tensor(xx, xx, gated2[:], ALU.add).then_inc(x_mlp, 1)
                    if l + 1 < L:
                        dve.wait_ge(ld_x, 64)
                        dve.wait_ge(x_mlp, upto_p(l, n))
                        statistics(l + 1, n, 0)
                if n2 is not None:
                    if j >= 0:
                        dve.wait_ge(hs_rdy, upto(l, B - 1))
                    normalise(l, n2, 1)
                if n is not None and l + 1 < L:
                    dve.wait_ge(hs2_rdy, upto_p(l, n))
                    normalise(l + 1, n, 0)

            for l in range(L):
                attention(dve, l, slot)
                mlp(dve, l, mlp_slot)

        @block.gpsimd
        def _(pool):
            def rstd_of(l, j, k):
                var_s, rstd_s, done = ((ln1_var, ln1_rstd, xn1_rdy), (ln2_var, ln2_rstd, xn2_rdy))[k]
                pool.wait_ge(var_s, upto_p(l, j))
                ge(pool, done, upto_p(l, j - 1))
                pool.tensor_tensor(rstd[:, k, :], var[:, k, :], half_neg[:], ALU.pow).then_inc(rstd_s, 1)

            def heads(ap):
                return ap.rearrange("p (h d) -> p h d", d=D)

            pool.wait_ge(set_ones, 5)
            for j in range(2):
                rstd_of(0, j, 0)
            with pool.Fori(2, PAIRS) as j:
                rstd_of(0, j, 0)

            def slot(l, s, at):
                lag = lags(l, 1)
                n = at("split")
                if n is not None:
                    par = (s - lag["split"]) % 2
                    slots = stack[:, par, :, 0:MROW].rearrange("p h (k d) -> p h k d", d=SW)
                    pool.wait_ge(x2_rdy, upto(l, n))
                    for who, k in ((slice(0, H), 5), (slice(H, 2 * H), 4)):
                        pool.tensor_tensor(slots[:, who, k, 0:D], heads(rem[:, par, :])[:, who, :],
                                           slots[:, who, 3, 0:D], ALU.subtract).then_inc(x3_rdy, 1)
                n = at("out")
                if n is not None:
                    xx = x[:, bass.ds(n, 1), :]
                    pool.wait_ge(gate_rdy, upto(l, n))
                    pool.tensor_tensor(xx, xx, gated[:].unsqueeze(1), ALU.add).then_inc(x_att, 1)
                n = at("ahead")
                if n is not None:
                    par = s % 2
                    if s == 0:
                        pool.wait_ge(ld_mod1, 16 * (l + 1))
                        pool.wait_ge(xn1_rdy, upto_p(l, PAIRS - 1))
                    ge(pool, hT_pe, upto(l, n - 2))
                    h = hs[:, par:par + 1, 0:C]
                    pool.tensor_tensor(h, xn[:, bass.ds(n, 1), :], mod1[:, bass.ds(n, 1), SCALE:SCALE + C],
                                       ALU.mult).then_inc(hs_mul, 1)
                    pool.wait_ge(hs_mul, upto(l, n))
                    pool.tensor_tensor(h, h, mod1[:, bass.ds(n, 1), SHIFT:SHIFT + C], ALU.add
                                       ).then_inc(hs_rdy, 1)
                n = at("score")
                if n is not None:
                    par = (s - lag["score"]) % 2
                    parts = m3[:, par, 0:3 * H].rearrange("p (e j h a) -> p e j h a", e=2, j=3, h=2)
                    full = mx[:, par, :].rearrange("p (h e a) -> p e h a", h=2, e=2)
                    rest = mrem[:, par, :].rearrange("p (h e a) -> p e h a", h=2, e=2)
                    pool.wait_ge(mx_rdy, upto(l, n, 4))
                    ge(pool, mT_pe, upto(l, n - 2))
                    zero = zeros[:].rearrange("p (h e a) -> p e h a", h=2, e=2)
                    pool.tensor_tensor(parts[:, :, 0], full, zero, ALU.add).then_inc(m_step, 1)
                    pool.wait_ge(m_step, upto(l, n, 3) - 2)
                    pool.tensor_tensor(rest, full, parts[:, :, 0], ALU.subtract).then_inc(m_step, 1)
                    pool.wait_ge(m_step, upto(l, n, 3) - 1)
                    pool.tensor_tensor(parts[:, :, 1], rest, zero, ALU.add).then_inc(m_step, 1)
                    pool.wait_ge(m_step, upto(l, n, 3))
                    pool.tensor_tensor(parts[:, :, 2], rest, parts[:, :, 1], ALU.subtract
                                       ).then_inc(m_rdy, 1)
                n = at("qkv")
                if NORMED[l] and n is not None:
                    y = qy[:, (s - 1) % 2, :]
                    pool.wait_ge(q_mid, upto_n(l, n))
                    if l == 1:
                        pool.tensor_tensor(y, y, qk_g[:, 0, :], ALU.mult).then_inc(q_rdy, 1)
                    else:
                        pool.tensor_tensor(y, y, qk_g[:, 1, :], ALU.mult).then_inc(q_gain, 1)
                        pool.wait_ge(q_gain, n + 1)
                        pool.tensor_tensor(y, y, qk_b[:], ALU.add).then_inc(q_rdy, 1)

            def mlp_slot(l, j, at):
                n2, n = at(-1), at(1)
                if n2 is not None:
                    rstd_of(l, n2, 1)
                if n is not None and l + 1 < L:
                    rstd_of(l + 1, n, 0)
                if n2 is not None:
                    par = (j + 1) % 2
                    pool.wait_ge(xn2_rdy, upto_p(l, n2))
                    if j == -1:
                        pool.wait_ge(ld_mod2, 16 * (l + 1))
                    ge(pool, h2T_pe, upto_p(l, n2 - 2))
                    h = hs2[:, par, :, 0:C]
                    b = bass.ds(2 * n2, 2)
                    pool.tensor_tensor(h, xn[:, b, :], mod2[:, b, SCALE:SCALE + C], ALU.mult
                                       ).then_inc(hs2_mul, 1)
                    pool.wait_ge(hs2_mul, upto_p(l, n2))
                    pool.tensor_tensor(h, h, mod2[:, b, SHIFT:SHIFT + C], ALU.add).then_inc(hs2_rdy, 1)

            for l in range(L):
                attention(pool, l, slot, behind=1)
                mlp(pool, l, mlp_slot)


def pack(i):
    import numpy as np

    def f(name):
        return np.asarray(i[name])

    one = np.ones((C,), np.float32)
    zero = np.zeros((C,), np.float32)
    wcat = np.zeros((L, C + 1, WCOLS + ACOLS), np.float32)
    w2cat = np.zeros((L, P, FC, C), np.float32)
    names = [
        ("L0_cond_W_qkv", "L0_cond_b_qkv", "L0_cond_W_proj", "L0_cond_b_proj", "L0_cond_W_fc1", "L0_cond_b_fc1",
         "L0_cond_W_ada", "L0_cond_b_ada", "L0_cond_W_fc2", "L0_cond_b_fc2"),
        ("L1_cond_qkv_w", "L1_cond_qkv_b", "L1_cond_proj_w", "L1_cond_proj_b", "L1_cond_fc1_w", "L1_cond_fc1_b",
         "L1_cond_ada_w", "L1_cond_ada_b", "L1_cond_fc2_w", "L1_cond_fc2_b"),
        (None, None, "L2_cond_wo", "L2_cond_wo_b", "L2_cond_fc1_w", "L2_cond_fc1_b",
         "L2_cond_ada_w", "L2_cond_ada_b", "L2_cond_fc2_w", "L2_cond_fc2_b"),
        ("L3_cond_w_qkv", "L3_cond_b_qkv", "L3_cond_w_proj", "L3_cond_b_proj", "L3_cond_w1", "L3_cond_b1",
         "L3_cond_w_ada", "L3_cond_b_ada", "L3_cond_w2", "L3_cond_b2"),
    ]
    for l, row in enumerate(names):
        for k, (at, width) in enumerate(((QKV, 3 * C), (PROJ, C), (FC1, FF), (ADA, ACOLS))):
            if row[2 * k] is None:
                for m, name in enumerate(("L2_cond_wq", "L2_cond_wk", "L2_cond_wv")):
                    wcat[l, 0:C, at + m * C:at + (m + 1) * C] = f(name)
                continue
            w = f(row[2 * k])
            w = w.T if l == 1 else w
            wcat[l, 0:C, at:at + width] = w.reshape(H, D, C)[HEAD_ORDER].reshape(C, C) if at == PROJ else w
            wcat[l, C, at:at + width] = f(row[2 * k + 1])
        w = f(row[8])
        w = w.T if l == 1 else w
        for c in range(FC):
            m = P if c < FC - 1 else FL
            w2cat[l, 0:m, c, :] = w[c * P:c * P + m]
        w2cat[l, FL, FC - 1, :] = f(row[9])
    aff = np.stack([
        np.stack([np.stack([one, zero])] * 2),
        np.stack([np.stack([np.broadcast_to(f("L1_cond_g1"), (C,)), zero]),
                  np.stack([np.broadcast_to(f("L1_cond_g2"), (C,)), zero])]),
        np.stack([np.stack([f("L2_cond_ln1_w"), f("L2_cond_ln1_b")]),
                  np.stack([f("L2_cond_ln2_w"), f("L2_cond_ln2_b")])]),
        np.stack([np.stack([one, zero])] * 2),
    ])
    qkaff = np.zeros((2, 2, 2 * C), np.float32)
    qkaff[0, 0] = np.concatenate([np.broadcast_to(f("L1_cond_qg"), (C,)), np.broadcast_to(f("L1_cond_kg"), (C,))])
    qkaff[1, 0] = np.concatenate([np.tile(f("L3_cond_qn_g"), H), np.tile(f("L3_cond_kn_g"), H)])
    qkaff[1, 1] = np.concatenate([np.tile(f("L3_cond_qn_b"), H), np.tile(f("L3_cond_kn_b"), H)])
    return {
        "x": np.ascontiguousarray(f("x")),
        "cT": np.ascontiguousarray(f("cond_1152").T),
        "wcat": wcat,
        "w2cat": w2cat,
        "aff": np.ascontiguousarray(aff),
        "qkaff": qkaff,
        "ident": np.eye(P, dtype=np.float32),
    }


def kernel(**inputs):
    import concourse.bacc as bacc
    import numpy as np
    from concourse.bass_utils import run_bass_kernel_spmd

    nc = bacc.Bacc("TRN2", target_bir_lowering=False, num_devices=1)
    arrays, args = {}, []
    for name, a in pack(inputs).items():
        arrays[f"in_{name}"] = a
        args.append(nc.dram_tensor(f"in_{name}", a.shape, mybir.dt.from_np(a.dtype), kind="ExternalInput").ap())
    args.append(nc.dram_tensor("out_x", (B, T, C), mybir.dt.from_np(np.dtype("float32")),
                               kind="ExternalOutput").ap())
    build(nc, *args)
    return run_bass_kernel_spmd(nc, [arrays], core_ids=[0]).results[0]["out_x"]
```

```python
from contextlib import ExitStack

import concourse.bass as bass
from concourse import mybir

F32 = mybir.dt.float32
BF16 = mybir.dt.bfloat16
I32 = mybir.dt.int32
ALU = mybir.AluOpType
ACT = mybir.ActivationFunctionType
AX_X = mybir.AxisListType.X

L = 4
B, T, C = 16, 128, 144
H = 16
D = C // H
P = 128
CR = C - P
KB = CR + 1
KS = 6 * CR + 3
FF = 4 * C
FC = (FF + P - 1) // P
FL = FF - (FC - 1) * P
PAIRS = B // 2
QKV, FC1, PROJ, ADA = 0, 3 * C, 3 * C + FF, 4 * C + FF
SCOLS = PROJ
WCOLS = ADA
ACOLS = 6 * C
SHIFT, SCALE, GATE = 0, C, 2 * C
SW = D + 1
NSLOT = 6
MROW = NSLOT * SW
HW = 64
GRP = 4
NG = H // GRP
VW = 32
HEAD_ORDER = [8 * (g // 2) + 2 * a + g % 2 for g in range(NG) for a in range(GRP)]
LN_EPS = (1e-6, None, 1e-5, 1e-6)
QK_EPS = 1e-5
TINY = 1e-24
MAGIC = float(0x5F3759DF)
KEY_FILL, QUERY_FILL, VALUE_FILL, FC2_FILL = (2, 0), (2, 0), 2, 2
START_FILL = 12
NORMED = (False, True, False, True)
Q_STEPS = {1: 14, 3: 16}


def build(nc, x_in, cT, wcat, wlast, masks, w2cat, aff, qkaff, ident, out):
    scratch = nc.dram_tensor("mod_scratch", (B, L, ACOLS), F32, kind="Internal").ap()
    ctx = ExitStack()
    with ctx:
        def sb(name, shape, dt=F32):
            return ctx.enter_context(nc.sbuf_tensor(name, shape, dt))

        def sem(name):
            return ctx.enter_context(nc.semaphore(name))

        x = sb("x", [P, B, C])
        xn = sb("xn", [P, B, C])
        mod1 = sb("mod1", [P, B, 3 * C])
        mod2 = sb("mod2", [P, B, 3 * C])
        wa = sb("wa", [P, 2, WCOLS])
        wb = sb("wb", [KB, 2, C])
        ws_raw = sb("ws_raw", [KS, SCOLS])
        ws_tmp = sb("ws_tmp", [KS, SCOLS])
        ws_part = sb("ws_part", [KS, SCOLS], BF16)
        ws = sb("ws", [KS, 2, SCOLS], BF16)
        part_mask = sb("part_mask", [KS, 2])
        bs = sb("bs", [P, 2, KS], BF16)
        bs_rem = sb("bs_rem", [P, 2, CR])
        bs2 = sb("bs2", [P, 2, 2, KS], BF16)
        bs2_rem = sb("bs2_rem", [P, 2, 2, CR])
        w2 = sb("w2", [P, 2, FC, C])
        idf = sb("idf", [P, P])
        idb = sb("idb", [P, P], BF16)
        busy = sb("busy", [P, 512], BF16)
        half_neg = sb("half_neg", [P, 2])
        qk_g = sb("qk_g", [P, 2, 2 * C])
        qk_b = sb("qk_b", [P, 2 * C])
        hs = sb("hs", [P, 2, C])
        hs2 = sb("hs2", [P, 2, 2, C])
        hA = sb("hA", [P, P])
        hB = sb("hB", [KS, P], BF16)
        stack = sb("stack", [P, 2, 2 * H, HW], BF16)
        rem = sb("rem", [P, 2, 2 * C])
        qT = sb("qT", [P, 2, H // 2, T], BF16)
        kT = sb("kT", [P, 2, H // 2, T], BF16)
        mx = sb("mx", [P, 2, H])
        mrem = sb("mrem", [P, 2, H])
        zeros = sb("zeros", [P, H])
        m3 = sb("m3", [P, 2, P], BF16)
        mT = sb("mT", [48, 2, T], BF16)
        e = sb("e", [P, H, T])
        v = sb("v", [P, 2, H, VW])
        oT = sb("oT", [P, NG, T])
        rsum = sb("rsum", [P, H])
        o = sb("o", [P, C + 1])
        otA = sb("otA", [P, P])
        otB = sb("otB", [KB, P])
        gated = sb("gated", [P, C])
        qkv = sb("qkv", [P, 2, 3 * C])
        qsq = sb("qsq", [P, 2 * C])
        qss = sb("qss", [P, 2 * H])
        qrs = sb("qrs", [P, 2 * H])
        qt1 = sb("qt1", [P, 2 * H])
        qt2 = sb("qt2", [P, 2 * H])
        qy = sb("qy", [P, 2, 2 * C])
        st6 = sb("st6", [P, 2, 2, 6])
        mv = sb("mv", [P, 2, 2, 2])
        var = sb("var", [P, 2, 2])
        rstd = sb("rstd", [P, 2, 2])
        h2A = sb("h2A", [P, 2, 2 * T])
        h2B = sb("h2B", [KS, 2, 2 * T], BF16)
        gT = sb("gT", [P, 2, FC, 2 * T])
        gated2 = sb("gated2", [P, 2, C])
        ada_a = sb("ada_a", [P, ACOLS])
        ada_b = sb("ada_b", [KB, ACOLS])
        c_a = sb("c_a", [P, B])
        c_b = sb("c_b", [CR, B])
        s_a = sb("s_a", [P, B])
        s_b = sb("s_b", [KB, B])
        aff_sb = sb("aff_sb", [B, L, 2, 2, C])
        m_sb = sb("m_sb", [B, L, ACOLS])
        sc1 = sb("sc1", [B, 2, C])
        shb = sb("shb", [B, 2, C])

        bank = [ctx.enter_context(nc.psum_tensor(f"bank{i}", [P, 512], F32)) for i in range(8)]

        ld_const, ld_x, ld_ada, ld_mod1, ld_mod2, ld_aff = (
            sem(n) for n in ("ld_const", "ld_x", "ld_ada", "ld_mod1", "ld_mod2", "ld_aff"))
        ld_w = [sem(f"ld_w{i}") for i in range(2)]
        set_ones, set_idb, silu_done, ada_mm, ada_sc, ada_b1, ada_mod, ada_gate, mod_out, set_qk = (
            sem(n) for n in ("set_ones", "set_idb", "silu_done", "ada_mm", "ada_sc", "ada_b1", "ada_mod",
                             "ada_gate", "mod_out", "set_qk"))
        hT_pe, qkv_pe, tk_pe, tq_pe, s_pe, mT_pe, st_pe, av_pe, ob_pe, oT_pe, proj_pe = (
            sem(n) for n in ("hT_pe", "qkv_pe", "tk_pe", "tq_pe", "s_pe", "mT_pe", "st_pe", "av_pe",
                             "ob_pe", "oT_pe", "proj_pe"))
        hs_mul, hs_rdy, hT_sb, x1_rdy, x2_rdy, rem_rdy, x3_rdy, slots_rdy, v_sb, kT_sb, qT_sb = (
            sem(n) for n in ("hs_mul", "hs_rdy", "hT_sb", "x1_rdy", "x2_rdy", "rem_rdy", "x3_rdy",
                             "slots_rdy", "v_sb", "kT_sb", "qT_sb"))
        mx_rdy, m_step, m_rdy, mT_sb, m_rows, e_rdy, ot_sb, rsum_rdy, o_rdy, oT_sb, gate_rdy, x_att = (
            sem(n) for n in ("mx_rdy", "m_step", "m_rdy", "mT_sb", "m_rows", "e_rdy", "ot_sb", "rsum_rdy",
                             "o_rdy", "oT_sb", "gate_rdy", "x_att"))
        qkv_sb, q_mid, q_gain, q_rdy = (sem(n) for n in ("qkv_sb", "q_mid", "q_gain", "q_rdy"))
        ld_ws, ws_step, ws_rdy, bs_step, bs_rdy, bs2_step, bs2_rdy = (
            sem(n) for n in ("ld_ws", "ws_step", "ws_rdy", "bs_step", "bs_rdy", "bs2_step", "bs2_rdy"))
        q_step = {l: sem(f"q_step{l}") for l in range(L) if NORMED[l]}
        h2T_pe, fc1_pe, fc2_pe, h2T_sb, gelu_rdy, gate2_rdy, x_mlp, hs2_mul, hs2_rdy = (
            sem(n) for n in ("h2T_pe", "fc1_pe", "fc2_pe", "h2T_sb", "gelu_rdy", "gate2_rdy", "x_mlp",
                             "hs2_mul", "hs2_rdy"))
        ln_mv, ln_sq, ln_sum = ([sem(f"{n}{k + 1}") for k in range(2)]
                                       for n in ("ln_mv", "ln_sq", "ln_sum"))
        ln1_var, ln1_rstd, xn1_rdy, ln2_var, ln2_rstd, xn2_rdy, out_done = (
            sem(n) for n in ("ln1_var", "ln1_rstd", "xn1_rdy", "ln2_var", "ln2_rstd", "xn2_rdy", "out_done"))

        def ge(eng, s, value):
            if isinstance(value, int) and value <= 0:
                return
            assert isinstance(value, int) or value.min_val > 0
            eng.wait_ge(s, value)

        def upto(l, b, per=1):
            return (b + (16 * l + 1)) * per

        def upto_p(l, j, per=1):
            return (j + (PAIRS * l + 1)) * per

        def upto_n(l, b, per=1):
            return (b + (16 * (l // 2) + 1)) * per

        def lags(l, behind=0):
            d = int(NORMED[l])
            return dict(ahead=-behind, qkv=behind, split=d + behind, score=1 + d + behind, prob=2 + d + behind,
                        out=3 + d + behind)

        def attention(eng, l, slot, behind=0):
            lag = lags(l, behind)
            first = lag["out"] + 1 + (lag["out"] + 1) % 2
            start = min(0, lag["ahead"])
            if l == 0:
                first += 2

            def plain(s):
                slot(l, s, lambda k: s - lag[k] if 0 <= s - lag[k] < B else None)
            for s in range(start, first):
                plain(s)
            end = B - 2 * behind
            with eng.Fori(first // 2, end // 2) as i:
                for u in range(2):
                    slot(l, first + u, lambda k, u=u: 2 * i + (u - lag[k]))
            for s in range(end, B + lag["out"]):
                plain(s)

        def mlp(eng, l, slot):
            def plain(j):
                slot(l, j, lambda k: j - k if 0 <= j - k < PAIRS else None)
            for j in (-2, -1, 0, 1):
                plain(j)
            with eng.Fori(1, PAIRS // 2 - 1) as i:
                for u in range(2):
                    slot(l, 2 + u, lambda k, u=u: 2 * i + (u - k))
            for j in (PAIRS - 2, PAIRS - 1, PAIRS):
                plain(j)

        def head(g, a):
            return HEAD_ORDER[GRP * g + a]

        def last(l, s, lag):
            return 0 <= s - 1 - lag < B

        def load_mod(eng, l, half):
            eng.dma_start((mod1, mod2)[half][:],
                          scratch[:, l, half * 3 * C:(half + 1) * 3 * C].partition_broadcast(P)
                          ).then_inc((ld_mod1, ld_mod2)[half], 16)

        def load_w(eng, l):
            eng.dma_start(wa[:, l % 2, :], wcat[l, 0:P, 0:WCOLS]).then_inc(ld_w[l % 2], 16)
            eng.dma_start(wb[:, l % 2, :], wcat[l, P:P + KB, PROJ:PROJ + C]).then_inc(ld_w[l % 2], 16)
            eng.dma_start(w2[:, l % 2], w2cat[l]).then_inc(ld_w[l % 2], 16)

        def load_ws(eng, l):
            ge(eng, ws_rdy, l)
            eng.dma_start(ws_raw[:], wlast[l]).then_inc(ld_ws, 16)

        block = ctx.enter_context(nc.Block())

        @block.sync
        def _(sp):
            sp.dma_start(c_a[:], cT[0:P, :]).then_inc(ld_const, 16)
            sp.dma_start(c_b[:], cT[P:C, :]).then_inc(ld_const, 16)
            sp.dma_start(idf[:], ident).then_inc(ld_const, 16)
            sp.dma_start(aff_sb[:], aff.partition_broadcast(B)).then_inc(ld_aff, 16)
            sp.dma_start(part_mask[:], masks).then_inc(ld_aff, 16)
            for l in range(L):
                if l:
                    sp.wait_ge(ada_mm, l)
                sp.dma_start(ada_a[:], wcat[l, 0:P, ADA:]).then_inc(ld_ada, 16)
                sp.dma_start(ada_b[:], wcat[l, P:P + KB, ADA:]).then_inc(ld_ada, 16)
                if l == 0:
                    for q in range(4):
                        sp.dma_start(x[:, 4 * q:4 * q + 4, :],
                                     x_in[4 * q:4 * q + 4].rearrange("b t c -> t b c")).then_inc(ld_x, 16)
                    sp.dma_start(qk_g[:], qkaff[:, 0, :].partition_broadcast(P)).then_inc(ld_aff, 16)
                    sp.dma_start(qk_b[:], qkaff[1, 1, :].partition_broadcast(P)).then_inc(ld_aff, 16)
                    load_ws(sp, 0)
                    load_w(sp, 0)
            sp.wait_ge(ada_mod, 2 * L)
            sp.wait_ge(ada_gate, L)
            sp.dma_start(scratch, m_sb[:]).then_inc(mod_out, 16)
            sp.wait_ge(mod_out, 16)

            load_mod(sp, 0, 0)
            load_mod(sp, 0, 1)
            load_w(sp, 1)
            load_ws(sp, 1)

            def slot(l, s, at):
                n = at("prob")
                if n is None:
                    return
                par = (s - lags(l)["prob"]) % 2
                sp.wait_ge(mT_sb, upto(l, n))
                for half in range(2):
                    sp.dma_start(qT[HW * half + MROW:HW * half + MROW + 3, par],
                                 mT[24 * half:24 * half + 24, par, :]).then_inc(m_rows, 16)

            for l in range(L):
                attention(sp, l, slot)
            for q in range(PAIRS):
                sp.wait_ge(x_mlp, upto_p(L - 1, q))
                sp.dma_start(out[2 * q:2 * q + 2].rearrange("b t c -> t b c"), x[:, 2 * q:2 * q + 2, :]
                             ).then_inc(out_done, 16)
            sp.wait_ge(out_done, 16 * PAIRS)

        @block.tensor
        def _(pe):
            pe.wait_ge(silu_done, 2)
            for l in range(L):
                pe.wait_ge(ld_ada, 32 * (l + 1))
                if l:
                    pe.wait_ge(ada_mod, 2 * l)
                    pe.wait_ge(ada_gate, l)
                for half in range(2):
                    cols = slice(half * 3 * C, (half + 1) * 3 * C)
                    pe.matmul(bank[half][0:B, 0:3 * C], s_a[:], ada_a[:, cols], start=True, stop=False)
                    mm = pe.matmul(bank[half][0:B, 0:3 * C], s_b[:], ada_b[:, cols], start=False, stop=True)
                mm.then_inc(ada_mm, 1)
            pe.wait_ge(ada_mod, 2 * L)
            pe.wait_ge(ada_gate, L)
            pe.wait_ge(set_idb, 1)

            bank1b = bank[1][:].bitcast(BF16)
            bank2b = bank[2][:].bitcast(BF16)
            bank3b = bank[3][:].bitcast(BF16)
            bank0b = bank[0][:].bitcast(BF16)

            def keep_clock(b, count):
                for _ in range(count):
                    pe.matmul(bank[b][:], idb[:], busy[:], start=True, stop=True)

            def slot(l, s, at):
                lag = lags(l)
                w = l % 2
                ns, ps = at("score"), (s - lag["score"]) % 2
                np_, pp = at("prob"), (s - lag["prob"]) % 2
                no, nq = at("out"), at("qkv")

                def qkv_read(n):
                    pe.wait_ge(qkv_sb, upto(l, n))
                    if not NORMED[l]:
                        pe.wait_ge(rem_rdy, upto(l, n))

                def key_scores(n, par, half):
                    ge(pe, e_rdy, upto(l, n, 4) - 4 + 2 * half)
                    keep_clock(6, KEY_FILL[half])
                    if half == 0:
                        pe.wait_ge(m_rows, upto(l, n, 32))
                    for a in range(GRP):
                        for odd in range(2):
                            r = slice(HW * odd, HW * odd + MROW + 3)
                            mm = pe.matmul(bank[6 + odd][:, a * T:(a + 1) * T], kT[r, par, GRP * half + a, :],
                                           qT[r, par, GRP * half + a, :], start=True, stop=True)
                            if a == GRP - 1:
                                mm.then_inc(st_pe, 1)

                def query_scores(n, par, half):
                    ge(pe, mx_rdy, upto(l, n, 4) - 4 + 2 * half)
                    keep_clock(4, QUERY_FILL[half])
                    if half == 0:
                        pe.wait_ge(kT_sb, upto(l, n))
                        pe.wait_ge(qT_sb, upto(l, n))
                    for a in range(GRP):
                        for odd in range(2):
                            r = slice(HW * odd, HW * odd + MROW)
                            mm = pe.matmul(bank[4 + odd][:, a * T:(a + 1) * T], qT[r, par, GRP * half + a, :],
                                           kT[r, par, GRP * half + a, :], start=True, stop=True)
                            if a == GRP - 1:
                                mm.then_inc(s_pe, 1)

                def values(n, par, g):
                    if g == 0:
                        pe.wait_ge(v_sb, upto(l, n))
                        if at("score") is not None:
                            pe.wait_ge(kT_sb, upto(l, at("score")))
                        else:
                            pe.wait_ge(ot_sb, upto(l, n - 1))
                        keep_clock(3, VALUE_FILL)
                    pe.wait_ge(e_rdy, upto(l, n, 4) - 3 + g)
                    for a in range(GRP):
                        h = head(g, a)
                        mm = pe.matmul(bank[3][VW * a:VW * (a + 1), g * T:(g + 1) * T], v[:, par, h, :],
                                       e[:, g * GRP + a, :], start=True, stop=True, tile_position=(0, VW * a))
                    mm.then_inc(av_pe, 1)

                if s == 1:
                    keep_clock(7, START_FILL)
                if ns is not None:
                    pe.wait_ge(slots_rdy, upto(l, ns, 4))
                    pe.wait_ge(x3_rdy, upto(l, ns, 2))
                    if last(l, s, 0):
                        qkv_read(ns + (lag["score"] - 1))
                    else:
                        pe.wait_ge(qT_sb, upto(l, ns - 1))
                    for i in range(H // 2):
                        tr = pe.transpose(bank1b[:, i * P:(i + 1) * P], stack[:, ps, 2 * i:2 * i + 2, :], idb[:])
                    tr.then_inc(tq_pe, 1)
                if nq is not None:
                    pe.wait_ge(bs_rdy, upto(l, nq))
                    if last(l, s, lag["out"]):
                        pe.wait_ge(oT_sb, upto(l, no - 1))
                    elif last(l, s, 0):
                        pe.wait_ge(hT_sb, upto(l, nq - 1))
                    par = s % 2
                    pe.transpose(bank[0][:, 0:P], hs[:, par, 0:P], idf[:])
                    pe.transpose(bank0b[0:KS, 2 * P:3 * P], bs[:, par, :], idb[:]).then_inc(hT_pe, 1)
                if no is not None:
                    values(no, (s - lag["out"]) % 2, 2)
                    values(no, (s - lag["out"]) % 2, 3)
                if np_ is not None:
                    if last(l, s, lag["out"]):
                        pe.wait_ge(gate_rdy, upto(l, no - 1))
                    elif last(l, s, lag["prob"]):
                        pe.wait_ge(mT_sb, upto(l, np_ - 1))
                    pe.wait_ge(m_rdy, upto(l, np_))
                    pe.transpose(bank2b[:, 0:P], m3[:, pp, :], idb[:]).then_inc(mT_pe, 1)
                if ns is not None:
                    if last(l, s, lag["prob"]):
                        pe.wait_ge(ot_sb, upto(l, ns + (lag["score"] - lag["prob"] - 1)))
                    elif last(l, s, lag["score"]):
                        pe.wait_ge(kT_sb, upto(l, ns - 1))
                    for i in range(H // 2):
                        tr = pe.transpose(bank3b[:, i * P:(i + 1) * P],
                                          stack[:, ps, H + 2 * i:H + 2 * i + 2, :], idb[:])
                    tr.then_inc(tk_pe, 1)
                if no is not None:
                    pe.wait_ge(ot_sb, upto(l, no))
                    if np_ is not None:
                        pe.wait_ge(mT_sb, upto(l, np_))
                    else:
                        pe.wait_ge(gate_rdy, upto(l, no - 1))
                    for g in range(NG):
                        tr = pe.transpose(bank[2][:, g * P:(g + 1) * P], oT[:, g, :], idf[:])
                    tr.then_inc(ob_pe, 1)
                if nq is not None:
                    if s == 0:
                        pe.wait_ge(ld_w[w], 48 * (l // 2 + 1))
                        pe.wait_ge(ws_rdy, l + 1)
                        if l:
                            pe.wait_ge(gate2_rdy, upto_p(l - 1, PAIRS - 1))
                    pe.wait_ge(hT_sb, upto(l, nq))
                    if ns is not None:
                        pe.wait_ge(qT_sb, upto(l, ns))
                    elif last(l, s, 0):
                        qkv_read(nq - 1)
                    pe.matmul(bank[1][:, 0:3 * C], hA[:], wa[:, w, QKV:QKV + 3 * C], start=True, stop=False)
                    pe.matmul(bank[1][:, 0:3 * C], hB[:], ws[:, w, QKV:QKV + 3 * C], start=False, stop=True
                              ).then_inc(qkv_pe, 1)

                if ns is not None:
                    query_scores(ns, ps, 0)
                if no is not None:
                    pe.wait_ge(o_rdy, upto(l, no))
                    if nq is not None:
                        pe.wait_ge(hT_sb, upto(l, nq))
                    else:
                        pe.wait_ge(oT_sb, upto(l, no - 1))
                    pe.transpose(bank[0][:, 0:P], o[:, 0:P], idf[:])
                    pe.transpose(bank[0][0:KB, P:2 * P], o[:, P:C + 1], idf[:]).then_inc(oT_pe, 1)
                if np_ is not None:
                    key_scores(np_, pp, 0)
                if ns is not None:
                    query_scores(ns, ps, 1)
                if no is not None:
                    pe.wait_ge(oT_sb, upto(l, no))
                    pe.matmul(bank[2][:, 0:C], otA[:], wa[:, w, PROJ:PROJ + C], start=True, stop=False)
                    pe.matmul(bank[2][:, 0:C], otB[:], wb[:, w, :], start=False, stop=True
                              ).then_inc(proj_pe, 1)
                if np_ is not None:
                    values(np_, pp, 0)
                    values(np_, pp, 1)
                    key_scores(np_, pp, 1)

            def mlp_slot(l, j, at):
                w = l % 2
                n = at(0)
                if n is not None:
                    par = j % 2
                    pe.wait_ge(bs2_rdy, upto_p(l, n))
                    if j == 0:
                        pe.wait_ge(oT_sb, upto(l, B - 1))
                    else:
                        pe.wait_ge(h2T_sb, upto_p(l, n - 1, 2))
                    for u in range(2):
                        pe.transpose(bank[0][:, u * P:(u + 1) * P], hs2[:, par, u, 0:P], idf[:])
                    for u in range(2):
                        tr = pe.transpose(bank0b[0:KS, (4 + u) * P:(5 + u) * P], bs2[:, par, u, :], idb[:])
                    tr.then_inc(h2T_pe, 1)
                n = at(1)
                if n is not None:
                    par = (j - 1) % 2
                    if j > 1:
                        pe.wait_ge(gate2_rdy, upto_p(l, n - 1))
                    keep_clock(1, FC2_FILL)
                    pe.wait_ge(gelu_rdy, upto_p(l, n, 3))
                    for u in range(2):
                        for c in range(FC):
                            k = P if c < FC - 1 else FL + 1
                            mm = pe.matmul(bank[1][:, u * C:(u + 1) * C], gT[0:k, par, c, u * T:(u + 1) * T],
                                           w2[0:k, w, c, :], start=(c == 0), stop=(c == FC - 1))
                    mm.then_inc(fc2_pe, 1)
                n = at(0)
                if n is not None:
                    par = j % 2
                    pe.wait_ge(h2T_sb, upto_p(l, n, 2))
                    if j == 0:
                        pe.wait_ge(gate_rdy, upto(l, B - 1))
                        pe.wait_ge(mx_rdy, upto(l, B - 1, 4))
                    for c in range(FC):
                        m = P if c < FC - 1 else FL
                        dst = bank[2 + 3 * par + c // 2][0:m, (c % 2) * 2 * T:(c % 2 + 1) * 2 * T]
                        cols = slice(FC1 + c * P, FC1 + c * P + m)
                        pe.matmul(dst, wa[:, w, cols], h2A[:, par, :], start=True, stop=False)
                        cols = slice(FC1 + c * P, FC1 + c * P + m)
                        mm = pe.matmul(dst, ws[:, w, cols], h2B[:, par, :], start=False, stop=True)
                        if c % 2 or c == FC - 1:
                            mm.then_inc(fc1_pe, 1)

            for l in range(L):
                attention(pe, l, slot)
                mlp(pe, l, mlp_slot)

        @block.scalar
        def _(act):
            act.wait_ge(ld_const, 48)
            act.wait_ge(set_ones, 1)
            act.activation(s_a[:], c_a[:], ACT.Silu).then_inc(silu_done, 1)
            act.activation(s_b[0:CR, :], c_b[:], ACT.Silu).then_inc(silu_done, 1)
            gates = m_sb[:].rearrange("b l (h k c) -> b l h k c", h=2, k=3)
            for l in range(L):
                act.wait_ge(ada_mm, l + 1)
                for half in range(2):
                    i = act.activation(gates[:, l, half, 2, :], bank[half][0:B, GATE:GATE + C],
                                       ACT.Tanh if l == 1 else ACT.Copy)
                i.then_inc(ada_gate, 1)

            def slot(l, s, at):
                lag = lags(l)
                n = at("qkv")
                if n is not None:
                    act.wait_ge(hT_pe, upto(l, n))
                    ge(act, qkv_pe, upto(l, n - 1))
                    act.copy(hA[:], bank[0][:, 0:P])
                    act.copy(hB[:], bank[0][0:KS, P:P + P // 2].bitcast(BF16)).then_inc(hT_sb, 1)
                n = at("prob")
                if n is not None:
                    par = (s - lag["prob"]) % 2
                    act.wait_ge(mT_pe, upto(l, n))
                    ge(act, m_rows, upto(l, n - 2, 32))
                    act.copy(mT[:, par, :], bank[2][0:48, 0:P // 2].bitcast(BF16)).then_inc(mT_sb, 1)
                n = at("score")
                if n is not None:
                    par = (s - lag["score"]) % 2
                    act.wait_ge(tk_pe, upto(l, n))
                    ge(act, st_pe, upto(l, n - 2, 4))
                    act.copy(kT[:, par], bank[3][:].bitcast(BF16)).then_inc(kT_sb, 1)
                    act.wait_ge(qkv_sb, upto(l, n))
                    ge(act, av_pe, upto(l, n - 2, 4))
                    act.copy(v[:, par, :, 0:D],
                             qkv[:, par, 2 * C:3 * C].rearrange("p (h d) -> p h d", d=D)).then_inc(v_sb, 1)

                def first_part():
                    n = at("split")
                    if n is None:
                        return
                    par = (s - lag["split"]) % 2
                    if NORMED[l]:
                        act.wait_ge(q_rdy, upto_n(l, n))
                        src = qy[:, par, :]
                    else:
                        act.wait_ge(qkv_pe, upto(l, n))
                        src = bank[1][:, 0:2 * C]
                    ge(act, tq_pe, upto(l, n - 2))
                    ge(act, tk_pe, upto(l, n - 2))
                    act.copy(stack[:, par, :, 0:D], src.rearrange("p (h d) -> p h d", d=D)).then_inc(x1_rdy, 1)

                def copy_qkv():
                    n = at("qkv")
                    if n is not None:
                        act.wait_ge(qkv_pe, upto(l, n))
                        if s >= 2:
                            act.wait_ge(v_sb, upto(l, n - 2))
                            if NORMED[l]:
                                act.wait_ge(q_mid, upto_n(l, n - 2))
                        cols = slice(0 if NORMED[l] else 2 * C, 3 * C)
                        act.copy(qkv[:, s % 2, cols], bank[1][:, cols]).then_inc(qkv_sb, 1)

                if NORMED[l]:
                    first_part()
                    copy_qkv()
                else:
                    copy_qkv()
                    first_part()

                def exps(groups):
                    n = at("prob")
                    if n is None:
                        return
                    for g in groups:
                        act.wait_ge(st_pe, upto(l, n, 4) - 3 + g)
                        ge(act, av_pe, upto(l, n - 1, 4) - 3 + g)
                        act.activation(e[:, g * GRP:(g + 1) * GRP, :], bank[6 + g % 2][:], ACT.Exp,
                                       scale=float(D) ** -0.5).then_inc(e_rdy, 1)

                n = at("out")
                if n is not None:
                    act.wait_ge(oT_pe, upto(l, n))
                    ge(act, proj_pe, upto(l, n - 1))
                    act.copy(otA[:], bank[0][:, 0:P])
                    act.copy(otB[:], bank[0][0:KB, P:2 * P]).then_inc(oT_sb, 1)
                exps((0,))
                n = at("split")
                if n is not None:
                    par = (s - lag["split"]) % 2
                    act.wait_ge(rem_rdy, upto(l, n))
                    act.copy(stack[:, par, :, 3 * SW:3 * SW + D],
                             rem[:, par, :].rearrange("p (h d) -> p h d", d=D)).then_inc(x2_rdy, 1)
                exps((1,))
                exps((2, 3))
                n = at("prob")
                if n is not None:
                    act.wait_ge(av_pe, upto(l, n, 4))
                    ge(act, ob_pe, upto(l, n - 1))
                    act.copy(oT[:], bank[3][:]).then_inc(ot_sb, 1)

            def mlp_slot(l, j, at):
                n = at(0)
                if n is None:
                    return
                par = j % 2
                act.wait_ge(h2T_pe, upto_p(l, n))
                ge(act, fc1_pe, upto_p(l, n - 2, 3))
                act.copy(h2A[:, par, :], bank[0][:, 0:2 * P]).then_inc(h2T_sb, 1)
                act.copy(h2B[:, par, :], bank[0][0:KS, 2 * P:3 * P].bitcast(BF16)).then_inc(h2T_sb, 1)
                ge(act, fc2_pe, upto_p(l, n - 2))
                for k in range(3):
                    act.wait_ge(fc1_pe, upto_p(l, n, 3) - 2 + k)
                    m = P if k < 2 else FL
                    cs = slice(2 * k, min(2 * k + 2, FC))
                    width = 4 * T if k < 2 else 2 * T
                    act.activation(gT[0:m, par, cs, :], bank[2 + 3 * par + k][0:m, 0:width],
                                   ACT.Gelu_apprx_tanh if l < 2 else ACT.Gelu).then_inc(gelu_rdy, 1)

            for l in range(L):
                attention(act, l, slot)
                if l + 1 < L:
                    act.wait_ge(gate_rdy, upto(l, B - 1))
                    load_mod(act, l + 1, 0)
                    if l:
                        load_ws(act, l + 1)
                mlp(act, l, mlp_slot)
                if l + 1 < L:
                    act.wait_ge(gate2_rdy, upto_p(l, PAIRS - 1))
                    load_mod(act, l + 1, 1)
                    if l + 2 < L:
                        load_w(act, l + 2)

        @block.vector
        def _(dve):
            dve.memset(s_b[:], 1.0).then_inc(set_ones, 1)
            dve.memset(zeros[:], 0.0)
            dve.memset(m3[:], 0.0)
            dve.memset(busy[:], 1.0)
            dve.memset(half_neg[:], -0.5).then_inc(set_ones, 1)
            dve.memset(stack[:], 0.0).then_inc(set_ones, 1)
            dve.memset(v[:], 0.0).then_inc(set_ones, 1)
            dve.memset(bs[:, :, 6 * CR:KS], 1.0)
            dve.memset(bs2[:, :, :, 6 * CR:KS], 1.0)
            dve.memset(o[:, C:C + 1], 1.0)
            dve.memset(gT[FL:FL + 1, :, FC - 1, :], 1.0).then_inc(set_ones, 1)
            dve.wait_ge(set_ones, 4)
            dve.memset(stack[:, :, H:2 * H, MROW:MROW + 3], -1.0)
            dve.memset(v[:, :, :, D:D + 1], 1.0).then_inc(set_ones, 1)
            dve.wait_ge(ld_const, 48)
            dve.tensor_copy(idb[:], idf[:]).then_inc(set_idb, 1)
            dve.wait_ge(ld_aff, 64)
            dve.tensor_scalar(qk_g[:, 0, :], qk_g[:, 0, :], float(D) ** 0.5, None, ALU.mult).then_inc(set_qk, 1)
            dve.tensor_scalar(aff_sb[:, 1, :, 0, :], aff_sb[:, 1, :, 0, :], float(C) ** 0.5, None,
                              ALU.mult).then_inc(set_qk, 1)
            dve.wait_ge(set_qk, 2)
            halves = m_sb[:].rearrange("b l (h k c) -> b l h k c", h=2, k=3)
            for l in range(L):
                dve.wait_ge(ada_gate, l + 1)
                if l:
                    dve.wait_ge(ada_mod, 2 * l)
                for half in range(2):
                    i = dve.tensor_scalar(sc1[:, half, :], bank[half][0:B, SCALE:SCALE + C], 1.0, None, ALU.add)
                i.then_inc(ada_sc, 1)
                dve.wait_ge(ada_sc, l + 1)
                dve.tensor_tensor(halves[:, l, :, 1, :], sc1[:], aff_sb[:, l, :, 0, :], ALU.mult).then_inc(ada_mod, 1)
                dve.tensor_tensor(shb[:], sc1[:], aff_sb[:, l, :, 1, :], ALU.mult).then_inc(ada_b1, 1)
                dve.wait_ge(ada_b1, l + 1)
                for half in range(2):
                    i = dve.tensor_tensor(halves[:, l, half, 0, :], bank[half][0:B, SHIFT:SHIFT + C],
                                          shb[:, half, :], ALU.add)
                i.then_inc(ada_mod, 1)

            def split_weights(l):
                dve.wait_ge(ld_ws, 16 * (l + 1))
                if l >= 2:
                    dve.wait_ge(fc1_pe, upto_p(l - 2, PAIRS - 1, 3))
                dve.tensor_copy(ws_part[:], ws_raw[:]).then_inc(ws_step, 1)
                dve.wait_ge(ws_step, 3 * l + 1)
                dve.scalar_tensor_tensor(out=ws_tmp[:], in0=ws_part[:], scalar=part_mask[:, 0:1], in1=ws_raw[:],
                                         op0=ALU.mult, op1=ALU.add).then_inc(ws_step, 1)
                dve.wait_ge(ws_step, 3 * l + 2)
                dve.tensor_copy(ws_part[:], ws_tmp[:]).then_inc(ws_step, 1)
                dve.wait_ge(ws_step, 3 * l + 3)
                dve.scalar_tensor_tensor(out=ws[:, l % 2, :], in0=ws_part[:], scalar=part_mask[:, 1:2],
                                         in1=ws_tmp[:], op0=ALU.mult, op1=ALU.add).then_inc(ws_rdy, 1)

            def statistics(l, j, k):
                var_s = (ln1_var, ln2_var)[k]
                for u in range(2):
                    i = dve.bn_stats(st6[:, k, u, :], x[:, bass.ds(2 * j + u, 1), :])
                dve.drain()
                for u in range(2):
                    i = dve.bn_aggr(mv[:, k, u, :], st6[:, k, u, :])
                i.then_inc(ln_mv[k], 1)
                dve.wait_ge(ln_mv[k], upto_p(l, j))
                if LN_EPS[l] is None:
                    dve.tensor_tensor(var[:, k, :], mv[:, k, :, 0], mv[:, k, :, 0], ALU.mult
                                      ).then_inc(ln_sq[k], 1)
                    dve.wait_ge(ln_sq[k], j + 1)
                    dve.tensor_tensor(var[:, k, :], var[:, k, :], mv[:, k, :, 1], ALU.add
                                      ).then_inc(ln_sum[k], 1)
                    dve.wait_ge(ln_sum[k], j + 1)
                    dve.tensor_scalar(var[:, k, :], var[:, k, :], float(C), TINY, ALU.mult, ALU.max
                                      ).then_inc(var_s, 1)
                else:
                    dve.tensor_scalar(var[:, k, :], mv[:, k, :, 1], LN_EPS[l], None, ALU.add).then_inc(var_s, 1)

            def normalise(l, j, k):
                rstd_s, done = ((ln1_rstd, xn1_rdy), (ln2_rstd, xn2_rdy))[k]
                dve.wait_ge(rstd_s, upto_p(l, j))
                for u in range(2):
                    dst, src = xn[:, bass.ds(2 * j + u, 1), :], x[:, bass.ds(2 * j + u, 1), :]
                    if LN_EPS[l] is None:
                        i = dve.tensor_scalar(dst, src, rstd[:, k, u:u + 1], None, ALU.mult)
                    else:
                        i = dve.tensor_scalar(dst, src, mv[:, k, u, 0:1], rstd[:, k, u:u + 1],
                                              ALU.subtract, ALU.mult)
                i.then_inc(done, 1)

            split_weights(0)
            dve.wait_ge(ld_x, 64)
            for j in range(2):
                statistics(0, j, 0)
                normalise(0, j, 0)
            with dve.Fori(2, PAIRS) as j:
                statistics(0, j, 0)
                normalise(0, j, 0)

            def rsqrt_heads(link):
                link(dve.tensor_scalar(qt1[:].bitcast(I32), qss[:].bitcast(I32), 1, None,
                                       ALU.arith_shift_right))
                link(dve.tensor_scalar(qrs[:].bitcast(I32), qt1[:].bitcast(I32), -1.0, MAGIC,
                                       ALU.mult, ALU.add))
                for _ in range(3):
                    link(dve.scalar_tensor_tensor(out=qt1[:], in0=qrs[:], scalar=-0.5, in1=qss[:],
                                                  op0=ALU.mult, op1=ALU.mult))
                    link(dve.tensor_tensor(qt2[:], qt1[:], qrs[:], ALU.mult))
                    link(dve.scalar_tensor_tensor(out=qrs[:], in0=qt2[:], scalar=1.5, in1=qrs[:],
                                                  op0=ALU.add, op1=ALU.mult))

            def heads(ap):
                return ap.rearrange("p (h d) -> p h d", d=D)

            def each_head(ap):
                return ap.unsqueeze(2).to_broadcast([P, 2 * H, D])

            def slot(l, s, at):
                lag = lags(l)
                def query_stack():
                    n = at("score")
                    if n is None:
                        return
                    par = (s - lag["score"]) % 2
                    dve.wait_ge(tq_pe, upto(l, n))
                    ge(dve, st_pe, upto(l, n - 2, 4))
                    dve.tensor_copy(qT[:, par], bank[1][:].bitcast(BF16)).then_inc(qT_sb, 1)

                def remainder():
                    n = at("split")
                    if n is None:
                        return
                    par = (s - lag["split"]) % 2
                    src = qy[:, par, :] if NORMED[l] else bank[1][:, 0:2 * C]
                    dve.wait_ge(x1_rdy, upto(l, n))
                    ge(dve, x3_rdy, upto(l, n - 2, 2))
                    dve.tensor_tensor(heads(rem[:, par, :]), heads(src), stack[:, par, :, 0:D], ALU.subtract
                                      ).then_inc(rem_rdy, 1)

                query_stack()
                n = at("out")
                if n is not None:
                    acc = bank[2][:].rearrange("p (h w) -> p h w", w=VW)
                    dve.wait_ge(ob_pe, upto(l, n))
                    ge(dve, oT_pe, upto(l, n - 1))
                    dve.reciprocal(rsum[:], acc[:, :, D]).then_inc(rsum_rdy, 1)
                    dve.wait_ge(rsum_rdy, upto(l, n))
                    dve.tensor_tensor(o[:, 0:C].rearrange("p (h d) -> p h d", d=D), acc[:, :, 0:D],
                                      rsum[:].unsqueeze(2).to_broadcast([P, H, D]), ALU.mult).then_inc(o_rdy, 1)
                remainder()

                def maxima(groups):
                    n = at("score")
                    if n is None:
                        return
                    par = (s - lag["score"]) % 2
                    for g in groups:
                        dve.wait_ge(s_pe, upto(l, n, 4) - 3 + g)
                        if g == 0:
                            ge(dve, m_rdy, upto(l, n - 2))
                        dve.tensor_reduce(mx[:, par, g * GRP:(g + 1) * GRP],
                                          bank[4 + g % 2][:].rearrange("p (h k) -> p h k", k=T), AX_X, ALU.max
                                          ).then_inc(mx_rdy, 1)

                maxima((0, 1))
                n = at("split")
                if n is not None:
                    par = (s - lag["split"]) % 2
                    slots = stack[:, par, :, 0:MROW].rearrange("p h (k d) -> p h k d", d=SW)
                    dve.wait_ge(x2_rdy, upto(l, n))
                    dve.tensor_copy(slots[:, 0:H, 1:5:3, :],
                                    slots[:, 0:H, 0:1, :].to_broadcast([P, H, 2, SW])).then_inc(slots_rdy, 1)
                    dve.tensor_copy(slots[:, 0:H, 2, :], slots[:, 0:H, 3, :]).then_inc(slots_rdy, 1)
                    dve.tensor_copy(slots[:, H:2 * H, 2:6:3, :],
                                    slots[:, H:2 * H, 0:1, :].to_broadcast([P, H, 2, SW])).then_inc(slots_rdy, 1)
                    dve.tensor_copy(slots[:, H:2 * H, 1, :], slots[:, H:2 * H, 3, :]).then_inc(slots_rdy, 1)
                maxima((2, 3))
                n = at("out")
                if n is not None:
                    dve.wait_ge(proj_pe, upto(l, n))
                    ge(dve, x_att, upto(l, n - 1))
                    dve.tensor_tensor(gated[:], bank[2][:, 0:C],
                                      mod1[:, bass.ds(n, 1), GATE:GATE + C], ALU.mult).then_inc(gate_rdy, 1)
                n = at("qkv")
                if NORMED[l] and n is not None:
                    qk = qkv[:, s % 2, 0:2 * C]
                    y = qy[:, s % 2, :]
                    dve.wait_ge(qkv_sb, upto(l, n))
                    ge(dve, x1_rdy, upto(l, n - 2))
                    ge(dve, rem_rdy, upto(l, n - 2))
                    steps = Q_STEPS[l]
                    done = [0]

                    def link(i):
                        done[0] += 1
                        i.then_inc(q_step[l], 1)
                        dve.wait_ge(q_step[l], steps * n + done[0])

                    if l == 3:
                        link(dve.tensor_reduce(qss[:], heads(qk), AX_X, ALU.add))
                        link(dve.scalar_tensor_tensor(out=heads(qk), in0=each_head(qss[:]), scalar=-1.0 / D,
                                                      in1=heads(qk), op0=ALU.mult, op1=ALU.add))
                    link(dve.tensor_tensor(qsq[:], qk, qk, ALU.mult))
                    link(dve.tensor_reduce(qss[:], heads(qsq[:]), AX_X, ALU.add))
                    if l == 3:
                        link(dve.tensor_scalar(qss[:], qss[:], 1.0 / D, QK_EPS, ALU.mult, ALU.add))
                    else:
                        link(dve.tensor_scalar(qss[:], qss[:], TINY, None, ALU.max))
                    rsqrt_heads(link)
                    assert done[0] == steps
                    dve.tensor_tensor(heads(y), heads(qk), each_head(qrs[:]), ALU.mult).then_inc(q_mid, 1)
                    dve.wait_ge(q_mid, upto_n(l, n))

            def mlp_slot(l, j, at):
                n2, n3 = at(-1), at(-2)
                if n2 is not None:
                    if j == -1:
                        dve.wait_ge(hs_rdy, upto(l, B - 1))
                    normalise(l, n2, 1)
                if n3 is not None:
                    dve.wait_ge(ld_x, 64)
                    dve.wait_ge(x_att, upto(l, 2 * n3 + 1))
                    statistics(l, n3, 1)
                n = at(1)
                if n is not None:
                    if j == 1:
                        dve.wait_ge(ld_mod2, 16 * (l + 1))
                    dve.wait_ge(fc2_pe, upto_p(l, n))
                    ge(dve, x_mlp, upto_p(l, n - 1))
                    dve.tensor_tensor(gated2[:], bank[1][:, 0:2 * C].rearrange("p (u c) -> p u c", u=2),
                                      mod2[:, bass.ds(2 * n, 2), GATE:GATE + C], ALU.mult).then_inc(gate2_rdy, 1)
                    dve.wait_ge(gate2_rdy, upto_p(l, n))
                    xx = x[:, bass.ds(2 * n, 2), :]
                    dve.tensor_tensor(xx, xx, gated2[:], ALU.add).then_inc(x_mlp, 1)
                    if l + 1 < L:
                        dve.wait_ge(ld_x, 64)
                        dve.wait_ge(x_mlp, upto_p(l, n))
                        statistics(l + 1, n, 0)
                if n is not None and l + 1 < L:
                    dve.wait_ge(hs2_rdy, upto_p(l, n))
                    normalise(l + 1, n, 0)
                if j == 1 and l + 1 < L:
                    split_weights(l + 1)

            for l in range(L):
                attention(dve, l, slot)
                mlp(dve, l, mlp_slot)

        @block.gpsimd
        def _(pool):
            def rstd_of(l, j, k):
                var_s, rstd_s, done = ((ln1_var, ln1_rstd, xn1_rdy), (ln2_var, ln2_rstd, xn2_rdy))[k]
                pool.wait_ge(var_s, upto_p(l, j))
                ge(pool, done, upto_p(l, j - 1))
                pool.tensor_tensor(rstd[:, k, :], var[:, k, :], half_neg[:], ALU.pow).then_inc(rstd_s, 1)

            def heads(ap):
                return ap.rearrange("p (h d) -> p h d", d=D)

            def split_last(dst, rest, src, m, step, steps, done):
                slots = dst[:, :, 0:6 * CR].rearrange("p m (k c) -> p m k c", c=CR)
                zero = zeros[:].unsqueeze(1).unsqueeze(1)
                for u in range(m):
                    i = pool.tensor_tensor(slots[:, u, 0:3], src[:, u:u + 1, :].to_broadcast([P, 3, CR]),
                                           zero[:, 0].to_broadcast([P, 3, CR]), ALU.add)
                i.then_inc(step, 1)
                pool.wait_ge(step, steps - 2)
                pool.tensor_tensor(rest, src, slots[:, :, 0], ALU.subtract).then_inc(step, 1)
                pool.wait_ge(step, steps - 1)
                for u in range(m):
                    i = pool.tensor_tensor(slots[:, u, 3:5], rest[:, u:u + 1, :].to_broadcast([P, 2, CR]),
                                           zero[:, 0].to_broadcast([P, 2, CR]), ALU.add)
                i.then_inc(step, 1)
                pool.wait_ge(step, steps)
                pool.tensor_tensor(slots[:, :, 5], rest, slots[:, :, 3], ALU.subtract).then_inc(done, 1)

            pool.wait_ge(set_ones, 5)
            for j in range(2):
                rstd_of(0, j, 0)
            with pool.Fori(2, PAIRS) as j:
                rstd_of(0, j, 0)

            def slot(l, s, at):
                lag = lags(l, 1)
                n = at("split")
                if n is not None:
                    par = (s - lag["split"]) % 2
                    slots = stack[:, par, :, 0:MROW].rearrange("p h (k d) -> p h k d", d=SW)
                    pool.wait_ge(x2_rdy, upto(l, n))
                    for who, k in ((slice(0, H), 5), (slice(H, 2 * H), 4)):
                        pool.tensor_tensor(slots[:, who, k, 0:D], heads(rem[:, par, :])[:, who, :],
                                           slots[:, who, 3, 0:D], ALU.subtract).then_inc(x3_rdy, 1)
                n = at("score")
                if n is not None:
                    par = (s - lag["score"]) % 2
                    parts = m3[:, par, 0:3 * H].rearrange("p (e j h a) -> p e j h a", e=2, j=3, h=2)
                    full = mx[:, par, :].rearrange("p (h e a) -> p e h a", h=2, e=2)
                    rest = mrem[:, par, :].rearrange("p (h e a) -> p e h a", h=2, e=2)
                    pool.wait_ge(mx_rdy, upto(l, n, 4))
                    ge(pool, mT_pe, upto(l, n - 2))
                    zero = zeros[:].rearrange("p (h e a) -> p e h a", h=2, e=2)
                    pool.tensor_tensor(parts[:, :, 0], full, zero, ALU.add).then_inc(m_step, 1)
                    pool.wait_ge(m_step, upto(l, n, 3) - 2)
                    pool.tensor_tensor(rest, full, parts[:, :, 0], ALU.subtract).then_inc(m_step, 1)
                    pool.wait_ge(m_step, upto(l, n, 3) - 1)
                    pool.tensor_tensor(parts[:, :, 1], rest, zero, ALU.add).then_inc(m_step, 1)
                    pool.wait_ge(m_step, upto(l, n, 3))
                    pool.tensor_tensor(parts[:, :, 2], rest, parts[:, :, 1], ALU.subtract
                                       ).then_inc(m_rdy, 1)
                n = at("qkv")
                if NORMED[l] and n is not None:
                    y = qy[:, (s - 1) % 2, :]
                    pool.wait_ge(q_mid, upto_n(l, n))
                    if l == 1:
                        pool.tensor_tensor(y, y, qk_g[:, 0, :], ALU.mult).then_inc(q_rdy, 1)
                    else:
                        pool.tensor_tensor(y, y, qk_g[:, 1, :], ALU.mult).then_inc(q_gain, 1)
                        pool.wait_ge(q_gain, n + 1)
                        pool.tensor_tensor(y, y, qk_b[:], ALU.add).then_inc(q_rdy, 1)
                n = at("out")
                if n is not None:
                    xx = x[:, bass.ds(n, 1), :]
                    pool.wait_ge(gate_rdy, upto(l, n))
                    pool.tensor_tensor(xx, xx, gated[:].unsqueeze(1), ALU.add).then_inc(x_att, 1)
                n = at("ahead")
                if n is not None:
                    par = (s + 1) % 2
                    if s == -1:
                        pool.wait_ge(ld_mod1, 16 * (l + 1))
                        pool.wait_ge(xn1_rdy, upto_p(l, PAIRS - 1))
                    ge(pool, hT_pe, upto(l, n - 2))
                    h = hs[:, par:par + 1, 0:C]
                    pool.tensor_tensor(h, xn[:, bass.ds(n, 1), :], mod1[:, bass.ds(n, 1), SCALE:SCALE + C],
                                       ALU.mult).then_inc(hs_mul, 1)
                    pool.wait_ge(hs_mul, upto(l, n))
                    pool.tensor_tensor(h, h, mod1[:, bass.ds(n, 1), SHIFT:SHIFT + C], ALU.add
                                       ).then_inc(hs_rdy, 1)
                    pool.wait_ge(hs_rdy, upto(l, n))
                    split_last(bs[:, par:par + 1, :], bs_rem[:, par:par + 1, :], hs[:, par:par + 1, P:C], 1,
                               bs_step, upto(l, n, 3), bs_rdy)

            def mlp_slot(l, j, at):
                n2, n3, n = at(-1), at(-2), at(1)
                if n2 is not None:
                    par = (j + 1) % 2
                    pool.wait_ge(xn2_rdy, upto_p(l, n2))
                    if j == -1:
                        pool.wait_ge(ld_mod2, 16 * (l + 1))
                    ge(pool, h2T_pe, upto_p(l, n2 - 2))
                    h = hs2[:, par, :, 0:C]
                    b = bass.ds(2 * n2, 2)
                    pool.tensor_tensor(h, xn[:, b, :], mod2[:, b, SCALE:SCALE + C], ALU.mult
                                       ).then_inc(hs2_mul, 1)
                    pool.wait_ge(hs2_mul, upto_p(l, n2))
                    pool.tensor_tensor(h, h, mod2[:, b, SHIFT:SHIFT + C], ALU.add).then_inc(hs2_rdy, 1)
                    pool.wait_ge(hs2_rdy, upto_p(l, n2))
                    split_last(bs2[:, par], bs2_rem[:, par], hs2[:, par, :, P:C], 2, bs2_step,
                               upto_p(l, n2, 3), bs2_rdy)
                if n3 is not None:
                    rstd_of(l, n3, 1)
                if n is not None and l + 1 < L:
                    rstd_of(l + 1, n, 0)

            for l in range(L):
                attention(pool, l, slot, behind=1)
                mlp(pool, l, mlp_slot)


def pack(i):
    import numpy as np

    def f(name):
        return np.asarray(i[name])

    one = np.ones((C,), np.float32)
    zero = np.zeros((C,), np.float32)
    wcat = np.zeros((L, C + 1, WCOLS + ACOLS), np.float32)
    w2cat = np.zeros((L, P, FC, C), np.float32)
    names = [
        ("L0_cond_W_qkv", "L0_cond_b_qkv", "L0_cond_W_proj", "L0_cond_b_proj", "L0_cond_W_fc1", "L0_cond_b_fc1",
         "L0_cond_W_ada", "L0_cond_b_ada", "L0_cond_W_fc2", "L0_cond_b_fc2"),
        ("L1_cond_qkv_w", "L1_cond_qkv_b", "L1_cond_proj_w", "L1_cond_proj_b", "L1_cond_fc1_w", "L1_cond_fc1_b",
         "L1_cond_ada_w", "L1_cond_ada_b", "L1_cond_fc2_w", "L1_cond_fc2_b"),
        (None, None, "L2_cond_wo", "L2_cond_wo_b", "L2_cond_fc1_w", "L2_cond_fc1_b",
         "L2_cond_ada_w", "L2_cond_ada_b", "L2_cond_fc2_w", "L2_cond_fc2_b"),
        ("L3_cond_w_qkv", "L3_cond_b_qkv", "L3_cond_w_proj", "L3_cond_b_proj", "L3_cond_w1", "L3_cond_b1",
         "L3_cond_w_ada", "L3_cond_b_ada", "L3_cond_w2", "L3_cond_b2"),
    ]
    for l, row in enumerate(names):
        for k, (at, width) in enumerate(((QKV, 3 * C), (PROJ, C), (FC1, FF), (ADA, ACOLS))):
            if row[2 * k] is None:
                for m, name in enumerate(("L2_cond_wq", "L2_cond_wk", "L2_cond_wv")):
                    wcat[l, 0:C, at + m * C:at + (m + 1) * C] = f(name)
                continue
            w = f(row[2 * k])
            w = w.T if l == 1 else w
            wcat[l, 0:C, at:at + width] = w.reshape(H, D, C)[HEAD_ORDER].reshape(C, C) if at == PROJ else w
            wcat[l, C, at:at + width] = f(row[2 * k + 1])
        w = f(row[8])
        w = w.T if l == 1 else w
        for c in range(FC):
            m = P if c < FC - 1 else FL
            w2cat[l, 0:m, c, :] = w[c * P:c * P + m]
        w2cat[l, FL, FC - 1, :] = f(row[9])
    wlast = np.concatenate([np.tile(wcat[:, P:C, 0:SCOLS], (1, 6, 1)), np.tile(wcat[:, C:C + 1, 0:SCOLS], (1, 3, 1))],
                           axis=1)
    part = np.concatenate([np.repeat([1, 2, 3, 1, 2, 1], CR), [1, 2, 3]])
    masks = -np.stack([part >= 2, part >= 3], axis=1).astype(np.float32)
    aff = np.stack([
        np.stack([np.stack([one, zero])] * 2),
        np.stack([np.stack([np.broadcast_to(f("L1_cond_g1"), (C,)), zero]),
                  np.stack([np.broadcast_to(f("L1_cond_g2"), (C,)), zero])]),
        np.stack([np.stack([f("L2_cond_ln1_w"), f("L2_cond_ln1_b")]),
                  np.stack([f("L2_cond_ln2_w"), f("L2_cond_ln2_b")])]),
        np.stack([np.stack([one, zero])] * 2),
    ])
    qkaff = np.zeros((2, 2, 2 * C), np.float32)
    qkaff[0, 0] = np.concatenate([np.broadcast_to(f("L1_cond_qg"), (C,)), np.broadcast_to(f("L1_cond_kg"), (C,))])
    qkaff[1, 0] = np.concatenate([np.tile(f("L3_cond_qn_g"), H), np.tile(f("L3_cond_kn_g"), H)])
    qkaff[1, 1] = np.concatenate([np.tile(f("L3_cond_qn_b"), H), np.tile(f("L3_cond_kn_b"), H)])
    return {
        "x": np.ascontiguousarray(f("x")),
        "cT": np.ascontiguousarray(f("cond_1152").T),
        "wcat": wcat,
        "wlast": np.ascontiguousarray(wlast),
        "masks": masks,
        "w2cat": w2cat,
        "aff": np.ascontiguousarray(aff),
        "qkaff": qkaff,
        "ident": np.eye(P, dtype=np.float32),
    }


def kernel(**inputs):
    import concourse.bacc as bacc
    import numpy as np
    from concourse.bass_utils import run_bass_kernel_spmd

    nc = bacc.Bacc("TRN2", target_bir_lowering=False, num_devices=1)
    arrays, args = {}, []
    for name, a in pack(inputs).items():
        arrays[f"in_{name}"] = a
        args.append(nc.dram_tensor(f"in_{name}", a.shape, mybir.dt.from_np(a.dtype), kind="ExternalInput").ap())
    args.append(nc.dram_tensor("out_x", (B, T, C), mybir.dt.from_np(np.dtype("float32")),
                               kind="ExternalOutput").ap())
    build(nc, *args)
    return run_bass_kernel_spmd(nc, [arrays], core_ids=[0]).results[0]["out_x"]
```

```python
from contextlib import ExitStack

import concourse.bass as bass
from concourse import mybir

F32 = mybir.dt.float32
BF16 = mybir.dt.bfloat16
I32 = mybir.dt.int32
ALU = mybir.AluOpType
ACT = mybir.ActivationFunctionType
AX_X = mybir.AxisListType.X

L = 4
B, T, C = 16, 128, 144
H = 16
D = C // H
P = 128
CR = C - P
KB = CR + 1
KS = 6 * CR + 3
FF = 4 * C
FC = (FF + P - 1) // P
FL = FF - (FC - 1) * P
PAIRS = B // 2
QKV, FC1, PROJ, ADA = 0, 3 * C, 3 * C + FF, 4 * C + FF
SCOLS = PROJ
WCOLS = ADA
ACOLS = 6 * C
SHIFT, SCALE, GATE = 0, C, 2 * C
SW = D + 1
NSLOT = 6
MROW = NSLOT * SW
HW = 64
GRP = 4
NG = H // GRP
VW = 32
HEAD_ORDER = [8 * (g // 2) + 2 * a + g % 2 for g in range(NG) for a in range(GRP)]
LN_EPS = (1e-6, None, 1e-5, 1e-6)
QK_EPS = 1e-5
TINY = 1e-24
MAGIC = float(0x5F3759DF)
FILL = ((1, 0), (1, 0), 0), ((2, 2), (2, 0), 0)
START_FILL = 12, 0
FIRST_FILL, ADA_FILL = 12, 2
NORMED = (False, True, False, True)
Q_STEPS = {1: 14, 3: 16}
Q_STEPS_BEFORE = {1: 5, 3: 7}


def build(nc, x_in, cT, wcat, wlast, masks, w2cat, aff, qkaff, ident, out):
    scratch = nc.dram_tensor("mod_scratch", (B, L, ACOLS), F32, kind="Internal").ap()
    ctx = ExitStack()
    with ctx:
        def sb(name, shape, dt=F32):
            return ctx.enter_context(nc.sbuf_tensor(name, shape, dt))

        def sem(name):
            return ctx.enter_context(nc.semaphore(name))

        x = sb("x", [P, B, C])
        xn = sb("xn", [P, B, C])
        mod1 = sb("mod1", [P, B, 3 * C])
        mod2 = sb("mod2", [P, B, 3 * C])
        wa = sb("wa", [P, 2, WCOLS])
        wb = sb("wb", [KB, 2, C])
        ws_raw = sb("ws_raw", [KS, SCOLS])
        ws_tmp = sb("ws_tmp", [KS, SCOLS])
        ws_part = sb("ws_part", [KS, SCOLS], BF16)
        ws = sb("ws", [KS, 2, SCOLS], BF16)
        part_mask = sb("part_mask", [KS, 2])
        bs = sb("bs", [P, 2, KS], BF16)
        bs_rem = sb("bs_rem", [P, 2, CR])
        bs2 = sb("bs2", [P, 2, 2, KS], BF16)
        bs2_rem = sb("bs2_rem", [P, 2, 2, CR])
        w2 = sb("w2", [P, 2, FC, C])
        idf = sb("idf", [P, P])
        idb = sb("idb", [P, P], BF16)
        busy = sb("busy", [P, 512], BF16)
        half_neg = sb("half_neg", [P, B // 2])
        qk_g = sb("qk_g", [P, 2, 2 * C])
        qk_b = sb("qk_b", [P, 2 * C])
        hs = sb("hs", [P, 2, C])
        hs2 = sb("hs2", [P, 2, 2, C])
        hA = sb("hA", [P, P])
        hB = sb("hB", [KS, P], BF16)
        stack = sb("stack", [P, 2, 2 * H, HW], BF16)
        rem = sb("rem", [P, 2, 2 * C])
        qT = sb("qT", [P, 2, H // 2, T], BF16)
        kT = sb("kT", [P, 2, H // 2, T], BF16)
        mx = sb("mx", [P, 2, H])
        mrem = sb("mrem", [P, 2, H])
        zeros = sb("zeros", [P, H])
        m3 = sb("m3", [P, 2, P], BF16)
        mT = sb("mT", [48, 2, T], BF16)
        e = sb("e", [P, H, T])
        v = sb("v", [P, 2, H, VW])
        oT = sb("oT", [P, NG, T])
        rsum = sb("rsum", [P, H])
        o = sb("o", [P, C + 1])
        otA = sb("otA", [P, P])
        otB = sb("otB", [KB, P])
        gated = sb("gated", [P, C])
        qkv = sb("qkv", [P, 2, 3 * C])
        qsq = sb("qsq", [P, 2 * C])
        qss = sb("qss", [P, 2 * H])
        qrs = sb("qrs", [P, 2 * H])
        qt1 = sb("qt1", [P, 2 * H])
        qt2 = sb("qt2", [P, 2 * H])
        qy = sb("qy", [P, 2, 2 * C])
        st6 = sb("st6", [P, 2, 2, 6])
        mv = sb("mv", [P, 2, 2, 2])
        var = sb("var", [P, 2, 2])
        rstd = sb("rstd", [P, 2, 2])
        h2A = sb("h2A", [P, 2, 2 * T])
        h2B = sb("h2B", [KS, 2, 2 * T], BF16)
        gT = sb("gT", [P, 2, FC, 2 * T])
        gated2 = sb("gated2", [P, 2, C])
        st0 = sb("st0", [P, B, 6])
        mv0 = sb("mv0", [P, B, 2])
        var0 = sb("var0", [P, B])
        rstd0 = sb("rstd0", [P, B])
        ada_a = e[:].rearrange("p h t -> p (h t)")[:, 0:2 * ACOLS].rearrange("p (u c) -> p u c", u=2)
        ada_b = gT[:].rearrange("p u c t -> p (u c t)")[0:KB, 0:2 * ACOLS].rearrange("p (u c) -> p u c", u=2)
        c_a = sb("c_a", [P, B])
        c_b = sb("c_b", [CR, B])
        s_a = sb("s_a", [P, B])
        s_b = sb("s_b", [KB, B])
        aff_sb = sb("aff_sb", [B, L, 2, 2, C])
        m_sb = sb("m_sb", [B, L, ACOLS])
        sc1 = sb("sc1", [B, 2, C])
        shb = sb("shb", [B, 2, C])

        bank = [ctx.enter_context(nc.psum_tensor(f"bank{i}", [P, 512], F32)) for i in range(8)]

        ld_c, ld_ident, ld_mod1, ld_mod1_rest, ld_mod2, ld_aff, ld_qk = (
            sem(n) for n in ("ld_c", "ld_ident", "ld_mod1", "ld_mod1_rest", "ld_mod2", "ld_aff", "ld_qk"))
        ld_x, ld_x_rest = sem("ld_x"), sem("ld_x_rest")
        ld_ada = [sem(f"ld_ada{i}") for i in range(2)]
        ld_w = [sem(f"ld_w{i}") for i in range(2)]
        set_ones, set_zero, set_stack, first_stats, set_idb, silu_done, ada_mm, ada_sc, ada_b1, ada_mod, ada_gate, mod_out, set_qk = (
            sem(n) for n in ("set_ones", "set_zero", "set_stack", "first_stats", "set_idb", "silu_done", "ada_mm", "ada_sc", "ada_b1", "ada_mod",
                             "ada_gate", "mod_out", "set_qk"))
        hT_pe, qkv_pe, tk_pe, tq_pe, s_pe, mT_pe, st_pe, av_pe, ob_pe, oT_pe, proj_pe = (
            sem(n) for n in ("hT_pe", "qkv_pe", "tk_pe", "tq_pe", "s_pe", "mT_pe", "st_pe", "av_pe",
                             "ob_pe", "oT_pe", "proj_pe"))
        hs_mul, hs_rdy, hT_sb, x1_rdy, x2_rdy, rem_rdy, x3_rdy, slots_rdy, v_sb, kT_sb, qT_sb = (
            sem(n) for n in ("hs_mul", "hs_rdy", "hT_sb", "x1_rdy", "x2_rdy", "rem_rdy", "x3_rdy",
                             "slots_rdy", "v_sb", "kT_sb", "qT_sb"))
        mx_rdy, m_step, m_rdy, mT_sb, m_rows, e_rdy, ot_sb, rsum_rdy, o_rdy, oT_sb, gate_rdy, x_att = (
            sem(n) for n in ("mx_rdy", "m_step", "m_rdy", "mT_sb", "m_rows", "e_rdy", "ot_sb", "rsum_rdy",
                             "o_rdy", "oT_sb", "gate_rdy", "x_att"))
        qkv_sb, q_mid, q_gain, q_rdy = (sem(n) for n in ("qkv_sb", "q_mid", "q_gain", "q_rdy"))
        ld_ws, ws_step, ws_rdy, bs_step, bs_rdy, bs2_step, bs2_rdy = (
            sem(n) for n in ("ld_ws", "ws_step", "ws_rdy", "bs_step", "bs_rdy", "bs2_step", "bs2_rdy"))
        q_step = {l: sem(f"q_step{l}") for l in range(L) if NORMED[l]}
        h2T_pe, fc1_pe, fc2_pe, h2T_sb, gelu_rdy, gate2_rdy, x_mlp, hs2_mul, hs2_rdy = (
            sem(n) for n in ("h2T_pe", "fc1_pe", "fc2_pe", "h2T_sb", "gelu_rdy", "gate2_rdy", "x_mlp",
                             "hs2_mul", "hs2_rdy"))
        ln_mv, ln_sq, ln_sum = ([sem(f"{n}{k + 1}") for k in range(2)]
                                       for n in ("ln_mv", "ln_sq", "ln_sum"))
        ln1_var, ln1_rstd, xn1_rdy, ln2_var, ln2_rstd, xn2_rdy, out_done = (
            sem(n) for n in ("ln1_var", "ln1_rstd", "xn1_rdy", "ln2_var", "ln2_rstd", "xn2_rdy", "out_done"))

        def ge(eng, s, value):
            if isinstance(value, int) and value <= 0:
                return
            assert isinstance(value, int) or value.min_val > 0
            eng.wait_ge(s, value)

        def upto(l, b, per=1):
            return (b + (16 * l + 1)) * per

        def upto_p(l, j, per=1):
            return (j + (PAIRS * l + 1)) * per

        def upto_n(l, b, per=1):
            return (b + (16 * (l // 2) + 1)) * per

        def lags(l, behind=0):
            d = int(NORMED[l])
            return dict(ahead=-behind, qkv=behind, norm=1 + behind, split=d + behind, score=1 + d + behind, prob=2 + d + behind,
                        out=3 + d + behind)

        def attention_slot(l, s, slot, behind):
            lag = lags(l, behind)
            slot(l, s, lambda k: s - lag[k] if 0 <= s - lag[k] < B else None)

        def mlp_slot_of(l, j, slot):
            slot(l, j, lambda k: j - k if 0 <= j - k < PAIRS else None)

        def first_of_loop(l, behind=0):
            out = lags(l, behind)["out"]
            return out + 1 + (out + 1) % 2 + 2 * (l == 0)

        def attention(eng, l, slot, mlp_slot, behind=0, prepares=False):
            lag = lags(l, behind)
            first = first_of_loop(l, behind)
            start = 3 if l else min(0, lag["ahead"])
            end = B - 2 * behind
            for s in range(start, first):
                attention_slot(l, s, slot, behind)
            with eng.Fori(first // 2, end // 2) as i:
                for u in range(2):
                    slot(l, first + u, lambda k, u=u: 2 * i + (u - lag[k]))
            for s in range(end, B - 1 + lag["out"]):
                attention_slot(l, s, slot, behind)
                if prepares and s - (B + lag["out"] - 1) == -2:
                    mlp_slot_of(l, -2, mlp_slot)
                    mlp_slot_of(l, -1, mlp_slot)
            mlp_slot_of(l, 0, mlp_slot)
            attention_slot(l, B - 1 + lag["out"], slot, behind)

        def mlp(eng, l, mlp_slot, slot, behind=0):
            def next_attention(s):
                if l + 1 < L:
                    attention_slot(l + 1, s, slot, behind)
            mlp_slot_of(l, 1, mlp_slot)
            with eng.Fori(1, PAIRS // 2 - 1) as i:
                for u in range(2):
                    mlp_slot(l, 2 + u, lambda k, u=u: 2 * i + (u - k))
            if behind:
                next_attention(-1)
            mlp_slot_of(l, PAIRS - 2, mlp_slot)
            next_attention(0)
            mlp_slot_of(l, PAIRS - 1, mlp_slot)
            next_attention(1)
            if behind:
                next_attention(2)
            mlp_slot_of(l, PAIRS, mlp_slot)
            if not behind:
                next_attention(2)
            mlp_slot_of(l, PAIRS + 1, mlp_slot)

        def fc2_bank(j):
            return 1 if j < PAIRS else 2

        def head(g, a):
            return HEAD_ORDER[GRP * g + a]

        def last(l, s, lag):
            return 0 <= s - 1 - lag < B

        def load_mod(eng, l, half, of=slice(0, B)):
            done = ld_mod1_rest if of.start and half == 0 else (ld_mod1, ld_mod2)[half]
            eng.dma_start((mod1, mod2)[half][:, of],
                          scratch[of, l, half * 3 * C:(half + 1) * 3 * C].partition_broadcast(P)
                          ).then_inc(done, 16)

        def load_w(eng, l):
            eng.dma_start(wa[:, l % 2, :], wcat[l, 0:P, 0:WCOLS]).then_inc(ld_w[l % 2], 16)
            eng.dma_start(wb[:, l % 2, :], wcat[l, P:P + KB, PROJ:PROJ + C]).then_inc(ld_w[l % 2], 16)
            eng.dma_start(w2[:, l % 2], w2cat[l]).then_inc(ld_w[l % 2], 16)

        def load_ada(eng, l):
            eng.dma_start(ada_a[:, l % 2, :], wcat[l, 0:P, ADA:]).then_inc(ld_ada[l % 2], 16)
            eng.dma_start(ada_b[:, l % 2, :], wcat[l, P:P + KB, ADA:]).then_inc(ld_ada[l % 2], 16)

        def load_ws(eng, l):
            ge(eng, ws_rdy, l)
            eng.dma_start(ws_raw[:], wlast[l]).then_inc(ld_ws, 16)

        block = ctx.enter_context(nc.Block())

        @block.sync
        def _(sp):
            sp.dma_start(c_a[:], cT[0:P, :]).then_inc(ld_c, 16)
            sp.dma_start(c_b[:], cT[P:C, :]).then_inc(ld_c, 16)
            load_ada(sp, 0)
            sp.dma_start(aff_sb[:], aff.partition_broadcast(B)).then_inc(ld_aff, 16)
            sp.dma_start(part_mask[:], masks).then_inc(ld_aff, 16)
            load_ws(sp, 0)
            load_ada(sp, 1)
            load_w(sp, 0)
            sp.dma_start(qk_g[:], qkaff[:, 0, :].partition_broadcast(P)).then_inc(ld_qk, 16)
            sp.dma_start(qk_b[:], qkaff[1, 1, :].partition_broadcast(P)).then_inc(ld_qk, 16)
            for l in range(L):
                sp.wait_ge(ada_mod, 2 * (l + 1))
                sp.wait_ge(ada_gate, l + 1)
                sp.dma_start(scratch[:, l], m_sb[:, l]).then_inc(mod_out, 16)
                sp.wait_ge(mod_out, 16 * (l + 1))
                if l == 0:
                    load_mod(sp, 0, 0, slice(0, B // 4))
                    load_mod(sp, 0, 0, slice(B // 4, B))
                    load_mod(sp, 0, 1)
            load_w(sp, 1)
            load_ws(sp, 1)

            def slot(l, s, at):
                n = at("prob")
                if n is None:
                    return
                par = (s - lags(l)["prob"]) % 2
                sp.wait_ge(mT_sb, upto(l, n))
                for half in range(2):
                    sp.dma_start(qT[HW * half + MROW:HW * half + MROW + 3, par],
                                 mT[24 * half:24 * half + 24, par, :]).then_inc(m_rows, 16)

            for l in range(L):
                if l:
                    for s in range(3):
                        attention_slot(l, s, slot, 0)
                attention(sp, l, slot, lambda l, j, at: None)
            for q in range(PAIRS):
                sp.wait_ge(x_mlp, upto_p(L - 1, q))
                sp.dma_start(out[2 * q:2 * q + 2].rearrange("b t c -> t b c"), x[:, 2 * q:2 * q + 2, :]
                             ).then_inc(out_done, 16)
            sp.wait_ge(out_done, 16 * PAIRS)

        @block.tensor
        def _(pe):
            def keep_clock(b, count):
                for _ in range(count):
                    pe.matmul(bank[b][:], busy[:, 0:P], busy[:], start=True, stop=True)

            pe.wait_ge(set_ones, 1)
            keep_clock(7, FIRST_FILL)
            pe.wait_ge(silu_done, 2)
            for l in range(L):
                pe.wait_ge(ld_ada[l % 2], 32 * (l // 2 + 1))
                if l >= 2:
                    pe.wait_ge(ada_mod, 2 * (l - 1))
                    pe.wait_ge(ada_gate, l - 1)
                for half in range(2):
                    cols = slice(half * 3 * C, (half + 1) * 3 * C)
                    dst = bank[2 * (l % 2) + half][0:B, 0:3 * C]
                    pe.matmul(dst, s_a[:], ada_a[:, l % 2, cols], start=True, stop=False)
                    mm = pe.matmul(dst, s_b[:], ada_b[:, l % 2, cols], start=False, stop=True)
                mm.then_inc(ada_mm, 1)
                keep_clock(7, ADA_FILL)
            pe.wait_ge(ada_mod, 2 * L)
            pe.wait_ge(ada_gate, L)
            pe.wait_ge(set_idb, 1)

            bank1b = bank[1][:].bitcast(BF16)
            bank2b = bank[2][:].bitcast(BF16)
            bank3b = bank[3][:].bitcast(BF16)
            bank0b = bank[0][:].bitcast(BF16)

            def slot(l, s, at):
                lag = lags(l)
                w = l % 2
                ns, ps = at("score"), (s - lag["score"]) % 2
                np_, pp = at("prob"), (s - lag["prob"]) % 2
                no, nq = at("out"), at("qkv")

                def qkv_read(n):
                    pe.wait_ge(qkv_sb, upto(l, n))
                    if not NORMED[l]:
                        pe.wait_ge(rem_rdy, upto(l, n))

                def key_scores(n, par, half):
                    ge(pe, e_rdy, upto(l, n, 4) - 4 + 2 * half)
                    keep_clock(6, FILL[NORMED[l]][0][half])
                    if half == 0:
                        pe.wait_ge(m_rows, upto(l, n, 32))
                    for a in range(GRP):
                        for odd in range(2):
                            r = slice(HW * odd, HW * odd + MROW + 3)
                            mm = pe.matmul(bank[6 + odd][:, a * T:(a + 1) * T], kT[r, par, GRP * half + a, :],
                                           qT[r, par, GRP * half + a, :], start=True, stop=True)
                            if a == GRP - 1:
                                mm.then_inc(st_pe, 1)

                def query_scores(n, par, half):
                    ge(pe, mx_rdy, upto(l, n, 4) - 4 + 2 * half)
                    keep_clock(4, FILL[NORMED[l]][1][half])
                    if half == 0:
                        pe.wait_ge(kT_sb, upto(l, n))
                        pe.wait_ge(qT_sb, upto(l, n))
                    for a in range(GRP):
                        for odd in range(2):
                            r = slice(HW * odd, HW * odd + MROW)
                            mm = pe.matmul(bank[4 + odd][:, a * T:(a + 1) * T], qT[r, par, GRP * half + a, :],
                                           kT[r, par, GRP * half + a, :], start=True, stop=True)
                            if a == GRP - 1:
                                mm.then_inc(s_pe, 1)

                def values(n, par, g):
                    if g == 0:
                        pe.wait_ge(v_sb, upto(l, n))
                        if at("score") is not None:
                            pe.wait_ge(kT_sb, upto(l, at("score")))
                        else:
                            pe.wait_ge(ot_sb, upto(l, n - 1))
                        keep_clock(3, FILL[NORMED[l]][2])
                    pe.wait_ge(e_rdy, upto(l, n, 4) - 3 + g)
                    for a in range(GRP):
                        h = head(g, a)
                        mm = pe.matmul(bank[3][VW * a:VW * (a + 1), g * T:(g + 1) * T], v[:, par, h, :],
                                       e[:, g * GRP + a, :], start=True, stop=True, tile_position=(0, VW * a))
                    mm.then_inc(av_pe, 1)

                if s == 1 and l:
                    pe.wait_ge(gate2_rdy, upto_p(l - 1, PAIRS - 2))
                    pe.wait_ge(gelu_rdy, upto_p(l - 1, PAIRS - 1, 3))
                if s == 1:
                    keep_clock(7, START_FILL[l > 0])
                if ns is not None:
                    pe.wait_ge(slots_rdy, upto(l, ns, 4))
                    pe.wait_ge(x3_rdy, upto(l, ns, 2))
                    if last(l, s, 0):
                        qkv_read(ns + (lag["score"] - 1))
                    else:
                        pe.wait_ge(qT_sb, upto(l, ns - 1))
                    for i in range(H // 2):
                        tr = pe.transpose(bank1b[:, i * P:(i + 1) * P], stack[:, ps, 2 * i:2 * i + 2, :], idb[:])
                    tr.then_inc(tq_pe, 1)
                if nq is not None:
                    pe.wait_ge(bs_rdy, upto(l, nq))
                    if last(l, s, lag["out"]):
                        pe.wait_ge(oT_sb, upto(l, no - 1))
                    elif last(l, s, 0):
                        pe.wait_ge(hT_sb, upto(l, nq - 1))
                    par = s % 2
                    pe.transpose(bank[0][:, 0:P], hs[:, par, 0:P], idf[:])
                    pe.transpose(bank0b[0:KS, 2 * P:3 * P], bs[:, par, :], idb[:]).then_inc(hT_pe, 1)
                if no is not None:
                    values(no, (s - lag["out"]) % 2, 2)
                    values(no, (s - lag["out"]) % 2, 3)
                if np_ is not None:
                    if s == lag["prob"] and l:
                        pe.wait_ge(gate2_rdy, upto_p(l - 1, PAIRS - 1))
                    if last(l, s, lag["out"]):
                        pe.wait_ge(gate_rdy, upto(l, no - 1))
                    elif last(l, s, lag["prob"]):
                        pe.wait_ge(mT_sb, upto(l, np_ - 1))
                    pe.wait_ge(m_rdy, upto(l, np_))
                    pe.transpose(bank2b[:, 0:P], m3[:, pp, :], idb[:]).then_inc(mT_pe, 1)
                if ns is not None:
                    if last(l, s, lag["prob"]):
                        pe.wait_ge(ot_sb, upto(l, ns + (lag["score"] - lag["prob"] - 1)))
                    elif last(l, s, lag["score"]):
                        pe.wait_ge(kT_sb, upto(l, ns - 1))
                    for i in range(H // 2):
                        tr = pe.transpose(bank3b[:, i * P:(i + 1) * P],
                                          stack[:, ps, H + 2 * i:H + 2 * i + 2, :], idb[:])
                    tr.then_inc(tk_pe, 1)
                if no is not None:
                    pe.wait_ge(ot_sb, upto(l, no))
                    if np_ is not None:
                        pe.wait_ge(mT_sb, upto(l, np_))
                    else:
                        pe.wait_ge(gate_rdy, upto(l, no - 1))
                    for g in range(NG):
                        tr = pe.transpose(bank[2][:, g * P:(g + 1) * P], oT[:, g, :], idf[:])
                    tr.then_inc(ob_pe, 1)
                if nq is not None:
                    if s == 0:
                        pe.wait_ge(ld_w[w], 48 * (l // 2 + 1))
                        pe.wait_ge(ws_rdy, l + 1)
                        if l:
                            pe.wait_ge(gate2_rdy, upto_p(l - 1, PAIRS - 3))
                    pe.wait_ge(hT_sb, upto(l, nq))
                    if ns is not None:
                        pe.wait_ge(qT_sb, upto(l, ns))
                    elif last(l, s, 0):
                        qkv_read(nq - 1)
                    pe.matmul(bank[1][:, 0:3 * C], hA[:], wa[:, w, QKV:QKV + 3 * C], start=True, stop=False)
                    pe.matmul(bank[1][:, 0:3 * C], hB[:], ws[:, w, QKV:QKV + 3 * C], start=False, stop=True
                              ).then_inc(qkv_pe, 1)

                if ns is not None:
                    query_scores(ns, ps, 0)
                if no is not None:
                    pe.wait_ge(o_rdy, upto(l, no))
                    if nq is not None:
                        pe.wait_ge(hT_sb, upto(l, nq))
                    elif no < B - 1:
                        pe.wait_ge(oT_sb, upto(l, no - 1))
                    else:
                        pe.wait_ge(h2T_sb, upto_p(l, 0, 2))
                    pe.transpose(bank[0][:, 0:P], o[:, 0:P], idf[:])
                    pe.transpose(bank[0][0:KB, P:2 * P], o[:, P:C + 1], idf[:]).then_inc(oT_pe, 1)
                if np_ is not None:
                    key_scores(np_, pp, 0)
                if ns is not None:
                    query_scores(ns, ps, 1)
                if no is not None:
                    pe.wait_ge(oT_sb, upto(l, no))
                    pe.matmul(bank[2][:, 0:C], otA[:], wa[:, w, PROJ:PROJ + C], start=True, stop=False)
                    pe.matmul(bank[2][:, 0:C], otB[:], wb[:, w, :], start=False, stop=True
                              ).then_inc(proj_pe, 1)
                if np_ is not None:
                    key_scores(np_, pp, 1)
                    values(np_, pp, 0)
                    values(np_, pp, 1)

            def mlp_slot(l, j, at):
                w = l % 2
                n = at(0)
                if n is not None:
                    par = j % 2
                    pe.wait_ge(bs2_rdy, upto_p(l, n))
                    if j == 0:
                        pe.wait_ge(oT_sb, upto(l, B - 2))
                    else:
                        pe.wait_ge(h2T_sb, upto_p(l, n - 1, 2))
                    for u in range(2):
                        pe.transpose(bank[0][:, u * P:(u + 1) * P], hs2[:, par, u, 0:P], idf[:])
                    for u in range(2):
                        tr = pe.transpose(bank0b[0:KS, (4 + u) * P:(5 + u) * P], bs2[:, par, u, :], idb[:])
                    tr.then_inc(h2T_pe, 1)
                n = at(1)
                if n is not None:
                    par = (j - 1) % 2
                    b = fc2_bank(j)
                    if j == PAIRS - 1 and l + 1 < L:
                        pe.wait_ge(qkv_sb, upto(l + 1, 0))
                        if not NORMED[l + 1]:
                            pe.wait_ge(rem_rdy, upto(l + 1, 0))
                    elif j > 1 and j < PAIRS:
                        pe.wait_ge(gate2_rdy, upto_p(l, n - 1))
                    pe.wait_ge(gelu_rdy, upto_p(l, n, 3))
                    for u in range(2):
                        for c in range(FC):
                            k = P if c < FC - 1 else FL + 1
                            mm = pe.matmul(bank[b][:, u * C:(u + 1) * C], gT[0:k, par, c, u * T:(u + 1) * T],
                                           w2[0:k, w, c, :], start=(c == 0), stop=(c == FC - 1))
                    mm.then_inc(fc2_pe, 1)
                n = at(0)
                if n is not None:
                    par = j % 2
                    pe.wait_ge(h2T_sb, upto_p(l, n, 2))
                    if j == 0:
                        pe.wait_ge(mx_rdy, upto(l, B - 1, 4))
                        pe.wait_ge(e_rdy, upto(l, B - 1, 4))
                    elif j == 1:
                        pe.wait_ge(gate_rdy, upto(l, B - 1))
                        pe.wait_ge(ot_sb, upto(l, B - 1))
                    for c in range(FC):
                        m = P if c < FC - 1 else FL
                        dst = bank[5 - 3 * par + c // 2][0:m, (c % 2) * 2 * T:(c % 2 + 1) * 2 * T]
                        cols = slice(FC1 + c * P, FC1 + c * P + m)
                        pe.matmul(dst, wa[:, w, cols], h2A[:, par, :], start=True, stop=False)
                        cols = slice(FC1 + c * P, FC1 + c * P + m)
                        mm = pe.matmul(dst, ws[:, w, cols], h2B[:, par, :], start=False, stop=True)
                        if c % 2 or c == FC - 1:
                            mm.then_inc(fc1_pe, 1)

            for l in range(L):
                attention(pe, l, slot, mlp_slot)
                mlp(pe, l, mlp_slot, slot)

        @block.scalar
        def _(act):
            for q in range(4):
                act.dma_start(x[:, 4 * q:4 * q + 4, :], x_in[4 * q:4 * q + 4].rearrange("b t c -> t b c")
                              ).then_inc(ld_x if q < 2 else ld_x_rest, 16)
            act.dma_start(idf[:], ident).then_inc(ld_ident, 16)
            act.wait_ge(ld_c, 32)
            act.wait_ge(set_ones, 1)
            act.activation(s_a[:], c_a[:], ACT.Silu).then_inc(silu_done, 1)
            act.activation(s_b[0:CR, :], c_b[:], ACT.Silu).then_inc(silu_done, 1)
            gates = m_sb[:].rearrange("b l (h k c) -> b l h k c", h=2, k=3)
            for l in range(L):
                act.wait_ge(ada_mm, l + 1)
                for half in range(2):
                    i = act.activation(gates[:, l, half, 2, :], bank[2 * (l % 2) + half][0:B, GATE:GATE + C],
                                       ACT.Tanh if l == 1 else ACT.Copy)
                i.then_inc(ada_gate, 1)
                if l + 2 < L:
                    load_ada(act, l + 2)

            def slot(l, s, at):
                lag = lags(l)
                n = at("qkv")
                if n is not None:
                    act.wait_ge(hT_pe, upto(l, n))
                    ge(act, qkv_pe, upto(l, n - 1))
                    act.copy(hA[:], bank[0][:, 0:P])
                    act.copy(hB[:], bank[0][0:KS, P:P + P // 2].bitcast(BF16)).then_inc(hT_sb, 1)
                n = at("out")
                if n is not None:
                    act.wait_ge(av_pe, upto(l, n, 4))
                    ge(act, ob_pe, upto(l, n - 1))
                    act.copy(oT[:], bank[3][:]).then_inc(ot_sb, 1)
                n = at("prob")
                if n is not None:
                    par = (s - lag["prob"]) % 2
                    act.wait_ge(mT_pe, upto(l, n))
                    ge(act, m_rows, upto(l, n - 2, 32))
                    act.copy(mT[:, par, :], bank[2][0:48, 0:P // 2].bitcast(BF16)).then_inc(mT_sb, 1)
                n = at("score")
                if n is not None:
                    par = (s - lag["score"]) % 2
                    act.wait_ge(tk_pe, upto(l, n))
                    ge(act, st_pe, upto(l, n - 2, 4))
                    act.copy(kT[:, par], bank[3][:].bitcast(BF16)).then_inc(kT_sb, 1)
                    act.wait_ge(qkv_sb, upto(l, n))
                    ge(act, av_pe, upto(l, n - 2, 4))
                    act.copy(v[:, par, :, 0:D],
                             qkv[:, par, 2 * C:3 * C].rearrange("p (h d) -> p h d", d=D)).then_inc(v_sb, 1)

                def first_part():
                    n = at("split")
                    if n is None:
                        return
                    par = (s - lag["split"]) % 2
                    if NORMED[l]:
                        act.wait_ge(q_rdy, upto_n(l, n))
                        src = qy[:, par, :]
                    else:
                        act.wait_ge(qkv_pe, upto(l, n))
                        src = bank[1][:, 0:2 * C]
                    ge(act, tq_pe, upto(l, n - 2))
                    ge(act, tk_pe, upto(l, n - 2))
                    act.copy(stack[:, par, :, 0:D], src.rearrange("p (h d) -> p h d", d=D)).then_inc(x1_rdy, 1)

                def copy_qkv():
                    n = at("qkv")
                    if n is not None:
                        act.wait_ge(qkv_pe, upto(l, n))
                        if s >= 2:
                            act.wait_ge(v_sb, upto(l, n - 2))
                            if NORMED[l]:
                                act.wait_ge(q_mid, upto_n(l, n - 2))
                        cols = slice(0 if NORMED[l] else 2 * C, 3 * C)
                        act.copy(qkv[:, s % 2, cols], bank[1][:, cols]).then_inc(qkv_sb, 1)

                copy_qkv()
                if not NORMED[l]:
                    first_part()

                def exps(groups):
                    n = at("prob")
                    if n is None:
                        return
                    for g in groups:
                        act.wait_ge(st_pe, upto(l, n, 4) - 3 + g)
                        ge(act, av_pe, upto(l, n - 1, 4) - 3 + g)
                        act.activation(e[:, g * GRP:(g + 1) * GRP, :], bank[6 + g % 2][:], ACT.Exp,
                                       scale=float(D) ** -0.5).then_inc(e_rdy, 1)

                n = at("out")
                if n is not None:
                    act.wait_ge(oT_pe, upto(l, n))
                    ge(act, proj_pe, upto(l, n - 1))
                    act.copy(otA[:], bank[0][:, 0:P])
                    act.copy(otB[:], bank[0][0:KB, P:2 * P]).then_inc(oT_sb, 1)
                exps((0,))
                if NORMED[l]:
                    first_part()
                    exps((1,))
                n = at("split")
                if n is not None:
                    par = (s - lag["split"]) % 2
                    act.wait_ge(rem_rdy, upto(l, n))
                    act.copy(stack[:, par, :, 3 * SW:3 * SW + D],
                             rem[:, par, :].rearrange("p (h d) -> p h d", d=D)).then_inc(x2_rdy, 1)
                if not NORMED[l]:
                    exps((1,))
                exps((2, 3))

            def next_mod2(l, j):
                last_pair = {PAIRS - 2: 3, PAIRS - 1: 5, PAIRS: 7}
                if l + 1 < L and j in last_pair:
                    act.wait_ge(gate2_rdy, upto_p(l, last_pair[j]))
                    start = 0 if j == PAIRS - 2 else 2 * last_pair[j - 1] + 2
                    load_mod(act, l + 1, 1, slice(start, 2 * last_pair[j] + 2))

            def mlp_slot(l, j, at):
                n = at(0)
                if n is None:
                    next_mod2(l, j)
                    return
                par = j % 2
                act.wait_ge(h2T_pe, upto_p(l, n))
                ge(act, fc1_pe, upto_p(l, n - 2, 3))
                act.copy(h2A[:, par, :], bank[0][:, 0:2 * P]).then_inc(h2T_sb, 1)
                act.copy(h2B[:, par, :], bank[0][0:KS, 2 * P:3 * P].bitcast(BF16)).then_inc(h2T_sb, 1)
                ge(act, fc2_pe, upto_p(l, n - 2))
                for k in range(3):
                    act.wait_ge(fc1_pe, upto_p(l, n, 3) - 2 + k)
                    m = P if k < 2 else FL
                    cs = slice(2 * k, min(2 * k + 2, FC))
                    width = 4 * T if k < 2 else 2 * T
                    act.activation(gT[0:m, par, cs, :], bank[5 - 3 * par + k][0:m, 0:width],
                                   ACT.Gelu_apprx_tanh if l < 2 else ACT.Gelu).then_inc(gelu_rdy, 1)
                next_mod2(l, j)

            act.wait_ge(set_stack, 1)
            for l in range(L):
                attention(act, l, slot, mlp_slot)
                if l + 1 < L:
                    act.wait_ge(gate_rdy, upto(l, B - 1))
                    load_mod(act, l + 1, 0)
                    if l + 2 < L:
                        load_ws(act, l + 2)
                    if l:
                        load_w(act, l + 1)
                mlp(act, l, mlp_slot, slot)

        @block.vector
        def _(dve):
            dve.memset(s_b[:], 1.0)
            dve.memset(busy[:], 1.0).then_inc(set_ones, 1)
            dve.memset(half_neg[:], -0.5)
            dve.memset(zeros[:], 0.0)
            dve.memset(m3[:], 0.0)
            dve.memset(bs[:, :, 6 * CR:KS], 1.0)
            dve.memset(bs2[:, :, :, 6 * CR:KS], 1.0)
            dve.memset(o[:, C:C + 1], 1.0)
            dve.memset(gT[FL:FL + 1, :, FC - 1, :], 1.0).then_inc(set_ones, 1)
            halves = m_sb[:].rearrange("b l (h k c) -> b l h k c", h=2, k=3)
            def conditioning(l):
                dve.wait_ge(ada_gate, l + 1)
                if l:
                    dve.wait_ge(ada_mod, 2 * l)
                for half in range(2):
                    i = dve.tensor_scalar(sc1[:, half, :], bank[2 * (l % 2) + half][0:B, SCALE:SCALE + C], 1.0, None, ALU.add)
                i.then_inc(ada_sc, 1)
                dve.wait_ge(ada_sc, l + 1)
                dve.tensor_tensor(halves[:, l, :, 1, :], sc1[:], aff_sb[:, l, :, 0, :], ALU.mult).then_inc(ada_mod, 1)
                dve.tensor_tensor(shb[:], sc1[:], aff_sb[:, l, :, 1, :], ALU.mult).then_inc(ada_b1, 1)
                dve.wait_ge(ada_b1, l + 1)
                for half in range(2):
                    i = dve.tensor_tensor(halves[:, l, half, 0, :], bank[2 * (l % 2) + half][0:B, SHIFT:SHIFT + C],
                                          shb[:, half, :], ALU.add)
                i.then_inc(ada_mod, 1)

            def split_weights(l, steps=range(4)):
                def masked(to, mask, rest, done):
                    dve.scalar_tensor_tensor(out=to, in0=ws_part[:], scalar=part_mask[:, mask:mask + 1], in1=rest,
                                             op0=ALU.mult, op1=ALU.add).then_inc(done, 1)
                if 0 in steps:
                    dve.wait_ge(ld_ws, 16 * (l + 1))
                    dve.tensor_copy(ws_part[:], ws_raw[:]).then_inc(ws_step, 1)
                if 1 in steps:
                    dve.wait_ge(ws_step, 3 * l + 1)
                    masked(ws_tmp[:], 0, ws_raw[:], ws_step)
                if 2 in steps:
                    dve.wait_ge(ws_step, 3 * l + 2)
                    dve.tensor_copy(ws_part[:], ws_tmp[:]).then_inc(ws_step, 1)
                if 3 in steps:
                    dve.wait_ge(ws_step, 3 * l + 3)
                    if l >= 2:
                        dve.wait_ge(fc1_pe, upto_p(l - 2, PAIRS - 1, 3))
                    masked(ws[:, l % 2, :], 1, ws_tmp[:], ws_rdy)

            def statistics(l, j, k):
                var_s = (ln1_var, ln2_var)[k]
                for u in range(2):
                    i = dve.bn_stats(st6[:, k, u, :], x[:, bass.ds(2 * j + u, 1), :])
                dve.drain()
                for u in range(2):
                    i = dve.bn_aggr(mv[:, k, u, :], st6[:, k, u, :])
                i.then_inc(ln_mv[k], 1)
                dve.wait_ge(ln_mv[k], upto_p(l, j))
                if LN_EPS[l] is None:
                    dve.tensor_tensor(var[:, k, :], mv[:, k, :, 0], mv[:, k, :, 0], ALU.mult
                                      ).then_inc(ln_sq[k], 1)
                    dve.wait_ge(ln_sq[k], j + 1)
                    dve.tensor_tensor(var[:, k, :], var[:, k, :], mv[:, k, :, 1], ALU.add
                                      ).then_inc(ln_sum[k], 1)
                    dve.wait_ge(ln_sum[k], j + 1)
                    dve.tensor_scalar(var[:, k, :], var[:, k, :], float(C), TINY, ALU.mult, ALU.max
                                      ).then_inc(var_s, 1)
                else:
                    dve.tensor_scalar(var[:, k, :], mv[:, k, :, 1], LN_EPS[l], None, ALU.add).then_inc(var_s, 1)

            def normalise(l, j, k):
                rstd_s, done = ((ln1_rstd, xn1_rdy), (ln2_rstd, xn2_rdy))[k]
                dve.wait_ge(rstd_s, upto_p(l, j))
                for u in range(2):
                    dst, src = xn[:, bass.ds(2 * j + u, 1), :], x[:, bass.ds(2 * j + u, 1), :]
                    if LN_EPS[l] is None:
                        i = dve.tensor_scalar(dst, src, rstd[:, k, u:u + 1], None, ALU.mult)
                    else:
                        i = dve.tensor_scalar(dst, src, mv[:, k, u, 0:1], rstd[:, k, u:u + 1],
                                              ALU.subtract, ALU.mult)
                i.then_inc(done, 1)

            def first_statistics(half):
                dve.wait_ge((ld_x, ld_x_rest)[half], 32)
                of = range(half * B // 2, (half + 1) * B // 2)
                for b in of:
                    i = dve.bn_stats(st0[:, b, :], x[:, b, :])
                i.then_inc(first_stats, 1)
                dve.wait_ge(first_stats, half + 1)
                for b in of:
                    i = dve.bn_aggr(mv0[:, b, :], st0[:, b, :])
                i.then_inc(ln_mv[0], PAIRS // 2)
                dve.wait_ge(ln_mv[0], (half + 1) * PAIRS // 2)
                dve.tensor_scalar(var0[:, of.start:of.stop], mv0[:, of.start:of.stop, 1], LN_EPS[0], None, ALU.add
                                  ).then_inc(ln1_var, PAIRS // 2)

            def first_normalise(half):
                dve.wait_ge(ln1_rstd, (half + 1) * PAIRS // 2)
                for b in range(half * B // 2, (half + 1) * B // 2):
                    i = dve.tensor_scalar(xn[:, b, :], x[:, b, :], mv0[:, b, 0:1], rstd0[:, b:b + 1],
                                          ALU.subtract, ALU.mult)
                i.then_inc(xn1_rdy, PAIRS // 2)

            first_statistics(0)
            dve.wait_ge(ld_aff, 32)
            dve.tensor_scalar(aff_sb[:, 1, :, 0, :], aff_sb[:, 1, :, 0, :], float(C) ** 0.5, None,
                              ALU.mult).then_inc(set_qk, 1)
            dve.wait_ge(ld_ident, 16)
            dve.tensor_copy(idb[:], idf[:]).then_inc(set_idb, 1)
            conditioning(0)
            first_normalise(0)
            split_weights(0)
            first_statistics(1)
            dve.wait_ge(set_qk, 1)
            conditioning(1)
            first_normalise(1)
            dve.wait_ge(ld_qk, 32)
            dve.tensor_scalar(qk_g[:, 0, :], qk_g[:, 0, :], float(D) ** 0.5, None, ALU.mult).then_inc(set_qk, 1)
            conditioning(2)
            conditioning(3)

            def heads(ap):
                return ap.rearrange("p (h d) -> p h d", d=D)

            def each_head(ap):
                return ap.unsqueeze(2).to_broadcast([P, 2 * H, D])

            def slot(l, s, at):
                lag = lags(l)
                steps, before = Q_STEPS.get(l), Q_STEPS_BEFORE.get(l)
                chain = [None, 0]

                def take_up(n, done):
                    chain[:] = n if NORMED[l] else None, done

                def chained(op, dst, *operands, **how):
                    n, done = chain
                    if n is None:
                        return
                    if done:
                        dve.wait_ge(q_step[l], steps * n + done)
                    op(dst, *operands, **how).then_inc(q_step[l], 1)
                    chain[1] += 1

                qk = qkv[:, s % 2, 0:2 * C]

                def head_sums():
                    if chain[0] is not None:
                        dve.wait_ge(qkv_sb, upto(l, chain[0]))
                    if l == 3:
                        chained(dve.tensor_reduce, qss[:], heads(qk), AX_X, ALU.add)

                def centre():
                    if l == 3:
                        chained(dve.scalar_tensor_tensor, heads(qk), in0=each_head(qss[:]), scalar=-1.0 / D,
                                in1=heads(qk), op0=ALU.mult, op1=ALU.add)

                def squares():
                    chained(dve.tensor_tensor, qsq[:], qk, qk, ALU.mult)

                def square_sums():
                    chained(dve.tensor_reduce, qss[:], heads(qsq[:]), AX_X, ALU.add)

                def guard():
                    if l == 3:
                        chained(dve.tensor_scalar, qss[:], qss[:], 1.0 / D, QK_EPS, ALU.mult, ALU.add)
                    else:
                        chained(dve.tensor_scalar, qss[:], qss[:], TINY, None, ALU.max)

                def halve_exponent():
                    chained(dve.tensor_scalar, qt1[:].bitcast(I32), qss[:].bitcast(I32), 1, None,
                            ALU.arith_shift_right)

                def guess():
                    chained(dve.tensor_scalar, qrs[:].bitcast(I32), qt1[:].bitcast(I32), -1.0, MAGIC,
                            ALU.mult, ALU.add)

                def newton(*steps):
                    if 1 in steps:
                        chained(dve.scalar_tensor_tensor, qt1[:], in0=qrs[:], scalar=-0.5, in1=qss[:],
                                op0=ALU.mult, op1=ALU.mult)
                    if 2 in steps:
                        chained(dve.tensor_tensor, qt2[:], qt1[:], qrs[:], ALU.mult)
                    if 3 in steps:
                        chained(dve.scalar_tensor_tensor, qrs[:], in0=qt2[:], scalar=1.5, in1=qrs[:],
                                op0=ALU.add, op1=ALU.mult)

                def query_stack():
                    n = at("score")
                    if n is None:
                        return
                    par = (s - lag["score"]) % 2
                    dve.wait_ge(tq_pe, upto(l, n))
                    ge(dve, st_pe, upto(l, n - 2, 4))
                    dve.tensor_copy(qT[:, par], bank[1][:].bitcast(BF16)).then_inc(qT_sb, 1)

                def remainder():
                    n = at("split")
                    if n is None:
                        return
                    par = (s - lag["split"]) % 2
                    src = qy[:, par, :] if NORMED[l] else bank[1][:, 0:2 * C]
                    dve.wait_ge(x1_rdy, upto(l, n))
                    ge(dve, x3_rdy, upto(l, n - 2, 2))
                    dve.tensor_tensor(heads(rem[:, par, :]), heads(src), stack[:, par, :, 0:D], ALU.subtract
                                      ).then_inc(rem_rdy, 1)

                take_up(at("norm"), before)
                newton(1)
                query_stack()
                newton(2, 3)
                newton(1, 2)
                n = at("out")
                if n is not None:
                    acc = bank[2][:].rearrange("p (h w) -> p h w", w=VW)
                    dve.wait_ge(ob_pe, upto(l, n))
                    ge(dve, oT_pe, upto(l, n - 1))
                    dve.reciprocal(rsum[:], acc[:, :, D]).then_inc(rsum_rdy, 1)
                newton(3)
                if n is not None:
                    dve.wait_ge(rsum_rdy, upto(l, n))
                    dve.tensor_tensor(o[:, 0:C].rearrange("p (h d) -> p h d", d=D), acc[:, :, 0:D],
                                      rsum[:].unsqueeze(2).to_broadcast([P, H, D]), ALU.mult).then_inc(o_rdy, 1)
                newton(1, 2, 3)
                n, done = chain
                if n is not None:
                    assert done == steps
                    ge(dve, x1_rdy, upto(l, n - 2))
                    ge(dve, rem_rdy, upto(l, n - 2))
                    dve.wait_ge(q_step[l], steps * n + steps)
                    par = (s - 1) % 2
                    dve.tensor_tensor(heads(qy[:, par, :]), heads(qkv[:, par, 0:2 * C]), each_head(qrs[:]), ALU.mult
                                      ).then_inc(q_mid, 1)
                def maxima(groups):
                    n = at("score")
                    if n is None:
                        return
                    par = (s - lag["score"]) % 2
                    for g in groups:
                        dve.wait_ge(s_pe, upto(l, n, 4) - 3 + g)
                        if g == 0:
                            ge(dve, m_rdy, upto(l, n - 2))
                        dve.tensor_reduce(mx[:, par, g * GRP:(g + 1) * GRP],
                                          bank[4 + g % 2][:].rearrange("p (h k) -> p h k", k=T), AX_X, ALU.max
                                          ).then_inc(mx_rdy, 1)

                nsp = at("split")
                slots = stack[:, (s - lag["split"]) % 2, :, 0:MROW].rearrange("p h (k d) -> p h k d", d=SW)

                def copy_slots(who, to, of, times):
                    if nsp is not None:
                        src = slots[:, who, of:of + 1, :]
                        dve.tensor_copy(slots[:, who, to, :], src.to_broadcast([P, H, times, SW])
                                        ).then_inc(slots_rdy, 1)

                queries, keys = slice(0, H), slice(H, 2 * H)
                maxima((0,))
                if NORMED[l]:
                    maxima((1,))
                    take_up(at("qkv"), 0)
                    head_sums()
                    centre()
                    squares()
                    if at("split") is not None:
                        dve.wait_ge(q_mid, upto_n(l, at("split")))
                    remainder()
                    square_sums()
                else:
                    remainder()
                    maxima((1,))
                if nsp is not None:
                    dve.wait_ge(x2_rdy, upto(l, nsp))
                copy_slots(queries, slice(1, 5, 3), 0, 2)
                guard()
                copy_slots(queries, slice(2, 3), 3, 1)
                halve_exponent()
                copy_slots(keys, slice(2, 6, 3), 0, 2)
                guess()
                copy_slots(keys, slice(1, 2), 3, 1)
                maxima((2, 3))
                n = at("out")
                if n is not None:
                    dve.wait_ge(proj_pe, upto(l, n))
                    ge(dve, x_att, upto(l, n - 1))
                    dve.tensor_tensor(gated[:], bank[2][:, 0:C],
                                      mod1[:, bass.ds(n, 1), GATE:GATE + C], ALU.mult).then_inc(gate_rdy, 1)
                assert chain[0] is None or chain[1] == before
                if l + 1 < L and isinstance(at("ahead"), int) and s >= first_of_loop(l) - 4 and s < B:
                    split_weights(l + 1, (s - first_of_loop(l) + 4,))

            def mlp_slot(l, j, at):
                n2, n3 = at(-1), at(-2)
                if n2 is not None:
                    if j == -1:
                        dve.wait_ge(hs_rdy, upto(l, B - 1))
                    normalise(l, n2, 1)
                if n3 is not None:
                    dve.wait_ge(ld_x, 32)
                    dve.wait_ge(x_att, upto(l, 2 * n3 + 1))
                    statistics(l, n3, 1)
                n = at(2)
                if n is not None and l + 1 < L:
                    dve.wait_ge(hs2_rdy, upto_p(l, n))
                    normalise(l + 1, n, 0)
                n = at(1)
                if n is not None:
                    if j == 1:
                        dve.wait_ge(ld_mod2, 16 * (3 * l + 1))
                    dve.wait_ge(fc2_pe, upto_p(l, n))
                    ge(dve, x_mlp, upto_p(l, n - 1))
                    dve.tensor_tensor(gated2[:], bank[fc2_bank(j)][:, 0:2 * C].rearrange("p (u c) -> p u c", u=2),
                                      mod2[:, bass.ds(2 * n, 2), GATE:GATE + C], ALU.mult).then_inc(gate2_rdy, 1)
                    dve.wait_ge(gate2_rdy, upto_p(l, n))
                    xx = x[:, bass.ds(2 * n, 2), :]
                    dve.tensor_tensor(xx, xx, gated2[:], ALU.add).then_inc(x_mlp, 1)
                    if l + 1 < L:
                        dve.wait_ge(ld_x, 32)
                        dve.wait_ge(x_mlp, upto_p(l, n))
                        statistics(l + 1, n, 0)

            for l in range(L):
                attention(dve, l, slot, mlp_slot, prepares=True)
                mlp(dve, l, mlp_slot, slot)

        @block.gpsimd
        def _(pool):
            def rstd_of(l, j, k):
                var_s, rstd_s, done = ((ln1_var, ln1_rstd, xn1_rdy), (ln2_var, ln2_rstd, xn2_rdy))[k]
                pool.wait_ge(var_s, upto_p(l, j))
                ge(pool, done, upto_p(l, j - 1))
                pool.tensor_tensor(rstd[:, k, :], var[:, k, :], half_neg[:, 0:2], ALU.pow).then_inc(rstd_s, 1)

            def heads(ap):
                return ap.rearrange("p (h d) -> p h d", d=D)

            def split_last(dst, rest, src, m, step, steps, done):
                slots = dst[:, :, 0:6 * CR].rearrange("p m (k c) -> p m k c", c=CR)
                zero = zeros[:].unsqueeze(1).unsqueeze(1)
                for u in range(m):
                    i = pool.tensor_tensor(slots[:, u, 0:3], src[:, u:u + 1, :].to_broadcast([P, 3, CR]),
                                           zero[:, 0].to_broadcast([P, 3, CR]), ALU.add)
                i.then_inc(step, 1)
                pool.wait_ge(step, steps - 2)
                pool.tensor_tensor(rest, src, slots[:, :, 0], ALU.subtract).then_inc(step, 1)
                pool.wait_ge(step, steps - 1)
                for u in range(m):
                    i = pool.tensor_tensor(slots[:, u, 3:5], rest[:, u:u + 1, :].to_broadcast([P, 2, CR]),
                                           zero[:, 0].to_broadcast([P, 2, CR]), ALU.add)
                i.then_inc(step, 1)
                pool.wait_ge(step, steps)
                pool.tensor_tensor(slots[:, :, 5], rest, slots[:, :, 3], ALU.subtract).then_inc(done, 1)

            pool.memset(v[:], 0.0)
            pool.memset(stack[:], 0.0).then_inc(set_zero, 1)
            pool.wait_ge(set_zero, 1)
            pool.memset(v[:, :, :, D:D + 1], 1.0)
            pool.memset(stack[:, :, H:2 * H, MROW:MROW + 3], -1.0).then_inc(set_stack, 1)
            pool.wait_ge(set_ones, 2)
            for half in range(2):
                of = slice(half * B // 2, (half + 1) * B // 2)
                pool.wait_ge(ln1_var, (half + 1) * PAIRS // 2)
                pool.tensor_tensor(rstd0[:, of], var0[:, of], half_neg[:], ALU.pow).then_inc(ln1_rstd, PAIRS // 2)
            pool.wait_ge(set_stack, 1)

            def slot(l, s, at):
                lag = lags(l, 1)
                n = at("split")
                if n is not None:
                    par = (s - lag["split"]) % 2
                    slots = stack[:, par, :, 0:MROW].rearrange("p h (k d) -> p h k d", d=SW)
                    pool.wait_ge(x2_rdy, upto(l, n))
                    for who, k in ((slice(0, H), 5), (slice(H, 2 * H), 4)):
                        pool.tensor_tensor(slots[:, who, k, 0:D], heads(rem[:, par, :])[:, who, :],
                                           slots[:, who, 3, 0:D], ALU.subtract).then_inc(x3_rdy, 1)
                n = at("score")
                if n is not None:
                    par = (s - lag["score"]) % 2
                    parts = m3[:, par, 0:3 * H].rearrange("p (e j h a) -> p e j h a", e=2, j=3, h=2)
                    full = mx[:, par, :].rearrange("p (h e a) -> p e h a", h=2, e=2)
                    rest = mrem[:, par, :].rearrange("p (h e a) -> p e h a", h=2, e=2)
                    pool.wait_ge(mx_rdy, upto(l, n, 4))
                    ge(pool, mT_pe, upto(l, n - 2))
                    zero = zeros[:].rearrange("p (h e a) -> p e h a", h=2, e=2)
                    pool.tensor_tensor(parts[:, :, 0], full, zero, ALU.add).then_inc(m_step, 1)
                    pool.wait_ge(m_step, upto(l, n, 3) - 2)
                    pool.tensor_tensor(rest, full, parts[:, :, 0], ALU.subtract).then_inc(m_step, 1)
                    pool.wait_ge(m_step, upto(l, n, 3) - 1)
                    pool.tensor_tensor(parts[:, :, 1], rest, zero, ALU.add).then_inc(m_step, 1)
                    pool.wait_ge(m_step, upto(l, n, 3))
                    pool.tensor_tensor(parts[:, :, 2], rest, parts[:, :, 1], ALU.subtract
                                       ).then_inc(m_rdy, 1)
                n = at("out")
                if n is not None:
                    xx = x[:, bass.ds(n, 1), :]
                    pool.wait_ge(gate_rdy, upto(l, n))
                    pool.tensor_tensor(xx, xx, gated[:].unsqueeze(1), ALU.add).then_inc(x_att, 1)
                n = at("ahead")
                if n is not None:
                    par = (s + 1) % 2
                    if s == -1:
                        pool.wait_ge(ld_mod1, 16 * (l + 1))
                        pool.wait_ge(xn1_rdy, upto_p(l, 1 if l else PAIRS // 2 - 1))
                    elif l and s == 3:
                        pool.wait_ge(xn1_rdy, upto_p(l, PAIRS - 1))
                    elif l == 0 and s == B // 4 - 1:
                        pool.wait_ge(ld_mod1_rest, 16)
                        pool.wait_ge(xn1_rdy, PAIRS)
                    ge(pool, hT_pe, upto(l, n - 2))
                    h = hs[:, par:par + 1, 0:C]
                    pool.tensor_tensor(h, xn[:, bass.ds(n, 1), :], mod1[:, bass.ds(n, 1), SCALE:SCALE + C],
                                       ALU.mult).then_inc(hs_mul, 1)
                    pool.wait_ge(hs_mul, upto(l, n))
                    pool.tensor_tensor(h, h, mod1[:, bass.ds(n, 1), SHIFT:SHIFT + C], ALU.add
                                       ).then_inc(hs_rdy, 1)
                    pool.wait_ge(hs_rdy, upto(l, n))
                    split_last(bs[:, par:par + 1, :], bs_rem[:, par:par + 1, :], hs[:, par:par + 1, P:C], 1,
                               bs_step, upto(l, n, 3), bs_rdy)
                n = at("qkv")
                if NORMED[l] and n is not None:
                    y = qy[:, (s - 1) % 2, :]
                    pool.wait_ge(q_mid, upto_n(l, n))
                    if l == 1:
                        pool.tensor_tensor(y, y, qk_g[:, 0, :], ALU.mult).then_inc(q_rdy, 1)
                    else:
                        pool.tensor_tensor(y, y, qk_g[:, 1, :], ALU.mult).then_inc(q_gain, 1)
                        pool.wait_ge(q_gain, n + 1)
                        pool.tensor_tensor(y, y, qk_b[:], ALU.add).then_inc(q_rdy, 1)

            def mlp_slot(l, j, at):
                n2, n3, n = at(-1), at(-2), at(1)
                if n2 is not None:
                    par = (j + 1) % 2
                    pool.wait_ge(xn2_rdy, upto_p(l, n2))
                    if j == -1:
                        pool.wait_ge(ld_mod2, 16 * (3 * l + 1))
                    ge(pool, h2T_pe, upto_p(l, n2 - 2))
                    h = hs2[:, par, :, 0:C]
                    b = bass.ds(2 * n2, 2)
                    pool.tensor_tensor(h, xn[:, b, :], mod2[:, b, SCALE:SCALE + C], ALU.mult
                                       ).then_inc(hs2_mul, 1)
                    pool.wait_ge(hs2_mul, upto_p(l, n2))
                    pool.tensor_tensor(h, h, mod2[:, b, SHIFT:SHIFT + C], ALU.add).then_inc(hs2_rdy, 1)
                    pool.wait_ge(hs2_rdy, upto_p(l, n2))
                    split_last(bs2[:, par], bs2_rem[:, par], hs2[:, par, :, P:C], 2, bs2_step,
                               upto_p(l, n2, 3), bs2_rdy)
                if n3 is not None:
                    rstd_of(l, n3, 1)
                if n is not None and l + 1 < L:
                    rstd_of(l + 1, n, 0)

            for l in range(L):
                attention(pool, l, slot, mlp_slot, behind=1, prepares=True)
                mlp(pool, l, mlp_slot, slot, behind=1)


def pack(i):
    import numpy as np

    def f(name):
        return np.asarray(i[name])

    one = np.ones((C,), np.float32)
    zero = np.zeros((C,), np.float32)
    wcat = np.zeros((L, C + 1, WCOLS + ACOLS), np.float32)
    w2cat = np.zeros((L, P, FC, C), np.float32)
    names = [
        ("L0_cond_W_qkv", "L0_cond_b_qkv", "L0_cond_W_proj", "L0_cond_b_proj", "L0_cond_W_fc1", "L0_cond_b_fc1",
         "L0_cond_W_ada", "L0_cond_b_ada", "L0_cond_W_fc2", "L0_cond_b_fc2"),
        ("L1_cond_qkv_w", "L1_cond_qkv_b", "L1_cond_proj_w", "L1_cond_proj_b", "L1_cond_fc1_w", "L1_cond_fc1_b",
         "L1_cond_ada_w", "L1_cond_ada_b", "L1_cond_fc2_w", "L1_cond_fc2_b"),
        (None, None, "L2_cond_wo", "L2_cond_wo_b", "L2_cond_fc1_w", "L2_cond_fc1_b",
         "L2_cond_ada_w", "L2_cond_ada_b", "L2_cond_fc2_w", "L2_cond_fc2_b"),
        ("L3_cond_w_qkv", "L3_cond_b_qkv", "L3_cond_w_proj", "L3_cond_b_proj", "L3_cond_w1", "L3_cond_b1",
         "L3_cond_w_ada", "L3_cond_b_ada", "L3_cond_w2", "L3_cond_b2"),
    ]
    for l, row in enumerate(names):
        for k, (at, width) in enumerate(((QKV, 3 * C), (PROJ, C), (FC1, FF), (ADA, ACOLS))):
            if row[2 * k] is None:
                for m, name in enumerate(("L2_cond_wq", "L2_cond_wk", "L2_cond_wv")):
                    wcat[l, 0:C, at + m * C:at + (m + 1) * C] = f(name)
                continue
            w = f(row[2 * k])
            w = w.T if l == 1 else w
            wcat[l, 0:C, at:at + width] = w.reshape(H, D, C)[HEAD_ORDER].reshape(C, C) if at == PROJ else w
            wcat[l, C, at:at + width] = f(row[2 * k + 1])
        w = f(row[8])
        w = w.T if l == 1 else w
        for c in range(FC):
            m = P if c < FC - 1 else FL
            w2cat[l, 0:m, c, :] = w[c * P:c * P + m]
        w2cat[l, FL, FC - 1, :] = f(row[9])
    wlast = np.concatenate([np.tile(wcat[:, P:C, 0:SCOLS], (1, 6, 1)), np.tile(wcat[:, C:C + 1, 0:SCOLS], (1, 3, 1))],
                           axis=1)
    part = np.concatenate([np.repeat([1, 2, 3, 1, 2, 1], CR), [1, 2, 3]])
    masks = -np.stack([part >= 2, part >= 3], axis=1).astype(np.float32)
    aff = np.stack([
        np.stack([np.stack([one, zero])] * 2),
        np.stack([np.stack([np.broadcast_to(f("L1_cond_g1"), (C,)), zero]),
                  np.stack([np.broadcast_to(f("L1_cond_g2"), (C,)), zero])]),
        np.stack([np.stack([f("L2_cond_ln1_w"), f("L2_cond_ln1_b")]),
                  np.stack([f("L2_cond_ln2_w"), f("L2_cond_ln2_b")])]),
        np.stack([np.stack([one, zero])] * 2),
    ])
    qkaff = np.zeros((2, 2, 2 * C), np.float32)
    qkaff[0, 0] = np.concatenate([np.broadcast_to(f("L1_cond_qg"), (C,)), np.broadcast_to(f("L1_cond_kg"), (C,))])
    qkaff[1, 0] = np.concatenate([np.tile(f("L3_cond_qn_g"), H), np.tile(f("L3_cond_kn_g"), H)])
    qkaff[1, 1] = np.concatenate([np.tile(f("L3_cond_qn_b"), H), np.tile(f("L3_cond_kn_b"), H)])
    return {
        "x": np.ascontiguousarray(f("x")),
        "cT": np.ascontiguousarray(f("cond_1152").T),
        "wcat": wcat,
        "wlast": np.ascontiguousarray(wlast),
        "masks": masks,
        "w2cat": w2cat,
        "aff": np.ascontiguousarray(aff),
        "qkaff": qkaff,
        "ident": np.eye(P, dtype=np.float32),
    }


def kernel(**inputs):
    import concourse.bacc as bacc
    import numpy as np
    from concourse.bass_utils import run_bass_kernel_spmd

    nc = bacc.Bacc("TRN2", target_bir_lowering=False, num_devices=1)
    arrays, args = {}, []
    for name, a in pack(inputs).items():
        arrays[f"in_{name}"] = a
        args.append(nc.dram_tensor(f"in_{name}", a.shape, mybir.dt.from_np(a.dtype), kind="ExternalInput").ap())
    args.append(nc.dram_tensor("out_x", (B, T, C), mybir.dt.from_np(np.dtype("float32")),
                               kind="ExternalOutput").ap())
    build(nc, *args)
    return run_bass_kernel_spmd(nc, [arrays], core_ids=[0]).results[0]["out_x"]
```
